# Optimizing a Trainium2 kernel written in Bass

```python
import numpy as np
import jax
import jax.numpy as jnp

def _softmax(x, axis=-1):
    return jax.nn.softmax(x, axis=axis)

def _gelu(x):
    return jax.nn.gelu(x, approximate=True)

def _silu(x):
    return jax.nn.silu(x)

def _sigmoid(x):
    return jax.nn.sigmoid(x)

def _layernorm(x, axis=-1, eps=1e-05):
    m = jnp.mean(x, axis=axis, keepdims=True)
    v = jnp.var(x, axis=axis, keepdims=True)
    return (x - m) / jnp.sqrt(v + eps)

def _scatter_add(tgt, idx, src, axis=0):
    return tgt.at[idx].add(src)

def _segment_sum(src, seg, n):
    return jax.ops.segment_sum(src, seg, n)
kernel_name = 'mk_conv_preact_d4_conv_nchw256_r4_1f32fe'

def setup_inputs(seed: int=0):
    np.random.seed(seed)
    _w = jnp.asarray

    def _rec_inputs():
        import jax
        import jax.numpy as jnp
        _gk = jax.random.key(seed)
        x = -0.0003929 + 0.9999 * jax.random.normal(jax.random.fold_in(_gk, 1), (16, 64, 16, 16), jnp.float32)
        return x
    x = _rec_inputs()

    def _L0_conv_setup():
        import jax, jax.numpy as jnp
        import numpy as np
        B, CIN, COUT, G, NB, S, H, W = (16, 64, 64, 4, 6, 16, 16, 16)
        GC = COUT // G
        GN_GROUPS = 8

        def group_norm(x, gamma, beta, ngroups, eps=1e-05):
            b, c, h, w = x.shape
            xg = x.reshape(b, ngroups, c // ngroups, h, w)
            mean = xg.mean(axis=(2, 3, 4), keepdims=True)
            var = xg.var(axis=(2, 3, 4), keepdims=True)
            xn = ((xg - mean) * jax.lax.rsqrt(var + eps)).reshape(b, c, h, w)
            return xn * gamma[None, :, None, None] + beta[None, :, None, None]

        def conv_gn_act(x, w, b, g, be):
            y = jnp.einsum('bchw,oc->bohw', x, w) + b[None, :, None, None]
            return jax.nn.silu(group_norm(y, g, be, GN_GROUPS))
        key = jax.random.key(seed)
        ks = jax.random.split(key, 24)
        sd = 0.05
        inp = {'x': jax.random.normal(ks[0], (B, CIN, H, W), jnp.float32), 'pre_w': jax.random.normal(ks[1], (COUT, CIN), jnp.float32) * sd, 'pre_b': jnp.zeros((COUT,), jnp.float32), 'pre_gn_g': jnp.ones((COUT,), jnp.float32), 'pre_gn_b': jnp.zeros((COUT,), jnp.float32), 'sp_w1': jax.random.normal(ks[2], (COUT, S), jnp.float32) * sd, 'sp_b1': jnp.zeros((S,), jnp.float32), 'sp_w2': jax.random.normal(ks[3], (S, S), jnp.float32) * sd, 'sp_b2': jnp.zeros((S,), jnp.float32), 'alpha_w': jax.random.normal(ks[4], (S, G * NB), jnp.float32) * sd, 'alpha_b': jnp.zeros((G * NB,), jnp.float32), 'mu_w': jax.random.normal(ks[5], (S, G * NB), jnp.float32) * sd, 'mu_b': jnp.zeros((G * NB,), jnp.float32), 'sigma_w': jax.random.normal(ks[6], (S, G * NB), jnp.float32) * sd, 'sigma_b': jnp.zeros((G * NB,), jnp.float32), 'mix_w': jax.random.normal(ks[7], (S, G * NB), jnp.float32) * sd, 'mix_b': jnp.zeros((G * NB,), jnp.float32), 'gate_w': jax.random.normal(ks[8], (S, G), jnp.float32) * sd, 'gate_b': jnp.zeros((G,), jnp.float32), 'post_w': jax.random.normal(ks[9], (COUT, COUT), jnp.float32) * sd, 'post_b': jnp.zeros((COUT,), jnp.float32), 'post_gn_g': jnp.ones((COUT,), jnp.float32), 'post_gn_b': jnp.zeros((COUT,), jnp.float32)}
        return inp
    _L0_conv_all = _L0_conv_setup()
    _L0_conv_in = {k: v for k, v in _L0_conv_all.items() if k in ('pre_w', 'pre_b', 'pre_gn_g', 'pre_gn_b', 'sp_w1', 'sp_b1', 'sp_w2', 'sp_b2', 'alpha_w', 'alpha_b', 'mu_w', 'mu_b', 'sigma_w', 'sigma_b', 'mix_w', 'mix_b', 'gate_w', 'gate_b', 'post_w', 'post_b', 'post_gn_g', 'post_gn_b')}
    del _L0_conv_all

    def _L1_conv_setup():
        import jax, jax.numpy as jnp
        import numpy as np
        D_MODEL = 64
        EXPAND = 2
        D_INNER = EXPAND * D_MODEL
        HEADDIM = 16
        NHEADS = D_INNER // HEADDIM
        D_STATE = 16
        CONV_DIM = D_INNER + 2 * D_STATE
        D_IN_PROJ = 2 * D_INNER + 2 * D_STATE + NHEADS
        BATCH, HH, WW = (16, 16, 16)
        key = jax.random.key(seed)
        ks = jax.random.split(key, 8)
        u = jax.random.normal(ks[0], (BATCH, D_MODEL, HH, WW), jnp.float32)
        W_in = jax.random.normal(ks[1], (D_IN_PROJ, D_MODEL), jnp.float32) * D_MODEL ** (-0.5)
        conv_w = jax.random.normal(ks[2], (CONV_DIM, 1, 3, 3), jnp.float32) * (1.0 / 3.0)
        conv_b = jnp.zeros((CONV_DIM,), jnp.float32)
        dt = jnp.exp(jax.random.uniform(ks[3], (NHEADS,)) * (np.log(0.1) - np.log(0.001)) + np.log(0.001))
        dt = jnp.clip(dt, 0.0001, None)
        dt_bias = dt + jnp.log(-jnp.expm1(-dt))
        A_log = jnp.log(jax.random.uniform(ks[4], (NHEADS,), minval=1.0, maxval=16.0))
        D = jnp.ones((NHEADS,), jnp.float32)
        ln_g = jnp.ones((D_INNER,), jnp.float32)
        ln_b = jnp.zeros((D_INNER,), jnp.float32)
        W_out = jax.random.normal(ks[5], (D_MODEL, D_INNER), jnp.float32) * D_INNER ** (-0.5)
        return dict(u=u, W_in=W_in, conv_w=conv_w, conv_b=conv_b, dt_bias=dt_bias, A_log=A_log, D=D, ln_g=ln_g, ln_b=ln_b, W_out=W_out, H=HH, W=WW)
    _L1_conv_all = _L1_conv_setup()
    _L1_conv_in = {k: v for k, v in _L1_conv_all.items() if k in ('W_in', 'conv_w', 'conv_b', 'dt_bias', 'A_log', 'D', 'ln_g', 'ln_b', 'W_out')}
    del _L1_conv_all

    def _L2_conv_setup():
        import jax, jax.numpy as jnp
        import numpy as np
        EMBED = 64
        HEADS = 8
        HEAD_DIM = EMBED // HEADS
        key = jax.random.key(seed)
        ks = jax.random.split(key, 6)
        B, C, H, W = (8, EMBED, 32, 32)
        x = jax.random.normal(ks[0], (B, C, H, W), dtype=jnp.float32)
        limit = float(np.sqrt(6.0 / (EMBED + EMBED)))

        def xavier(k):
            return jax.random.uniform(k, (EMBED, EMBED), jnp.float32, -limit, limit)
        return {'x': x, 'Wq': xavier(ks[1]), 'bq': jnp.zeros((EMBED,), jnp.float32), 'Wk': xavier(ks[2]), 'bk': jnp.zeros((EMBED,), jnp.float32), 'Wv': xavier(ks[3]), 'bv': jnp.zeros((EMBED,), jnp.float32), 'Wo': xavier(ks[4]), 'bo': jnp.zeros((EMBED,), jnp.float32)}
    _L2_conv_all = _L2_conv_setup()
    _L2_conv_in = {k: v for k, v in _L2_conv_all.items() if k in ('Wq', 'bq', 'Wk', 'bk', 'Wv', 'bv', 'Wo', 'bo')}
    del _L2_conv_all

    def _L3_conv_setup():
        import jax, jax.numpy as jnp
        import numpy as np
        K = 3
        PAD = 1
        STRIDE = 1

        def conv2d(x, w, b, stride=STRIDE, pad=PAD):
            out = jax.lax.conv_general_dilated(x, w, (stride, stride), [(pad, pad), (pad, pad)], dimension_numbers=('NCHW', 'OIHW', 'NCHW'))
            return out + b[None, :, None, None]

        def deform_sample(x, offset, mask):
            B, C, H, W = x.shape
            KK = mask.shape[1]
            Ho, Wo = (offset.shape[2], offset.shape[3])
            off = offset.reshape(B, KK, 2, Ho, Wo)
            dy, dx = (off[:, :, 0], off[:, :, 1])
            ky, kx = jnp.meshgrid(jnp.arange(K), jnp.arange(K), indexing='ij')
            ky = ky.reshape(-1).astype(x.dtype)
            kx = kx.reshape(-1).astype(x.dtype)
            base_y = (jnp.arange(Ho) * STRIDE - PAD).astype(x.dtype)
            base_x = (jnp.arange(Wo) * STRIDE - PAD).astype(x.dtype)
            py = base_y[None, None, :, None] + ky[None, :, None, None] + dy
            px = base_x[None, None, None, :] + kx[None, :, None, None] + dx
            y0 = jnp.floor(py)
            x0 = jnp.floor(px)
            wy1 = py - y0
            wx1 = px - x0
            wy0 = 1.0 - wy1
            wx0 = 1.0 - wx1

            def gather(yi, xi):
                valid = ((yi >= 0) & (yi < H) & (xi >= 0) & (xi < W)).astype(x.dtype)
                yc = jnp.clip(yi, 0, H - 1).astype(jnp.int32)
                xc = jnp.clip(xi, 0, W - 1).astype(jnp.int32)
                vals = jax.vmap(lambda xb, yb, xib: xb[:, yb, xib])(x, yc, xc)
                return vals * valid[:, None]
            samp = gather(y0, x0) * (wy0 * wx0)[:, None] + gather(y0, x0 + 1.0) * (wy0 * wx1)[:, None] + gather(y0 + 1.0, x0) * (wy1 * wx0)[:, None] + gather(y0 + 1.0, x0 + 1.0) * (wy1 * wx1)[:, None]
            return samp * mask[:, None]
        key = jax.random.key(seed)
        k = jax.random.split(key, 8)
        B, Cin, Cout, H, W = (4, 64, 64, 16, 16)
        stdv = 1.0 / np.sqrt(Cin * K * K)
        x = jax.random.normal(k[0], (B, Cin, H, W), dtype=jnp.float32)
        weight = jax.random.uniform(k[1], (Cout, Cin, K, K), minval=-stdv, maxval=stdv, dtype=jnp.float32)
        bias = jnp.zeros((Cout,), dtype=jnp.float32)
        off_w = jax.random.normal(k[2], (2 * K * K, Cin, K, K), dtype=jnp.float32) * 0.01
        off_b = jax.random.normal(k[3], (2 * K * K,), dtype=jnp.float32) * 0.5
        mask_w = jax.random.normal(k[4], (K * K, Cin, K, K), dtype=jnp.float32) * 0.01
        mask_b = jax.random.normal(k[5], (K * K,), dtype=jnp.float32) * 0.1
        return {'x': x, 'weight': weight, 'bias': bias, 'off_w': off_w, 'off_b': off_b, 'mask_w': mask_w, 'mask_b': mask_b}
    _L3_conv_all = _L3_conv_setup()
    _L3_conv_in = {k: v for k, v in _L3_conv_all.items() if k in ('weight', 'bias', 'off_w', 'off_b', 'mask_w', 'mask_b')}
    del _L3_conv_all
    return {'x': x, 'L0_conv_pre_w': _L0_conv_in['pre_w'], 'L0_conv_pre_b': _L0_conv_in['pre_b'], 'L0_conv_pre_gn_g': _L0_conv_in['pre_gn_g'], 'L0_conv_pre_gn_b': _L0_conv_in['pre_gn_b'], 'L0_conv_sp_w1': _L0_conv_in['sp_w1'], 'L0_conv_sp_b1': _L0_conv_in['sp_b1'], 'L0_conv_sp_w2': _L0_conv_in['sp_w2'], 'L0_conv_sp_b2': _L0_conv_in['sp_b2'], 'L0_conv_alpha_w': _L0_conv_in['alpha_w'], 'L0_conv_alpha_b': _L0_conv_in['alpha_b'], 'L0_conv_mu_w': _L0_conv_in['mu_w'], 'L0_conv_mu_b': _L0_conv_in['mu_b'], 'L0_conv_sigma_w': _L0_conv_in['sigma_w'], 'L0_conv_sigma_b': _L0_conv_in['sigma_b'], 'L0_conv_mix_w': _L0_conv_in['mix_w'], 'L0_conv_mix_b': _L0_conv_in['mix_b'], 'L0_conv_gate_w': _L0_conv_in['gate_w'], 'L0_conv_gate_b': _L0_conv_in['gate_b'], 'L0_conv_post_w': _L0_conv_in['post_w'], 'L0_conv_post_b': _L0_conv_in['post_b'], 'L0_conv_post_gn_g': _L0_conv_in['post_gn_g'], 'L0_conv_post_gn_b': _L0_conv_in['post_gn_b'], 'L1_conv_W_in': _L1_conv_in['W_in'], 'L1_conv_conv_w': _L1_conv_in['conv_w'], 'L1_conv_conv_b': _L1_conv_in['conv_b'], 'L1_conv_dt_bias': _L1_conv_in['dt_bias'], 'L1_conv_A_log': _L1_conv_in['A_log'], 'L1_conv_D': _L1_conv_in['D'], 'L1_conv_ln_g': _L1_conv_in['ln_g'], 'L1_conv_ln_b': _L1_conv_in['ln_b'], 'L1_conv_W_out': _L1_conv_in['W_out'], 'L2_conv_Wq': _L2_conv_in['Wq'], 'L2_conv_bq': _L2_conv_in['bq'], 'L2_conv_Wk': _L2_conv_in['Wk'], 'L2_conv_bk': _L2_conv_in['bk'], 'L2_conv_Wv': _L2_conv_in['Wv'], 'L2_conv_bv': _L2_conv_in['bv'], 'L2_conv_Wo': _L2_conv_in['Wo'], 'L2_conv_bo': _L2_conv_in['bo'], 'L3_conv_weight': _L3_conv_in['weight'], 'L3_conv_bias': _L3_conv_in['bias'], 'L3_conv_off_w': _L3_conv_in['off_w'], 'L3_conv_off_b': _L3_conv_in['off_b'], 'L3_conv_mask_w': _L3_conv_in['mask_w'], 'L3_conv_mask_b': _L3_conv_in['mask_b']}

def reference(x, L0_conv_pre_w, L0_conv_pre_b, L0_conv_pre_gn_g, L0_conv_pre_gn_b, L0_conv_sp_w1, L0_conv_sp_b1, L0_conv_sp_w2, L0_conv_sp_b2, L0_conv_alpha_w, L0_conv_alpha_b, L0_conv_mu_w, L0_conv_mu_b, L0_conv_sigma_w, L0_conv_sigma_b, L0_conv_mix_w, L0_conv_mix_b, L0_conv_gate_w, L0_conv_gate_b, L0_conv_post_w, L0_conv_post_b, L0_conv_post_gn_g, L0_conv_post_gn_b, L1_conv_W_in, L1_conv_conv_w, L1_conv_conv_b, L1_conv_dt_bias, L1_conv_A_log, L1_conv_D, L1_conv_ln_g, L1_conv_ln_b, L1_conv_W_out, L2_conv_Wq, L2_conv_bq, L2_conv_Wk, L2_conv_bk, L2_conv_Wv, L2_conv_bv, L2_conv_Wo, L2_conv_bo, L3_conv_weight, L3_conv_bias, L3_conv_off_w, L3_conv_off_b, L3_conv_mask_w, L3_conv_mask_b):
    import jax
    import jax.numpy as jnp

    def _L0_conv_ref(x, pre_w, pre_b, pre_gn_g, pre_gn_b, sp_w1, sp_b1, sp_w2, sp_b2, alpha_w, alpha_b, mu_w, mu_b, sigma_w, sigma_b, mix_w, mix_b, gate_w, gate_b, post_w, post_b, post_gn_g, post_gn_b):
        import jax, jax.numpy as jnp
        import numpy as np
        B, CIN, COUT, G, NB, S, H, W = (16, 64, 64, 4, 6, 16, 16, 16)
        GC = COUT // G
        GN_GROUPS = 8

        def group_norm(x, gamma, beta, ngroups, eps=1e-05):
            b, c, h, w = x.shape
            xg = x.reshape(b, ngroups, c // ngroups, h, w)
            mean = xg.mean(axis=(2, 3, 4), keepdims=True)
            var = xg.var(axis=(2, 3, 4), keepdims=True)
            xn = ((xg - mean) * jax.lax.rsqrt(var + eps)).reshape(b, c, h, w)
            return xn * gamma[None, :, None, None] + beta[None, :, None, None]

        def conv_gn_act(x, w, b, g, be):
            y = jnp.einsum('bchw,oc->bohw', x, w) + b[None, :, None, None]
            return jax.nn.silu(group_norm(y, g, be, GN_GROUPS))
        z = conv_gn_act(x, pre_w, pre_b, pre_gn_g, pre_gn_b)
        b, c, h, w = z.shape
        pooled = z.mean(axis=(2, 3))
        s = jax.nn.gelu(jax.nn.gelu(pooled @ sp_w1 + sp_b1) @ sp_w2 + sp_b2)
        alpha = jax.nn.softmax((s @ alpha_w + alpha_b).reshape(b, G, NB), axis=-1)
        mu = (s @ mu_w + mu_b).reshape(b, G, NB)
        sigma = jax.nn.softplus(s @ sigma_w + sigma_b).reshape(b, G, NB) + 0.001
        mix = jax.nn.sigmoid(s @ mix_w + mix_b).reshape(b, G, NB)
        gate = jax.nn.sigmoid(s @ gate_w + gate_b).reshape(b, G, 1, 1, 1)
        zg = z.reshape(b, G, GC, h, w)
        u = (zg[:, :, :, None] - mu[:, :, None, :, None, None]) / sigma[:, :, None, :, None, None]
        eu = jnp.exp(-u * u)
        mixb = mix[:, :, None, :, None, None]
        basis = mixb * eu + (1.0 - mixb) * (u * eu)
        response = (alpha[:, :, None, :, None, None] * basis).sum(axis=3)
        y = (zg + gate * response).reshape(b, c, h, w)
        return conv_gn_act(y, post_w, post_b, post_gn_g, post_gn_b)

    def _L1_conv_ref(u, W_in, conv_w, conv_b, dt_bias, A_log, D, ln_g, ln_b, W_out, H, W):
        import jax, jax.numpy as jnp
        import numpy as np
        D_MODEL = 64
        EXPAND = 2
        D_INNER = EXPAND * D_MODEL
        HEADDIM = 16
        NHEADS = D_INNER // HEADDIM
        D_STATE = 16
        CONV_DIM = D_INNER + 2 * D_STATE
        D_IN_PROJ = 2 * D_INNER + 2 * D_STATE + NHEADS
        BATCH, HH, WW = (16, 16, 16)
        B = u.shape[0]
        L = H * W
        x = jnp.transpose(u, (0, 2, 3, 1))
        zxbcdt = jnp.einsum('bhwc,oc->bhwo', x, W_in)
        z = zxbcdt[..., :D_INNER]
        xBC = zxbcdt[..., D_INNER:D_INNER + CONV_DIM]
        dt = jax.nn.softplus(zxbcdt[..., D_INNER + CONV_DIM:] + dt_bias)
        xBC = jnp.transpose(xBC, (0, 3, 1, 2))
        xBC = jax.lax.conv_general_dilated(xBC, conv_w, (1, 1), 'SAME', dimension_numbers=('NCHW', 'OIHW', 'NCHW'), feature_group_count=CONV_DIM) + conv_b[None, :, None, None]
        xBC = jax.nn.silu(xBC)
        xBC = jnp.transpose(xBC, (0, 2, 3, 1)).reshape(B, L, CONV_DIM)
        dt = dt.reshape(B, L, NHEADS)
        z = z.reshape(B, L, D_INNER)
        xs = xBC[..., :D_INNER].reshape(B, L, NHEADS, HEADDIM)
        Bm = xBC[..., D_INNER:D_INNER + D_STATE]
        Cm = xBC[..., D_INNER + D_STATE:]
        A = -jnp.exp(A_log)
        dA = -(dt * A)
        V_scaled = xs * dA[..., None]
        KV = jnp.einsum('bln,blhd->bhnd', Bm, V_scaled)
        y = jnp.einsum('bln,bhnd->blhd', Cm, KV) + xs * D[None, None, :, None]
        y = y.reshape(B, L, D_INNER)
        y = y * jax.nn.silu(z)
        mu = jnp.mean(y, axis=-1, keepdims=True)
        var = jnp.mean(jnp.square(y - mu), axis=-1, keepdims=True)
        y = (y - mu) * jax.lax.rsqrt(var + 1e-05) * ln_g + ln_b
        out = jnp.einsum('bld,od->blo', y, W_out)
        return jnp.transpose(out.reshape(B, H, W, D_MODEL), (0, 3, 1, 2))

    def _L2_conv_ref(x, Wq, bq, Wk, bk, Wv, bv, Wo, bo):
        import jax, jax.numpy as jnp
        import numpy as np
        EMBED = 64
        HEADS = 8
        HEAD_DIM = EMBED // HEADS
        B, C, H, W = x.shape
        N = H * W
        xf = jnp.transpose(x, (0, 2, 3, 1)).reshape(B, N, C)

        def proj(Wt, bt):
            y = jnp.einsum('bnc,dc->bnd', xf, Wt) + bt
            return y.reshape(B, N, HEADS, HEAD_DIM).transpose(0, 2, 1, 3)
        q = proj(Wq, bq)
        k = proj(Wk, bk)
        v = proj(Wv, bv)
        scale = 1.0 / jnp.sqrt(jnp.float32(HEAD_DIM))
        scores = jnp.einsum('bhqd,bhkd->bhqk', q, k) * scale
        attn = jax.nn.softmax(scores, axis=-1)
        ctx = jnp.einsum('bhqk,bhkd->bhqd', attn, v)
        ctx = ctx.transpose(0, 2, 1, 3).reshape(B, H, W, C)
        out = jnp.einsum('bhwc,dc->bhwd', ctx, Wo) + bo
        return jnp.transpose(out, (0, 3, 1, 2))

    def _L3_conv_ref(x, weight, bias, off_w, off_b, mask_w, mask_b):
        import jax, jax.numpy as jnp
        import numpy as np
        K = 3
        PAD = 1
        STRIDE = 1

        def conv2d(x, w, b, stride=STRIDE, pad=PAD):
            out = jax.lax.conv_general_dilated(x, w, (stride, stride), [(pad, pad), (pad, pad)], dimension_numbers=('NCHW', 'OIHW', 'NCHW'))
            return out + b[None, :, None, None]

        def deform_sample(x, offset, mask):
            B, C, H, W = x.shape
            KK = mask.shape[1]
            Ho, Wo = (offset.shape[2], offset.shape[3])
            off = offset.reshape(B, KK, 2, Ho, Wo)
            dy, dx = (off[:, :, 0], off[:, :, 1])
            ky, kx = jnp.meshgrid(jnp.arange(K), jnp.arange(K), indexing='ij')
            ky = ky.reshape(-1).astype(x.dtype)
            kx = kx.reshape(-1).astype(x.dtype)
            base_y = (jnp.arange(Ho) * STRIDE - PAD).astype(x.dtype)
            base_x = (jnp.arange(Wo) * STRIDE - PAD).astype(x.dtype)
            py = base_y[None, None, :, None] + ky[None, :, None, None] + dy
            px = base_x[None, None, None, :] + kx[None, :, None, None] + dx
            y0 = jnp.floor(py)
            x0 = jnp.floor(px)
            wy1 = py - y0
            wx1 = px - x0
            wy0 = 1.0 - wy1
            wx0 = 1.0 - wx1

            def gather(yi, xi):
                valid = ((yi >= 0) & (yi < H) & (xi >= 0) & (xi < W)).astype(x.dtype)
                yc = jnp.clip(yi, 0, H - 1).astype(jnp.int32)
                xc = jnp.clip(xi, 0, W - 1).astype(jnp.int32)
                vals = jax.vmap(lambda xb, yb, xib: xb[:, yb, xib])(x, yc, xc)
                return vals * valid[:, None]
            samp = gather(y0, x0) * (wy0 * wx0)[:, None] + gather(y0, x0 + 1.0) * (wy0 * wx1)[:, None] + gather(y0 + 1.0, x0) * (wy1 * wx0)[:, None] + gather(y0 + 1.0, x0 + 1.0) * (wy1 * wx1)[:, None]
            return samp * mask[:, None]
        offset = conv2d(x, off_w, off_b)
        mask = jax.nn.sigmoid(conv2d(x, mask_w, mask_b))
        samp = deform_sample(x, offset, mask)
        O, C = (weight.shape[0], weight.shape[1])
        out = jnp.einsum('bckhw,ock->bohw', samp, weight.reshape(O, C, K * K))
        return out + bias[None, :, None, None]

    def _gn(v, G=32, eps=1e-05):
        B_, C_, H_, W_ = v.shape
        g = v.reshape(B_, G, C_ // G, H_, W_)
        m = jnp.mean(g, axis=(2, 3, 4), keepdims=True)
        s = jnp.var(g, axis=(2, 3, 4), keepdims=True)
        return ((g - m) / jnp.sqrt(s + eps)).reshape(v.shape)

    def _ln_c(v, eps=1e-06):
        m = jnp.mean(v, axis=1, keepdims=True)
        s = jnp.var(v, axis=1, keepdims=True)
        return (v - m) / jnp.sqrt(s + eps)

    def _ln_t(v, eps=1e-05):
        m = jnp.mean(v, axis=-1, keepdims=True)
        s = jnp.var(v, axis=-1, keepdims=True)
        return (v - m) / jnp.sqrt(s + eps)

    def _to_tokens(v):
        B_, C_, H_, W_ = v.shape
        return v.reshape(B_, C_, H_ * W_).transpose(0, 2, 1)

    def _from_tokens(t, like):
        B_, C_, H_, W_ = like.shape
        return t.transpose(0, 2, 1).reshape(B_, C_, H_, W_)
    x = x + _L0_conv_ref(_gn(x), L0_conv_pre_w, L0_conv_pre_b, L0_conv_pre_gn_g, L0_conv_pre_gn_b, L0_conv_sp_w1, L0_conv_sp_b1, L0_conv_sp_w2, L0_conv_sp_b2, L0_conv_alpha_w, L0_conv_alpha_b, L0_conv_mu_w, L0_conv_mu_b, L0_conv_sigma_w, L0_conv_sigma_b, L0_conv_mix_w, L0_conv_mix_b, L0_conv_gate_w, L0_conv_gate_b, L0_conv_post_w, L0_conv_post_b, L0_conv_post_gn_g, L0_conv_post_gn_b)
    x = x + _L1_conv_ref(_gn(x), L1_conv_W_in, L1_conv_conv_w, L1_conv_conv_b, L1_conv_dt_bias, L1_conv_A_log, L1_conv_D, L1_conv_ln_g, L1_conv_ln_b, L1_conv_W_out, 16, 16)
    x = x + _L2_conv_ref(_gn(x), L2_conv_Wq, L2_conv_bq, L2_conv_Wk, L2_conv_bk, L2_conv_Wv, L2_conv_bv, L2_conv_Wo, L2_conv_bo)
    x = x + _L3_conv_ref(_gn(x), L3_conv_weight, L3_conv_bias, L3_conv_off_w, L3_conv_off_b, L3_conv_mask_w, L3_conv_mask_b)
    return x

_drawn_inputs = setup_inputs


def setup_inputs(seed=0):
    import zlib

    import numpy as np

    out = dict(_drawn_inputs(seed))
    spreads = {'L0_conv_pre_b': (0.0, 0.1),
     'L0_conv_pre_gn_g': (1.0, 0.2),
     'L0_conv_pre_gn_b': (0.0, 0.1),
     'L0_conv_sp_b1': (0.0, 0.8),
     'L0_conv_sp_b2': (0.0, 0.8),
     'L0_conv_alpha_b': (0.0, 0.8),
     'L0_conv_mu_b': (0.0, 0.586),
     'L0_conv_sigma_b': (0.0, 0.8),
     'L0_conv_mix_b': (0.0, 0.8),
     'L0_conv_gate_b': (0.0, 2.0),
     'L0_conv_post_b': (0.0, 0.1),
     'L0_conv_post_gn_g': (1.0, 0.2),
     'L0_conv_post_gn_b': (0.0, 0.1),
     'L1_conv_conv_b': (0.0, 0.1),
     'L1_conv_D': (1.0, 0.6),
     'L1_conv_ln_g': (1.0, 0.2),
     'L1_conv_ln_b': (0.0, 0.1),
     'L2_conv_bq': (0.0, 0.626),
     'L2_conv_bk': (0.0, 2.0),
     'L2_conv_bv': (0.0, 0.1),
     'L2_conv_bo': (0.0, 0.1),
     'L3_conv_bias': (0.0, 0.1)}
    factors = {'L0_conv_sp_w1': 8.0,
     'L0_conv_sp_w2': 8.0,
     'L0_conv_alpha_w': 8.0,
     'L0_conv_mu_w': 8.0,
     'L0_conv_sigma_w': 8.0,
     'L0_conv_mix_w': 8.0,
     'L0_conv_gate_w': 8.0,
     'L3_conv_mask_w': 4.121}
    for name, (base, spread) in spreads.items():
        noise = np.random.default_rng([zlib.crc32(name.encode()), seed]).standard_normal(out[name].shape)
        drawn = base * np.exp(spread * noise) if base else spread * noise
        out[name] = jnp.asarray(drawn.astype(out[name].dtype))
    for name, factor in factors.items():
        out[name] = (out[name] * factor).astype(out[name].dtype)
    return out
```

```python
from contextlib import ExitStack

import numpy as np

import concourse.bass as bass
from concourse import mybir

F32 = mybir.dt.float32
BF16 = mybir.dt.bfloat16
ALU = mybir.AluOpType
ACT = mybir.ActivationFunctionType
AX = mybir.AxisListType

B, C, H, W = 16, 64, 16, 16
N = H * W
P = 128
NP = B // 2
EPS = 1e-5

G0, NB, S0 = 4, 6, 16
NPAR = 4 * NB + 1

DI, NH1, HD1, DS1 = 128, 8, 16, 16
HP, WP = H + 2, W + 2
W3 = 3
NH2, HD2 = 8, 8
NQ = B // 4


def ds(start, size):
    return bass.ds(start, size)


class Memory:

    semaphores = None

    def __init__(self, nc, name):
        self.nc, self.name, self.ctx = nc, name, ExitStack()

    def __enter__(self):
        self.ctx.__enter__()
        return self

    def __exit__(self, *a):
        return self.ctx.__exit__(*a)

    def sb(self, name, shape, dt=F32):
        return self.ctx.enter_context(self.nc.sbuf_tensor(f"{self.name}_{name}", shape, dt))

    def ps(self, name, shape, dt=F32):
        return self.ctx.enter_context(self.nc.psum_tensor(f"{self.name}_{name}", shape, dt))

    def sem(self, name):
        return Memory.semaphores.enter_context(self.nc.semaphore(f"{self.name}_{name}"))

    def sems(self, names):
        return [self.sem(n) for n in names.split()]


class Steps:

    def __init__(self, eng, sem, n=0):
        self.eng, self.sem, self.n = eng, sem, n

    def __call__(self, ins):
        ins.then_inc(self.sem, 1)
        self.n += 1
        self.eng.wait_ge(self.sem, self.n)

    def free(self, ins):
        ins.then_inc(self.sem, 1)
        self.n += 1

    def settle(self):
        self.eng.wait_ge(self.sem, self.n)


class NormSignals:

    def __init__(self, mem):
        self.own, self.stats_ready, self.mean_ready, self.sp_ready, self.spread_ready, self.var_ready, self.sd_ready = (
            mem.sems("norm_own norm_stats norm_mean norm_sp norm_spread norm_var norm_sd"))
        self.norms = self.own_steps = 0


class GroupNorm:

    def __init__(self, mem, signals, name, avg, mean, spread):
        self.signals = signals
        signals.norms += 1
        self.turn = signals.norms
        self.avg, self.mean, self.spread = avg, mean, spread
        self.bn, self.mv = mem.sb(name + "_bn", [P, NP, 6]), mem.sb(name + "_mv", [P, NP, 2])
        self.d, self.sp, self.var, self.sd, self.scale, self.shift = (
            mem.sb(f"{name}_{n}", [P, NP]) for n in ("d", "sp", "var", "sd", "scale", "shift"))

    def vector(self, dve, source, bias=None, gamma=None, beta=None):
        on, turn = self.signals, self.turn
        step = Steps(dve, on.own, on.own_steps)
        for p in range(NP):
            step.free(dve.bn_stats(self.bn[:, p, :], source(p)))
        step.settle()
        for p in range(NP):
            step.free(dve.bn_aggr(self.mv[:, p, :], self.bn[:, p, :]))
        step.settle()
        if bias is not None:
            step(dve.tensor_scalar(self.mv[:, :, 0], self.mv[:, :, 0], bias, None, ALU.add))
        dve.sem_inc(on.stats_ready, 1)
        dve.wait_ge(on.mean_ready, turn)
        step(dve.tensor_tensor(self.d[:], self.mv[:, :, 0], self.mean, ALU.subtract))
        step(dve.tensor_tensor(self.sp[:], self.d[:], self.d[:], ALU.mult))
        dve.tensor_tensor(self.var[:], self.sp[:], self.mv[:, :, 1], ALU.add).then_inc(on.sp_ready, 1)
        dve.wait_ge(on.spread_ready, turn)
        dve.tensor_scalar(self.sp[:], self.spread, EPS, None, ALU.add).then_inc(on.var_ready, 1)
        dve.wait_ge(on.sd_ready, turn)
        step(dve.reciprocal(self.scale[:], self.sd[:]))
        if gamma is not None:
            step(dve.tensor_scalar(self.scale[:], self.scale[:], gamma, None, ALU.mult))
        if bias is None:
            step(dve.tensor_scalar(self.d[:], self.mean, -1.0, None, ALU.mult))
        else:
            step(dve.tensor_scalar(self.d[:], self.mean, bias, -1.0, ALU.subtract, ALU.mult))
        step(dve.tensor_tensor(self.shift[:], self.d[:], self.scale[:], ALU.mult))
        if beta is not None:
            step(dve.tensor_scalar(self.shift[:], self.shift[:], beta, None, ALU.add))
        on.own_steps = step.n

    def tensor(self, pe):
        on, turn = self.signals, self.turn
        pe.wait_ge(on.stats_ready, turn)
        pe.matmul(self.mean, self.avg[:], self.mv[:, :, 0], start=True, stop=True).then_inc(on.mean_ready, 1)
        pe.wait_ge(on.sp_ready, turn)
        pe.matmul(self.spread, self.avg[:], self.var[:], start=True, stop=True).then_inc(on.spread_ready, 1)

    def scalar(self, act):
        on, turn = self.signals, self.turn
        act.wait_ge(on.var_ready, turn)
        act.activation(self.sd[:], self.sp[:], ACT.Sqrt).then_inc(on.sd_ready, 1)


def layer0(nc, ins, signals, x, x_in, avg2):
    with Memory(nc, "L0") as m:
        w_pre, w_post, avg8, same_group, w_s2 = (m.sb(n, [P, P]) for n in ("w_pre", "w_post", "avg8", "same_group", "w_s2"))
        w_s1, w_par, b_par = m.sb("w_s1", [P, 32]), m.sb("w_par", [P, NPAR]), m.sb("b_par", [P, NPAR])
        b_s1, b_s2, vec = m.sb("b_s1", [P, 1]), m.sb("b_s2", [P, 1]), m.sb("vec", [P, 6])
        xn, z = m.sb("xn", [P, NP, N]), m.sb("z", [P, NP, N])
        pooled, h1, h2, h2_sel = m.sb("pooled", [P, NP]), m.sb("h1", [32, NP]), m.sb("h2", [P, NP]), m.sb("h2_sel", [P, NP, P])
        par = m.sb("par", [P, NP, NPAR])
        ealpha, esigma, lnsigma, sigma, inv, minus_mu, mix, c0, c1, zc0, zc1, alpha = (
            m.sb(n, [P, NP, NB]) for n in ("ealpha", "esigma", "lnsigma", "sigma", "inv", "minus_mu", "mix", "c0", "c1", "zc0", "zc1", "alpha"))
        amax, asum, gate = m.sb("amax", [P, NP]), m.sb("asum", [P, NP]), m.sb("gate", [P, NP])
        uu, ex, poly, t = (m.sb(n, [P, 2, NB, N]) for n in ("uu", "ex", "poly", "t"))
        y1, y2 = m.ps("y1", [P, NP, N]), m.ps("y2", [P, NP, N])
        gn_x = GroupNorm(m, signals, "gn_x", avg2, y2[:, 0, 0:NP], y2[:, 2, 0:NP])
        gn_1 = GroupNorm(m, signals, "gn_1", avg8, y2[:, 0, 0:NP], y2[:, 2, 0:NP])
        gn_2 = GroupNorm(m, signals, "gn_2", avg8, y1[:, 0, 0:NP], y1[:, 2, 0:NP])
        s1, s2 = y2[0:32, 4, 0:NP], y2[:, 6, 0:NP]
        par_ps = y2[:, 4, 0:NP * NPAR].rearrange("p (n k) -> p n k", n=NP)

        (loaded, own, xn_ready, y1_ready, norm1_ready, z_ready, s1_ready, h1_ready, s2_ready, h2_ready, sel_ready,
         par_ready, exp_in, exp_out, coef_ready) = m.sems(
            "loaded own xn_ready y1_ready norm1_ready z_ready s1_ready h1_ready s2_ready h2_ready sel_ready "
            "par_ready exp_in exp_out coef_ready")
        (uu_ready, e_ready, poly_ready, t_ready, t_used, norm2_ready, out_ready, added) = m.sems(
            "uu_ready e_ready poly_ready t_ready t_used norm2_ready out_ready added")
        LOADS = [(w_pre[:], "w_pre"), (avg8[:], "avg8"), (vec[:], "l0_vec"), (w_s1[:], "w_s1"), (b_s1[0:32, :], "b_s1"),
                 (w_s2[0:32, :], "w_s2"), (b_s2[:], "b_s2"), (same_group[:], "same_group"), (w_par[:], "w_par"),
                 (b_par[:], "b_par"), (w_post[:], "w_post")]

        with nc.Block() as block:
            @block.sync
            def _(sp):
                for dst, src in LOADS:
                    sp.dma_start(dst, ins[src]).then_inc(loaded, 16)

            @block.vector
            def _(dve):
                def x_pair(p):
                    if p == 0:
                        dve.wait_ge(x_in, 32)
                    return x[:, p, :]

                gn_x.vector(dve, x_pair)
                for p in range(NP):
                    dve.tensor_scalar(xn[:, p, :], x[:, p, :], gn_x.scale[:, p:p + 1], gn_x.shift[:, p:p + 1],
                                      ALU.mult, ALU.add).then_inc(xn_ready, 1)

                def y1_pair(p):
                    if p % 2 == 0:
                        dve.wait_ge(y1_ready, p // 2 + 1)
                    return y1[:, p, :]

                dve.wait_ge(loaded, 16 * len(LOADS))
                gn_1.vector(dve, y1_pair, vec[:, 0:1], vec[:, 1:2], vec[:, 2:3])
                dve.sem_inc(norm1_ready, 1)

                step = Steps(dve, own)
                dve.wait_ge(h2_ready, 1)
                for p in range(NP):
                    dve.tensor_scalar(h2_sel[:, p, :], same_group[:], h2[:, p:p + 1], None, ALU.mult).then_inc(sel_ready, 1)
                dve.wait_ge(par_ready, 1)
                step(dve.tensor_tensor(par[:], par_ps, b_par[:, :].unsqueeze(1).broadcast_to([P, NP, NPAR]), ALU.add))
                al, mu, sg, mx = (par[:, :, NB * k:NB * (k + 1)] for k in range(4))
                per_basis = lambda v: v[:, :].unsqueeze(2).broadcast_to([P, NP, NB])
                step(dve.tensor_reduce(amax[:], al, AX.X, ALU.max))
                step(dve.tensor_tensor(alpha[:], al, per_basis(amax), ALU.subtract))
                step(dve.tensor_scalar(sigma[:], sg, -1.0, None, ALU.mult))
                step(dve.tensor_tensor(sigma[:], sigma[:], sg, ALU.min))
                dve.sem_inc(exp_in, 1)
                dve.wait_ge(exp_out, 5)
                step(dve.tensor_reduce(asum[:], ealpha[:], AX.X, ALU.add))
                step(dve.tensor_scalar(gate[:], gate[:], 1.0, None, ALU.add))
                step(dve.tensor_tensor(asum[:], asum[:], gate[:], ALU.mult))
                step(dve.reciprocal(asum[:], asum[:]))
                step(dve.tensor_tensor(alpha[:], ealpha[:], per_basis(asum), ALU.mult))
                step(dve.tensor_scalar(mix[:], mix[:], 1.0, None, ALU.add))
                step(dve.reciprocal(mix[:], mix[:]))
                step(dve.scalar_tensor_tensor(out=sigma[:], in0=sg, scalar=0.0, in1=lnsigma[:], op0=ALU.max, op1=ALU.add))
                step(dve.tensor_scalar(sigma[:], sigma[:], 0.001, None, ALU.add))
                step(dve.reciprocal(inv[:], sigma[:]))
                step(dve.scalar_tensor_tensor(out=minus_mu[:], in0=mu, scalar=-1.0, in1=inv[:], op0=ALU.mult, op1=ALU.mult))
                dve.sem_inc(coef_ready, 1)
                step(dve.tensor_tensor(c0[:], alpha[:], mix[:], ALU.mult))
                step(dve.tensor_tensor(c1[:], alpha[:], c0[:], ALU.subtract))
                step(dve.tensor_tensor(zc1[:], c1[:], inv[:], ALU.mult))
                step(dve.tensor_tensor(zc0[:], c1[:], minus_mu[:], ALU.mult))
                step(dve.tensor_tensor(zc0[:], zc0[:], c0[:], ALU.add))
                dve.sem_inc(t_ready, 2)

                with dve.Fori(0, NP // 2) as i:
                    for q in range(2):
                        k = 2 * i + q
                        dve.wait_ge(t_ready, k + 1)
                        for j in range(NB):
                            dve.tensor_scalar(poly[:, q, j, :], z[:, ds(k, 1), :], zc1[:, ds(k, 1), j], zc0[:, ds(k, 1), j],
                                              ALU.mult, ALU.add).then_inc(poly_ready, 1)
                        dve.wait_ge(poly_ready, NB * k + NB)
                        dve.wait_ge(e_ready, k + 1)
                        dve.wait_ge(t_used, k + 1)
                        dve.tensor_tensor(t[:, q], poly[:, q], ex[:, q], ALU.mult).then_inc(t_ready, 1)

                def y2_pair(p):
                    dve.wait_ge(t_used, (p | 1) + 3)
                    return y2[:, p, :]

                gn_2.vector(dve, y2_pair, vec[:, 3:4], vec[:, 4:5], vec[:, 5:6])
                dve.sem_inc(norm2_ready, 1)
                for p in range(NP):
                    dve.wait_ge(out_ready, p + 1)
                    dve.tensor_tensor(x[:, p, :], x[:, p, :], xn[:, p, :], ALU.add).then_inc(added, 1)
                dve.wait_ge(added, NP)

            @block.tensor
            def _(pe):
                pe.wait_ge(loaded, 16 * len(LOADS))
                gn_x.tensor(pe)
                for h in range(NP // 2):
                    pe.wait_ge(xn_ready, 2 * h + 2)
                    pe.matmul(y1[:, 2 * h:2 * h + 2, :], w_pre[:], xn[:, 2 * h:2 * h + 2, :], start=True, stop=True).then_inc(y1_ready, 1)
                gn_1.tensor(pe)
                pe.wait_ge(z_ready, NP)
                pe.matmul(s1, w_s1[:], pooled[:], start=True, stop=True).then_inc(s1_ready, 1)
                pe.wait_ge(h1_ready, 1)
                pe.matmul(s2, w_s2[0:32, :], h1[:], start=True, stop=True).then_inc(s2_ready, 1)
                for p in range(NP):
                    pe.wait_ge(sel_ready, p + 1)
                    mm = pe.matmul(par_ps[:, p, :], h2_sel[:, p, :], w_par[:], start=True, stop=True)
                mm.then_inc(par_ready, 1)
                pe.sem_inc(t_used, 2)
                pe.wait_ge(coef_ready, 1)
                with pe.Fori(0, NP // 2) as i:
                    for q in range(2):
                        k = 2 * i + q
                        pe.matmul(y2[:, ds(k, 1), :], w_post[:], z[:, ds(k, 1), :], start=True, stop=False)
                        pe.wait_ge(t_ready, k + 3)
                        for j in range(NB):
                            mm = pe.matmul(y2[:, ds(k, 1), :], w_post[:], t[:, q, j:j + 1, :], start=False, stop=(j == NB - 1))
                        mm.then_inc(t_used, 1)
                gn_2.tensor(pe)

            @block.scalar
            def _(act):
                gn_x.scalar(act)
                gn_1.scalar(act)
                act.wait_ge(norm1_ready, 1)
                for p in range(NP):
                    act.activation(z[:, p, :], y1[:, p, :], ACT.Silu, scale=gn_1.scale[:, p:p + 1], bias=gn_1.shift[:, p:p + 1],
                                   accum_out=pooled[:, p:p + 1]).then_inc(z_ready, 1)
                act.wait_ge(s1_ready, 1)
                act.activation(h1[:], s1, ACT.Gelu_apprx_tanh, scale=1.0 / N, bias=b_s1[0:32, :]).then_inc(h1_ready, 1)
                act.wait_ge(s2_ready, 1)
                act.activation(h2[:], s2, ACT.Gelu_apprx_tanh, bias=b_s2[:]).then_inc(h2_ready, 1)
                act.wait_ge(exp_in, 1)
                act.activation(ealpha[:], alpha[:], ACT.Exp).then_inc(exp_out, 1)
                act.activation(esigma[:], sigma[:], ACT.Exp).then_inc(exp_out, 1)
                act.activation(mix[:], par[:, :, 3 * NB:4 * NB], ACT.Exp, scale=-1.0).then_inc(exp_out, 1)
                act.activation(gate[:], par[:, :, NPAR - 1], ACT.Exp, scale=-1.0).then_inc(exp_out, 1)
                act.wait_ge(exp_out, 4)
                act.activation(lnsigma[:], esigma[:], ACT.Ln, bias=1.0).then_inc(exp_out, 1)
                act.wait_ge(coef_ready, 1)
                with act.Fori(0, NP // 2) as i:
                    for q in range(2):
                        k = 2 * i + q
                        act.wait_ge(t_ready, k + 1)
                        for j in range(NB):
                            act.activation(uu[:, q, j, :], z[:, ds(k, 1), :], ACT.Square, scale=inv[:, ds(k, 1), j],
                                           bias=minus_mu[:, ds(k, 1), j]).then_inc(uu_ready, 1)
                        act.wait_ge(uu_ready, NB * k + NB)
                        act.activation(ex[:, q], uu[:, q], ACT.Exp, scale=-1.0).then_inc(e_ready, 1)
                gn_2.scalar(act)
                act.wait_ge(norm2_ready, 1)
                for p in range(NP):
                    act.activation(xn[:, p, :], y2[:, p, :], ACT.Silu, scale=gn_2.scale[:, p:p + 1],
                                   bias=gn_2.shift[:, p:p + 1]).then_inc(out_ready, 1)


def pad_stack(nc, pool, edge_ready, xpad, stack):
    pool.memset(xpad[:], 0.0).then_inc(edge_ready, 1)
    pool.wait_ge(edge_ready, 1)
    pool.memset(stack[C:P, :, H * WP + WP:HP * WP], 0.0).then_inc(edge_ready, 1)


def send_stack(sp, xpad_ready, stack_in, xpad, stack):
    for g in range(NQ):
        sp.wait_ge(xpad_ready, 2 * g + 2)
        src = xpad[:, 2 * g:2 * g + 2, :]
        dst = stack[:, 4 * g:4 * g + 4, :].rearrange("p (n e) s -> p n e s", e=2)
        for e in range(2):
            sp.dma_start(dst[0:C, :, e, :], src[C * e:C * e + C]).then_inc(stack_in[g], 16)
            sp.dma_start(dst[C:P, :, e, 0:(HP - 1) * WP], src[C * e:C * e + C, :, WP:HP * WP]).then_inc(stack_in[g], 16)


def image(stack, b, n=1):
    return stack[:, ds(b, n), :].rearrange("p n (r c) -> p n r c", c=WP)


def tap(stack, b, g, n=1):
    r, c = (0, g) if g < 3 else (2, g - 3)
    return image(stack, b, n)[:, :, r:r + H, c:c + W]


def layer1(nc, ins, signals, x, avg2):
    with Memory(nc, "L1") as m:
        w_in, cw = m.sb("w_in", [P, DI + 32]), m.sb("cw", [P, 6, DI + 32])
        w_tap = m.sb("w_tap", [P, 6, DI + 32])
        w_z, w_dt, w_out, w_out2, w_cen = m.sb("w_z", [P, DI]), m.sb("w_dt", [P, 32]), m.sb("w_out", [P, C]), m.sb("w_out2", [P, P]), m.sb("w_cen", [P, C])
        w_g = m.sb("w_g", [P, C])
        ident, center, ones = m.sb("ident", [P, P]), m.sb("center", [P, P]), m.sb("ones", [P, C])
        quarter, vec = m.sb("quarter", [P, 4]), m.sb("vec", [P, 7])
        a_exp, b_out = m.sb("a_exp", [P, 1]), m.sb("b_out", [P, 1])
        xpad, stack = m.sb("xpad", [P, NP, HP * WP]), m.sb("stack", [P, B, HP * WP])
        dt, dt_e, da = m.sb("dt", [P, NQ, N]), m.sb("dt_e", [P, NQ, N]), m.sb("da", [P, NQ, N])
        xs, zs, bc = m.sb("xs", [P, 4, N]), m.sb("zs", [P, 4, N]), m.sb("bc", [P, NQ, N])
        b_t, bt_all, da_t, v = m.sb("b_t", [P, 2, 4, 32]), m.sb("bt_all", [P, NQ, 2, 4, DS1]), m.sb("da_t", [P, NQ, 2, 4, NH1]), m.sb("v", [P, 2, 4, DI])
        kv, y, sq = m.sb("kv", [P, 4, DI]), m.sb("y", [P, 4, N]), m.sb("sq", [P, 4, N])
        o_all, var_all = m.sb("o_all", [P, NP, N]), m.sb("var_all", [P, NP, N])
        xs_ps, z_ps, bc_ps = m.ps("xs_ps", [P, 4, N]), m.ps("z_ps", [P, 4, N]), m.ps("bc_ps", [P, NP])
        t_ps, k_ps = m.ps("t_ps", [P, 2, 4, DI]), m.ps("k_ps", [P, 2, N])
        gn = GroupNorm(m, signals, "gn", avg2, k_ps[:, 0, 0:NP], bc_ps[:])
        flat = lambda ap: ap.rearrange("p a n -> p (a n)")
        t_y = t_ps[:, :, :, :].rearrange("p h j d -> p (h j d)").rearrange("p (j n) -> p j n", n=N)

        (loaded, weights_in, own, edge_ready, xpad_ready, tap_ready, g_ready, cen_ps, cen_ready, dt_ps, dt_v, dt_exp, dt_ln, act_own, da_tps, bc_conv, bc_ready) = m.sems(
            "loaded weights_in own edge_ready xpad_ready tap_ready g_ready cen_ps cen_ready dt_ps dt_v dt_exp dt_ln act_own da_tps bc_conv bc_ready")
        stack_in = m.sems("stack_in0 stack_in1 stack_in2 stack_in3")
        (conv_ready, acts_ready, bt_ready, xt_ready, bt_copied, v_ready, kv_ps, kv_ready, y_ps, y_own, y_ready, cen_y, sq_ready, o_ready,
         var_ready, o_copied) = m.sems(
            "conv_ready acts_ready bt_ready xt_ready bt_copied v_ready kv_ps kv_ready y_ps y_own y_ready cen_y sq_ready o_ready var_ready o_copied")
        added, sd_ready, sd_in = m.sems("added sd_ready sd_in")
        LOADS = [(w_in[:], "w_in"), (w_z[:], "w_z"), (w_dt[:], "w_dt"), (w_out[:], "w_out"), (w_out2[:], "w_out2"),
                 (ident[:], "ident"), (center[:], "center"), (ones[:], "ones"), (quarter[:], "quarter"), (vec[:], "l1_vec")]
        LOADS += [(cw[C * e:C * e + C, 3 * k:3 * k + 3, :], ins["conv_w"][2 * k + e:2 * k + e + 1].broadcast_to([C, 3, DI + 32]))
                  for k, e in ((0, 0), (0, 1), (1, 0))]

        with nc.Block() as block:
            @block.sync
            def _(sp):
                for dst, src in LOADS:
                    sp.dma_start(dst, ins[src] if isinstance(src, str) else src).then_inc(loaded, 16)
                sp.wait_ge(edge_ready, 3)
                send_stack(sp, xpad_ready, stack_in, xpad, stack)

            @block.gpsimd
            def _(pool):
                pad_stack(nc, pool, edge_ready, xpad, stack)
                pool.wait_ge(edge_ready, 2)
                pool.memset(cw[C:P, 3:6, :], 0.0).then_inc(edge_ready, 1)
                pool.wait_ge(edge_ready, 3)
                pool.memset(b_t[:], 0.0).then_inc(edge_ready, 1)

            @block.vector
            def _(dve):
                gn.vector(dve, lambda p: x[:, p, :])
                dve.wait_ge(edge_ready, 4)
                for p in range(NP):
                    dst = xpad[:, p, :].rearrange("p (r c) -> p r c", c=WP)[:, 1:1 + H, 1:1 + W]
                    dve.tensor_scalar(dst, x[:, p, :].rearrange("p (r c) -> p r c", c=W), gn.scale[:, p:p + 1], gn.shift[:, p:p + 1],
                                      ALU.mult, ALU.add).then_inc(xpad_ready, 1)
                dve.wait_ge(loaded, 16 * len(LOADS))
                dve.tensor_tensor(w_tap[:], cw[:], w_in[:, :].unsqueeze(1).broadcast_to([P, 6, DI + 32]), ALU.mult).then_inc(tap_ready, 1)
                dve.tensor_scalar(w_g[:], w_out[:], vec[:, 3:4], None, ALU.mult).then_inc(g_ready, 1)
                dve.wait_ge(cen_ps, 2)
                dve.tensor_copy(w_cen[:], k_ps[:, 0, 0:C]).then_inc(cen_ready, 1)
                dve.tensor_copy(b_out[:], k_ps[:, 0, C:C + 1]).then_inc(cen_ready, 1)
                step = Steps(dve, own)
                dve.wait_ge(dt_ps, 16)
                step(dve.tensor_scalar(dt[:], t_y, vec[:, 5:6], None, ALU.add))
                step(dve.scalar_tensor_tensor(out=dt_e[:], in0=dt[:], scalar=-1.0, in1=dt[:], op0=ALU.mult, op1=ALU.min))
                dve.sem_inc(dt_v, 1)
                dve.wait_ge(dt_ln, 1)
                step(dve.scalar_tensor_tensor(out=da[:], in0=dt[:], scalar=0.0, in1=da[:], op0=ALU.max, op1=ALU.add))
                step(dve.tensor_scalar(da[:], da[:], a_exp[:], None, ALU.mult))
                dve.sem_inc(dt_v, 1)
                dve.wait_ge(da_tps, 1)
                step(dve.tensor_copy(da_t[:].rearrange("p q h j k -> p (q h j) k"), t_ps[:].rearrange("p a j (e k) -> p (a j e) k", k=32)[:, :, 0:NH1]))
                dve.wait_ge(bt_ready, 1)
                step(dve.tensor_copy(bt_all[:].rearrange("p q h j k -> p (q h j) k"),
                                     z_ps[:].rearrange("p q (h j k) -> p (q h j) k", h=2, k=32)[:, :, 0:DS1]))
                dve.sem_inc(y_ready, 2)
                dve.sem_inc(o_copied, 2)
                with dve.Fori(0, NQ) as q:
                    dve.tensor_copy(b_t[:, :, :, DS1:2 * DS1].rearrange("p h j k -> p (h j) k"),
                                    bt_all[:, ds(q, 1)].rearrange("p q h j k -> p (q h j) k")).then_inc(bt_copied, 1)
                    dve.wait_ge(xt_ready, q + 1)
                    for h in range(2):
                        dve.tensor_tensor(v[:, h].rearrange("p j (h d) -> p (j h) d", d=HD1),
                                          t_ps[:, h].rearrange("p j (h d) -> p (j h) d", d=HD1),
                                          da_t[:, ds(q, 1), h].rearrange("p q j h -> p (q j h)").unsqueeze(2).broadcast_to([P, 4 * NH1, HD1]),
                                          ALU.mult).then_inc(v_ready, 1)
                    dve.wait_ge(kv_ps, q + 1)
                    dve.tensor_tensor(kv[:], k_ps[:, 0, 0:DI].unsqueeze(1).broadcast_to([P, 4, DI]),
                                      quarter[:, :].unsqueeze(2).broadcast_to([P, 4, DI]), ALU.mult).then_inc(kv_ready, 1)
                    dve.wait_ge(y_ps, q + 1)
                    for h in range(2):
                        dve.scalar_tensor_tensor(out=y[:, 2 * h:2 * h + 2, :], in0=xs[:, 2 * h:2 * h + 2, :], scalar=vec[:, 2:3],
                                                 in1=t_y[:, 2 * h:2 * h + 2, :], op0=ALU.mult, op1=ALU.add).then_inc(y_own, 1)
                    dve.wait_ge(acts_ready, 2 * q + 2)
                    for h in range(2):
                        dve.wait_ge(y_own, 2 * q + 1 + h)
                        dve.tensor_tensor(y[:, 2 * h:2 * h + 2, :], y[:, 2 * h:2 * h + 2, :], zs[:, 2 * h:2 * h + 2, :],
                                          ALU.mult).then_inc(y_ready, 1)
                    dve.wait_ge(o_ready, q + 1)
                    dve.tensor_copy(o_all[:, ds(2 * q, 2), :], k_ps[:]).then_inc(o_copied, 1)
                    dve.wait_ge(var_ready, q + 1)
                    dve.tensor_copy(var_all[:, ds(2 * q, 2), :], t_y[:, 0:2, :]).then_inc(o_copied, 1)
                dve.wait_ge(o_copied, 2 * NQ + 2)
                for h in range(2):
                    r = slice(4 * h, 4 * h + 4)
                    step(dve.tensor_scalar(var_all[:, r, :], var_all[:, r, :], EPS, None, ALU.add))
                    dve.sem_inc(sd_in, 1)
                for h in range(2):
                    r = slice(4 * h, 4 * h + 4)
                    dve.wait_ge(sd_ready, h + 1)
                    step(dve.reciprocal(var_all[:, r, :], var_all[:, r, :]))
                    step(dve.tensor_tensor(o_all[:, r, :], o_all[:, r, :], var_all[:, r, :], ALU.mult))
                    step(dve.scalar_tensor_tensor(out=x[:, r, :], in0=o_all[:, r, :], scalar=b_out[:], in1=x[:, r, :], op0=ALU.add, op1=ALU.add))

            @block.scalar
            def _(act):
                gn.scalar(act)
                act.wait_ge(loaded, 16 * len(LOADS))
                act.activation(a_exp[:], vec[:, 6:7], ACT.Exp).then_inc(act_own, 1)
                act.wait_ge(dt_v, 1)
                act.activation(dt_e[:], dt_e[:], ACT.Exp).then_inc(dt_exp, 1)
                act.wait_ge(dt_exp, 1)
                act.wait_ge(act_own, 1)
                act.activation(da[:], dt_e[:], ACT.Ln, bias=1.0).then_inc(dt_ln, 1)
                act.wait_ge(bc_conv, 1)
                act.activation(bc[:], z_ps[:], ACT.Silu, bias=vec[:, 1:2]).then_inc(bc_ready, 1)
                with act.Fori(0, NQ) as q:
                    act.wait_ge(conv_ready, 2 * q + 2)
                    act.wait_ge(y_ready, 2 * q + 2)
                    act.activation(xs[:], xs_ps[:], ACT.Silu, bias=vec[:, 0:1]).then_inc(acts_ready, 1)
                    act.activation(zs[:], z_ps[:], ACT.Silu).then_inc(acts_ready, 1)
                    act.wait_ge(cen_y, q + 1)
                    act.activation(sq[:], t_y, ACT.Square).then_inc(sq_ready, 1)
                for h in range(2):
                    r = slice(4 * h, 4 * h + 4)
                    act.wait_ge(sd_in, h + 1)
                    act.activation(var_all[:, r, :], var_all[:, r, :], ACT.Sqrt).then_inc(sd_ready, 1)

            @block.tensor
            def _(pe):
                gn.tensor(pe)
                pe.wait_ge(loaded, 16 * len(LOADS))
                pe.wait_ge(g_ready, 1)
                pe.matmul(k_ps[:, 0, 0:C], center[:], w_g[:], start=True, stop=True).then_inc(cen_ps, 1)
                pe.matmul(k_ps[:, 0, C:C + 1], w_out2[:], vec[:, 4:5], start=True, stop=True).then_inc(cen_ps, 1)
                for g in range(NQ):
                    pe.wait_ge(stack_in[g], 64)
                    for j in range(4):
                        pe.matmul(t_y[32 * j:32 * j + 32, g, :], w_dt[:], image(stack, 4 * g + j)[:, 0, 1:1 + H, 1:1 + W],
                                  start=True, stop=True).then_inc(dt_ps, 1)
                pe.wait_ge(tap_ready, 1)

                def conv_xs(q, h):
                    for g in range(6):
                        mm = pe.matmul(xs_ps[:, 2 * h:2 * h + 2, :], w_tap[:, g, 0:DI], tap(stack, 4 * q + 2 * h, g, 2),
                                       start=(g == 0), stop=(g == 5))
                    if h == 1:
                        mm.then_inc(conv_ready, 1)

                def conv_bc(q):
                    for g in range(6):
                        for j in range(4):
                            mm = pe.matmul(z_ps[32 * j:32 * j + 32, q, :], w_tap[:, g, DI:DI + 32], tap(stack, 4 * q + j, g),
                                           start=(g == 0), stop=(g == 5))
                    return mm

                def proj_z(q):
                    for h in range(2):
                        mm = pe.matmul(z_ps[:, 2 * h:2 * h + 2, :], w_z[:], image(stack, 4 * q + 2 * h, 2)[:, :, 1:1 + H, 1:1 + W],
                                       start=True, stop=True)
                    mm.then_inc(conv_ready, 1)

                def quad(q, more):
                    pe.wait_ge(o_copied, 2 * q + 2)
                    pe.wait_ge(acts_ready, 2 * q + 1)
                    for h in range(2):
                        for j in range(4):
                            mm = pe.transpose(t_ps[:, h, j, :], xs[:, j, h * P:(h + 1) * P], ident[:])
                    mm.then_inc(xt_ready, 1)
                    if more:
                        conv_xs(q + 1, 0)
                    pe.wait_ge(bt_copied, q + 1)
                    pe.wait_ge(v_ready, 2 * q + 2)
                    for h in range(2):
                        for j in range(4):
                            mm = pe.matmul(k_ps[32 * j:32 * j + 32, 0, 0:DI], b_t[:, h, j, :], v[:, h, j, :], start=(h == 0), stop=(h == 1))
                    mm.then_inc(kv_ps, 1)
                    if more:
                        conv_xs(q + 1, 1)
                    pe.wait_ge(kv_ready, q + 1)
                    for j in range(4):
                        mm = pe.matmul(t_y[:, j, :], kv[:, j, :], bc[:, ds(q, 1), :], start=True, stop=True)
                    mm.then_inc(y_ps, 1)
                    if more:
                        pe.wait_ge(acts_ready, 2 * q + 2)
                        proj_z(q + 1)
                    pe.wait_ge(y_ready, 2 * q + 4)
                    for h in range(2):
                        mm = pe.matmul(t_y[:, 2 * h:2 * h + 2, :], center[:], y[:, 2 * h:2 * h + 2, :], start=True, stop=True)
                    mm.then_inc(cen_y, 1)
                    for j in range(4):
                        mm = pe.matmul(k_ps[C * (j % 2):C * (j % 2) + C, j // 2, :], w_cen[:], y[:, j, :], start=True, stop=True)
                    mm.then_inc(o_ready, 1)
                    pe.wait_ge(sq_ready, q + 1)
                    for j in range(4):
                        mm = pe.matmul(t_y[C * (j % 2):C * (j % 2) + C, j // 2, :], ones[:], sq[:, j, :], start=True, stop=True)
                    mm.then_inc(var_ready, 1)

                for g in range(NQ):
                    mm = conv_bc(g)
                mm.then_inc(bc_conv, 1)
                for h in range(2):
                    conv_xs(0, h)
                pe.wait_ge(dt_v, 2)
                for g in range(NQ):
                    for h in range(2):
                        mm = pe.transpose(t_ps[:, g // 2, 2 * (g % 2) + h, :], da[:, g, h * P:(h + 1) * P], ident[:])
                mm.then_inc(da_tps, 1)
                pe.wait_ge(bc_ready, 1)
                for g in range(NQ):
                    for h in range(2):
                        mm = pe.transpose(z_ps[:, g, h * P:(h + 1) * P], bc[:, g, h * P:(h + 1) * P], ident[:])
                mm.then_inc(bt_ready, 1)
                pe.wait_ge(y_ready, 2)
                proj_z(0)
                with pe.Fori(0, NQ - 1) as q:
                    quad(q, True)
                quad(NQ - 1, False)


def layer2(nc, ins, signals, x, avg2):
    TOP = 48
    with Memory(nc, "L2") as m:
        w_q, w_k, w_v, ident = (m.sb(n, [P, P]) for n in ("w_q", "w_k", "w_v", "ident"))
        w_o, b_v, vec = m.sb("w_o", [P, 2, C]), m.sb("b_v", [P, P]), m.sb("vec", [P, 3])
        xn = m.sb("xn", [P, NP, N])
        full, rest = m.sb("full", [P, 2, 2 * N]), m.sb("rest", [P, 2, 2 * N])
        parts = m.sb("parts", [P, 4, 2, 3, 2 * N], BF16)
        k_st, q_st = m.sb("k_st", [P, 4, B, N], BF16), m.sb("q_st", [P, 2, 4, B, N], BF16)
        v_all, v_x = m.sb("v_all", [P, NP, 2, 2, C]), m.sb("v_x", [P, 2, 2, NH2, 32])
        e = m.sb("e", [P, 8, 2 * N])
        mx, m_parts = m.sb("mx", [P, 2, 2, 8]), m.sb("m_parts", [8, 2, 2, N], BF16)
        ctx, ctx_r, ctx_n, ctx_c = m.sb("ctx", [P, 2, 2, N]), m.sb("ctx_r", [P, 16]), m.sb("ctx_n", [P, 2, 2, 4 * HD2]), m.sb("ctx_c", [P, P])
        ring, ctx_ps, a_ps, m_ps = m.ps("ring", [P, 4, 2 * N]), m.ps("ctx_ps", [P, 2, 2 * N]), m.ps("a_ps", [P, 2 * N]), m.ps("m_ps", [P, 2 * N])
        k_bank = lambda g: [ctx_ps[:, 0], ctx_ps[:, 1], a_ps[:], m_ps[:]][g]
        gn = GroupNorm(m, signals, "gn", avg2, a_ps[:, 0:NP], m_ps[:, 0:NP])
        scratch = [nc.dram_tensor(f"L2_{n}_parts", (2, 3, HD2, 4, B, N), BF16, kind="Internal").ap() for n in "qk"]

        (loaded, own, filled, xn_ready, q_ps_ready, k_ps_ready, full_ready, hi_ready, parts_ready, v_ps_ready, v_all_ready,
         pool_own) = m.sems("loaded own filled xn_ready q_ps_ready k_ps_ready full_ready hi_ready parts_ready v_ps_ready v_all_ready pool_own")
        stored = m.sems("stored0 stored1 stored2 stored3")
        stacked = m.sems("stacked0 stacked1 stacked2 stacked3")
        (max_ps, max_read, mx_turned, m_ready, m_stacked, s_ready, e_ready, ev_done, ctx_ready, ctx_turned, ctx_normed, ctx_back,
         ctx_copied, o_ready, o_added, v_x_ready, norm_own, passed) = m.sems(
            "max_ps max_read mx_turned m_ready m_stacked s_ready e_ready ev_done ctx_ready ctx_turned ctx_normed ctx_back "
            "ctx_copied o_ready o_added v_x_ready norm_own passed")
        LOADS = [(t[:], n) for t, n in ((w_q, "w_q"), (w_k, "w_k"), (w_v, "w_v"), (ident, "ident"), (w_o, "w_o"), (b_v, "b_v"), (vec, "l2_vec"))]

        with nc.Block() as block:
            @block.sync
            def _(sp):
                for dst, src in LOADS:
                    sp.dma_start(dst, ins[src]).then_inc(loaded, 16)
                sp.sem_inc(m_stacked, 128)
                sp.wait_ge(filled, 4)
                for g in range(NQ):
                    sp.wait_ge(parts_ready, 2 * g + 2)
                    two = slice(2 * g, 2 * g + 2)
                    for s in range(2):
                        for b in range(2):
                            for h in range(2):
                                dst = scratch[s].rearrange("e t d h (b n) s -> b e (d h) t n s", b=2)[b, h, :, :, two]
                                src = parts[C * b + 32 * h:C * b + 32 * h + 32, g, s].rearrange("p t (n s) -> p t n s", n=2)
                                sp.dma_start(dst, src).then_inc(stored[g], 16)
                    sp.wait_ge(stored[g], 128)
                    for h in range(2):
                        for s, pieces in ((0, [(slot, part, 1) for slot, part in enumerate((0, 0, 0, 1, 1, 2))]),
                                          (1, [(0, 0, 3), (3, 0, 2), (5, 0, 1)])):
                            for slot, part, count in pieces:
                                rows = slice(64 * h + HD2 * slot, 64 * h + HD2 * (slot + count))
                                dst = (q_st[rows, h] if s == 0 else k_st[rows]).rearrange("r h (b n) s -> r (h b) n s", b=2)[:, :, two]
                                src = scratch[s][h, part:part + count].rearrange("t d h (b n) s -> (t d) (h b) n s", b=2)[:, :, two]
                                sp.dma_start(dst, src).then_inc(stacked[g], 16)
                with sp.Fori(0, NP) as i:
                    for b in range(2):
                        n = 2 * i + b
                        sp.wait_ge(m_ready, 2 * n + 2)
                        sp.sem_inc(passed, 1)
                        for h in range(2):
                            for t in range(2):
                                dst = q_st[64 * h + TOP + t:64 * h + TOP + t + 1, h, :, ds(NP * b + i, 1), :]
                                sp.dma_start(dst, m_parts[4 * h:4 * h + 4, b, t, :]).then_inc(m_stacked, 16)
                        sp.wait_ge(m_stacked, 64 * n + 192)
                        sp.sem_inc(passed, 1)

            @block.gpsimd
            def _(pool):
                pool.memset(q_st[:], 0.0).then_inc(filled, 1)
                pool.wait_ge(filled, 1)
                for h in range(2):
                    pool.memset(k_st[64 * h + 32:64 * h + 64], 1.0).then_inc(filled, 1)
                    pool.wait_ge(filled, 2 + h)
                pool.memset(v_x[:], 0.0).then_inc(pool_own, 1)
                pool.wait_ge(pool_own, 1)
                pool.memset(v_x[:, :, :, :, HD2:HD2 + 1], 1.0).then_inc(filled, 1)
                pool.wait_ge(v_all_ready, 2)
                with pool.Fori(0, NP) as i:
                    for b in range(2):
                        n = 2 * i + b
                        pool.wait_ge(ev_done, 2 * n + 2)
                        pool.tensor_copy(v_x[:, b, :, :, 0:HD2],
                                         v_all[:, ds(i, 1), :, b, :].rearrange("p i t (h d) -> p (i t) h d", d=HD2)).then_inc(v_x_ready, 1)

            @block.vector
            def _(dve):
                gn.vector(dve, lambda p: x[:, p, :])
                for p in range(NP):
                    dve.tensor_scalar(xn[:, p, :], x[:, p, :], gn.scale[:, p:p + 1], gn.shift[:, p:p + 1],
                                      ALU.mult, ALU.add).then_inc(xn_ready, 1)
                step = Steps(dve, own)
                for g in range(NQ):
                    for s in range(2):
                        dve.wait_ge(hi_ready, 2 * g + s + 1)
                        step(dve.tensor_tensor(rest[:, s], full[:, s], parts[:, g, s, 0], ALU.subtract))
                        step(dve.tensor_copy(parts[:, g, s, 1], rest[:, s]))
                        dve.tensor_tensor(parts[:, g, s, 2], rest[:, s], parts[:, g, s, 1], ALU.subtract).then_inc(parts_ready, 1)
                for h in range(2):
                    dve.wait_ge(v_ps_ready, h + 1)
                    dve.tensor_tensor(v_all[:, 4 * h:4 * h + 4].rearrange("p n t e c -> p (n t) (e c)"),
                                      ring[:, 2 * h:2 * h + 2].rearrange("p a (t c) -> p (a t) c", c=P),
                                      b_v[:, :].unsqueeze(1).broadcast_to([P, 8, P]), ALU.add).then_inc(v_all_ready, 1)
                dve.sem_inc(max_read, 2)
                dve.sem_inc(o_added, 1)

                def largest(n, b, k):
                    if k == 0:
                        dve.wait_ge(mx_turned, n + 1)
                    dve.wait_ge(max_ps, 8 * n + k + 1)
                    head = 4 * (k % 2) + k // 2
                    dve.tensor_reduce(mx[:, b, :, head], ring[:, k % 2].rearrange("p (q s) -> p q s", q=2), AX.X, ALU.max).then_inc(max_read, 1)

                def split_max(n, b):
                    dve.wait_ge(mx_turned, n + 3)
                    dve.wait_ge(m_stacked, 64 * n + 64)
                    dve.tensor_scalar(m_parts[:, b, 0], m_ps[0:8, 0:N], -1.0, None, ALU.mult).then_inc(m_ready, 1)
                    dve.wait_ge(m_ready, 2 * n + 1)
                    dve.scalar_tensor_tensor(out=m_parts[:, b, 1], in0=m_ps[0:8, 0:N], scalar=-1.0, in1=m_parts[:, b, 0],
                                             op0=ALU.mult, op1=ALU.subtract).then_inc(m_ready, 1)

                def normalize(n):
                    dve.wait_ge(ctx_turned, n + 3)
                    cols = a_ps[:, :].rearrange("p (g q j k) -> p (g q) j k", g=2, q=2, j=4)
                    dve.reciprocal(ctx_r[:].rearrange("p (a j) -> p a j", j=4), cols[:, :, :, HD2]).then_inc(norm_own, 1)
                    dve.wait_ge(norm_own, n + 1)
                    for q in range(2):
                        ins_ = dve.tensor_tensor(ctx_n[:, q].rearrange("p g (j d) -> p g j d", d=HD2), cols[:, q::2, :, 0:HD2],
                                                 ctx_r[:].rearrange("p (g q j) -> p g q j", g=2, q=2)[:, :, q, :].unsqueeze(3).broadcast_to([P, 2, 4, HD2]),
                                                 ALU.mult).then_inc(ctx_normed, 1)

                def take_back(n):
                    dve.wait_ge(ctx_back, n + 1)
                    dve.tensor_copy(ctx_c[:], a_ps[:, 0:P]).then_inc(ctx_copied, 1)

                def add(n, i, b):
                    half = slice(C * b, C * b + C)
                    dve.wait_ge(o_ready, n + 1)
                    dve.scalar_tensor_tensor(out=x[half, ds(i, 1), :], in0=a_ps[half, N:2 * N], scalar=vec[half, 2:3], in1=x[half, ds(i, 1), :],
                                             op0=ALU.add, op1=ALU.add).then_inc(o_added, 1)

                def turn(i, b, A, S, D):
                    n = 2 * i + b
                    for k in range(8):
                        if A:
                            largest(n, b, k)
                        if k == 1 and S:
                            split_max(n - 1, 1 - b)
                        if k == 3 and D:
                            normalize(n - 3)
                        if k == 5 and D:
                            take_back(n - 3)
                        if k == 7 and D:
                            add(n - 3, i - 2 + b, 1 - b)

                turns(dve, turn)

            @block.scalar
            def _(act):
                gn.scalar(act)
                act.wait_ge(loaded, 16 * len(LOADS))
                for g in range(NQ):
                    for s, src, ready in ((0, ring[:, g], q_ps_ready), (1, k_bank(g), k_ps_ready)):
                        act.wait_ge(ready, g + 1)
                        if g:
                            act.wait_ge(parts_ready, 2 * g)
                        act.activation(full[:, s], src, ACT.Identity, bias=vec[:, s:s + 1]).then_inc(full_ready, 1)
                        act.wait_ge(full_ready, 2 * g + s + 1)
                        act.activation(parts[:, g, s, 0], src, ACT.Identity, bias=vec[:, s:s + 1]).then_inc(hi_ready, 1)
                act.sem_inc(e_ready, 2)
                act.sem_inc(ctx_ready, 2)

                def turn(i, b, A, S, D):
                    n = 2 * i + b
                    c = n - 2
                    for k in range(8):
                        if A:
                            act.wait_ge(s_ready, 8 * c + k + 1)
                            if k in (0, 4):
                                act.wait_ge(ev_done, 2 * c + 3 + k // 4)
                            act.activation(e[:, k], ring[:, 2 + k % 2], ACT.Exp, scale=HD2 ** -0.5).then_inc(e_ready, 1)
                        if k == 1 and D:
                            act.wait_ge(ev_done, 2 * (c - 1) + 6)
                            act.wait_ge(ctx_turned, c)
                            act.activation(ctx[:, 1 - b], ctx_ps[:, 1 - b], ACT.Copy).then_inc(ctx_ready, 1)

                turns(act, turn, lag=2)

            @block.tensor
            def _(pe):
                gn.tensor(pe)
                pe.wait_ge(loaded, 16 * len(LOADS))
                for g in range(NQ):
                    pe.wait_ge(xn_ready, 2 * g + 2)
                    if g == 0:
                        pe.wait_ge(xn_ready, NP)
                    pe.matmul(ring[:, g], w_q[:], xn[:, 2 * g:2 * g + 2, :], start=True, stop=True).then_inc(q_ps_ready, 1)
                    pe.matmul(k_bank(g), w_k[:], xn[:, 2 * g:2 * g + 2, :], start=True, stop=True).then_inc(k_ps_ready, 1)
                for h in range(2):
                    pe.wait_ge(hi_ready, 4 * h + 4)
                    for p in range(4 * h, 4 * h + 4):
                        for t in range(2):
                            mm = pe.matmul(ring[:, p // 2, (2 * (p % 2) + t) * P:(2 * (p % 2) + t + 1) * P], xn[:, p, t * P:(t + 1) * P], w_v[:],
                                           start=True, stop=True)
                    mm.then_inc(v_ps_ready, 1)
                pe.sem_inc(mx_turned, 2)
                pe.sem_inc(ev_done, 4)
                pe.sem_inc(ctx_turned, 2)
                pe.wait_ge(v_all_ready, 2)
                pe.wait_ge(hi_ready, 2 * NQ)
                pe.wait_ge(stacked[0], 18 * 16)

                def largest(n, k, at):
                    h, p = k % 2, k // 2
                    pe.wait_ge(max_read, 8 * n + k + 1)
                    for q in range(2):
                        mm = pe.matmul(ring[:, k % 2, q * N:(q + 1) * N], q_st[:, h, p, ds(at, 1), q * P:(q + 1) * P], k_st[:, p, ds(at, 1), :],
                                       start=True, stop=True)
                    mm.then_inc(max_ps, 1)

                def scores(c, k, at):
                    p, t = k // 2, k % 2
                    if k == 0:
                        pe.wait_ge(m_stacked, 64 * c + 192)
                    pe.wait_ge(e_ready, 8 * c + k + 1)
                    pe.matmul(ring[:, 2 + k % 2], k_st[:, p, ds(at, 1), t * P:(t + 1) * P], q_st[:, :, p, ds(at, 1), :],
                              start=True, stop=True).then_inc(s_ready, 1)

                def context(c, b, g):
                    pe.wait_ge(e_ready, 8 * c + 4 * g + 6)
                    pe.wait_ge(v_x_ready, c + 1)
                    pe.wait_ge(ctx_ready, c + 1)
                    for t in range(2):
                        for j in range(4):
                            mm = pe.matmul(ctx_ps[32 * j:32 * j + 32, b, g * N:(g + 1) * N], v_x[:, b, t, 4 * g + j, :],
                                           e[:, 4 * g + 2 * (j // 2) + t, (j % 2) * N:(j % 2 + 1) * N], start=(t == 0), stop=(t == 1))
                    mm.then_inc(ev_done, 1)

                def turn(i, b, A, S, D):
                    n = 2 * i + b
                    C_ = not isinstance(i, int) or 2 <= n < B + 2
                    for k in range(8):
                        if A:
                            largest(n, k, NP * b + i)
                        if C_:
                            scores(n - 2, k, NP * b + i - 1)
                        if k == 0 and S:
                            if not isinstance(i, int) or n > 1:
                                pe.wait_ge(m_ready, 2 * n - 2)
                            pe.wait_ge(max_read, 8 * n + 2)
                            for q in range(2):
                                mm = pe.transpose(m_ps[0:8, q * P:(q + 1) * P], mx[:, 1 - b, q, :], ident[:])
                            mm.then_inc(mx_turned, 1)
                        if k == 1 and D:
                            context(n - 3, 1 - b, 1)
                        if k == 2 and D:
                            pe.wait_ge(ctx_ready, n)
                            pe.wait_ge(o_added, n - 2)
                            for g in range(2):
                                for q in range(2):
                                    mm = pe.transpose(a_ps[:, (2 * g + q) * P:(2 * g + q + 1) * P], ctx[:, 1 - b, g, q * P:(q + 1) * P], ident[:])
                            mm.then_inc(ctx_turned, 1)
                        if k == 4 and D:
                            pe.wait_ge(ctx_normed, 2 * (n - 3) + 2)
                            pe.transpose(a_ps[:, 0:P], ctx_n[:].rearrange("p q g c -> p (q g c)"), ident[:]).then_inc(ctx_back, 1)
                        if k == 5 and C_:
                            context(n - 2, b, 0)
                        if k == 6 and D:
                            pe.wait_ge(ctx_copied, n - 2)
                            half = slice(C * (1 - b), C * (1 - b) + C)
                            for q in range(2):
                                mm = pe.matmul(a_ps[half, N + q * P:N + (q + 1) * P], w_o[:, q, :], ctx_c[:], start=True, stop=True)
                            mm.then_inc(o_ready, 1)
                    if isinstance(n, int) and n == 3:
                        for g in range(1, NQ):
                            pe.wait_ge(stacked[g], 18 * 16)

                turns(pe, turn)


def turns(eng, turn, lag=0):
    for n in range(4):
        enter = n < B if lag == 0 else n >= lag
        turn(n // 2, n % 2, enter, n >= 1, n >= 3)
    with eng.Fori(2, NP) as i:
        for b in range(2):
            turn(i, b, True, True, True)
    for n in range(B, B + 3):
        enter = False if lag == 0 else n < B + lag
        turn(n // 2, n % 2, enter, n == B, True)


def layer3(nc, ins, signals, x, avg2):
    KK = 9
    TN = KK * N
    TW = 2 * KK * C // 3
    with Memory(nc, "L3") as m:
        w_off, w_all = m.sb("w_off", [P, 6, 32]), m.sb("w_all", [P, 2 * KK * C])
        sel_f, sel = m.sb("sel_f", [P, 3, P]), m.sb("sel", [P, 3, P], BF16)
        grid, vec = m.sb("grid", [P, 2, TN]), m.sb("vec", [P, 3])
        xpad, stack = m.sb("xpad", [P, NP, HP * WP]), m.sb("stack", [P, B, HP * WP])
        off, sig = m.sb("off", [P, NQ, N]), m.sb("sig", [P, NQ, N])
        rep, rest, parts = m.sb("rep", [P, 3, TN]), m.sb("rest", [P, TN]), m.sb("parts", [P, 2, 3, TN], BF16)
        hats = m.sb("hats", [P, 2, 2, TN], BF16)
        xn, t_sb = m.sb("xn", [P, 2, N]), m.sb("t_sb", [P, 2, 2, 2 * KK * C])
        cols, s = m.sb("cols", [P, 2, 2 * N]), m.sb("s", [P, 2, 2, 2 * N])
        row_ps, col_ps, acc = m.ps("row_ps", [P, 2, 2, 2 * N]), m.ps("col_ps", [P, 2, 2 * N]), m.ps("acc", [P, 2, 2 * N])
        off_ps = row_ps[:, 0].rearrange("p a (g n) -> p (a g) n", n=N)
        gn = GroupNorm(m, signals, "gn", avg2, acc[:, 0, 0:NP], acc[:, 1, 0:NP])
        off_dram = nc.dram_tensor("L3_offsets", (B, 3 * KK, N), F32, kind="Internal").ap()
        hat_dram = nc.dram_tensor("L3_hat_parts", (2, B, H, 3, TN), BF16, kind="Internal").ap()

        (loaded, edge_ready, xpad_ready, sel_ready, off_conv, off_ready, off_stored, grid_added, dist_ready, hat_own, hat_ready, hi_ready,
         own, parts_ready, hats_stored) = m.sems(
            "loaded edge_ready xpad_ready sel_ready off_conv off_ready off_stored grid_added dist_ready hat_own hat_ready hi_ready "
            "own parts_ready hats_stored")
        stack_in = m.sems("stack_in0 stack_in1 stack_in2 stack_in3")
        rep_in = m.sems("rep_in0 rep_in1")
        (hats_in, xn_ready, row_ready, col_ready, col_read, s_ready, s_used, added, passed) = m.sems(
            "hats_in xn_ready row_ready col_ready col_read s_ready s_used added passed")
        LOADS = [(w_off[:], "w_off"), (w_all[:], "w_all"), (sel_f[:], "sel"), (grid[:].rearrange("p k n -> p (k n)"), ins["grid"].broadcast_to([P, 2 * TN])), (vec[:], "l3_vec")]

        with nc.Block() as block:
            @block.sync
            def _(sp):
                for dst, src in LOADS:
                    sp.dma_start(dst, ins[src] if isinstance(src, str) else src).then_inc(loaded, 16)
                sp.wait_ge(edge_ready, 2)
                send_stack(sp, xpad_ready, stack_in, xpad, stack)
                sp.wait_ge(off_ready, 2)
                for j in range(4):
                    dst = off_dram.rearrange("(g j) r n -> j r g n", j=4)[j]
                    sp.dma_start(dst[0:2 * KK], off[32 * j:32 * j + 2 * KK]).then_inc(off_stored, 16)
                    sp.dma_start(dst[2 * KK:], sig[32 * j + 2 * KK:32 * j + 3 * KK]).then_inc(off_stored, 16)
                sp.wait_ge(off_stored, 128)
                for w in range(2):
                    if w:
                        sp.wait_ge(parts_ready, 2)
                    src = off_dram[8 * w:8 * w + 8].rearrange("u r n -> u (r n)").unsqueeze(1).broadcast_to([8, H, 3 * TN])
                    sp.dma_start(rep[:].rearrange("p k n -> p (k n)"), src).then_inc(rep_in[w], 16)
                    for k in range(2):
                        sp.wait_ge(parts_ready, 2 * w + k + 1)
                        sp.dma_start(hat_dram[k, 8 * w:8 * w + 8].rearrange("u y t n -> (u y) (t n)"),
                                     parts[:, k].rearrange("p t n -> p (t n)")).then_inc(hats_stored, 16)
                sp.wait_ge(hats_stored, 64)
                sp.wait_ge(edge_ready, 3)

                def load_hats(n, b):
                    for k in range(2):
                        src = hat_dram[k, ds(2 * n, 2)].rearrange("e y t n -> (y t) e n")
                        sp.dma_start(hats[64 * k:64 * k + 3 * H, b], src).then_inc(hats_in, 16)
                    sp.wait_ge(hats_in, 32 * n + 32)
                    sp.sem_inc(passed, 1)

                load_hats(0, 0)
                load_hats(1, 1)
                with sp.Fori(1, NP // 2) as i:
                    for b in range(2):
                        sp.wait_ge(s_used, KK * (2 * i + b) - 7)
                        sp.sem_inc(passed, 1)
                        load_hats(2 * i + b, b)

            @block.gpsimd
            def _(pool):
                pad_stack(nc, pool, edge_ready, xpad, stack)
                pool.wait_ge(edge_ready, 2)
                pool.memset(hats[32:64], 0.0).then_inc(edge_ready, 1)
                pool.wait_ge(edge_ready, 3)
                for w in range(2):
                    pool.wait_ge(rep_in[w], 16)
                    for k in range(2):
                        pool.tensor_tensor(rep[:, k], rep[:, k], grid[:, k], ALU.add).then_inc(grid_added, 1)

            @block.vector
            def _(dve):
                gn.vector(dve, lambda p: x[:, p, :])
                dve.wait_ge(edge_ready, 2)
                for p in range(NP):
                    dst = xpad[:, p, :].rearrange("p (r c) -> p r c", c=WP)[:, 1:1 + H, 1:1 + W]
                    dve.tensor_scalar(dst, x[:, p, :].rearrange("p (r c) -> p r c", c=W), gn.scale[:, p:p + 1], gn.shift[:, p:p + 1],
                                      ALU.mult, ALU.add).then_inc(xpad_ready, 1)
                dve.wait_ge(loaded, 16 * len(LOADS))
                dve.tensor_copy(sel[:], sel_f[:]).then_inc(sel_ready, 1)
                step = Steps(dve, own)
                for w in range(2):
                    for k in range(2):
                        hat = rep[:, k]
                        dve.wait_ge(hat_ready, 2 * w + k + 1)
                        if k == 0:
                            step(dve.tensor_tensor(hat, hat, rep[:, 2], ALU.mult))
                        if w:
                            dve.wait_ge(hats_stored, 32)
                        step(dve.tensor_copy(parts[:, k, 0], hat))
                        step(dve.tensor_tensor(rest[:], hat, parts[:, k, 0], ALU.subtract))
                        step(dve.tensor_copy(parts[:, k, 1], rest[:]))
                        step(dve.tensor_tensor(parts[:, k, 2], rest[:], parts[:, k, 1], ALU.subtract))
                        dve.sem_inc(parts_ready, 1)
                dve.sem_inc(s_ready, 2)
                dve.sem_inc(added, 2)

                def norm(n, b):
                    dve.tensor_scalar(xn[:, b, :], x[:, ds(n, 1), :], gn.scale[:, ds(n, 1)], gn.shift[:, ds(n, 1)], ALU.mult, ALU.add).then_inc(xn_ready, 1)

                norm(0, 0)
                norm(1, 1)

                def sample(n, b, t, c):
                    u, q = KK * n + t, (b + t) % 2
                    dve.wait_ge(row_ready, u + 1)
                    dve.wait_ge(col_read, c + 1)
                    dve.wait_ge(s_used, u + 1)
                    dve.tensor_tensor(s[:, q], row_ps[:, q], cols[:, q:q + 1].broadcast_to([P, 2, 2 * N]), ALU.mult).then_inc(s_ready, 1)

                def pair(n, b, more):
                    for t in range(1, KK):
                        sample(n, b, t, 7 + 15 * n + col_step(t - 1, more))
                        if t == 4 and more > 1:
                            dve.wait_ge(col_ready, 15 * n + 6)
                            norm(n + 2, b)
                    if more:
                        sample(n + 1, 1 - b, 0, 7 + 15 * n + col_step(KK - 1, more))
                    dve.wait_ge(s_used, KK * n + KK + 2)
                    dve.scalar_tensor_tensor(out=x[:, ds(n, 1), :], in0=acc[:, b, 0:N], scalar=vec[:, 2:3], in1=x[:, ds(n, 1), :],
                                             op0=ALU.add, op1=ALU.add).then_inc(added, 1)

                sample(0, 0, 0, 6)
                pairs(dve, pair)

            @block.scalar
            def _(act):
                gn.scalar(act)
                act.wait_ge(loaded, 16 * len(LOADS))
                act.wait_ge(off_conv, 1)
                act.activation(off[:], off_ps, ACT.Identity, bias=vec[:, 0:1]).then_inc(off_ready, 1)
                act.activation(sig[:], off_ps, ACT.Sigmoid, bias=vec[:, 0:1]).then_inc(off_ready, 1)
                for w in range(2):
                    for k in range(2):
                        act.wait_ge(grid_added, 2 * w + k + 1)
                        act.activation(rep[:, k], rep[:, k], ACT.Abs, bias=vec[:, 1:2]).then_inc(dist_ready, 1)
                        act.wait_ge(dist_ready, 2 * w + k + 1)
                        act.activation(rep[:, k], rep[:, k], ACT.Relu, bias=1.0, scale=-1.0).then_inc(hat_ready, 1)

                def take_cols(v, c, q, r):
                    act.wait_ge(col_ready, c + 1)
                    act.wait_ge(s_ready, v + 1)
                    act.activation(cols[:, q], col_ps[:, r], ACT.Copy).then_inc(col_read, 1)

                def take_t(b, c, k, r):
                    act.wait_ge(col_ready, c + 1)
                    act.activation(t_sb[:, b, k // 3, ds(k % 3 * TW, TW)], col_ps[:, r, 0:TW], ACT.Copy).then_inc(col_read, 1)

                for k in range(6):
                    take_t(0, k, k, k % 2)
                take_cols(0, 6, 0, 0)

                def pair(n, b, more):
                    for t in range(KK):
                        loc = col_step(t, more)
                        c, r = 7 + 15 * n + loc, (1 + b + loc) % 2
                        if t < KK - 1 or more:
                            take_cols(KK * n + t + 1, c, (b + t + 1) % 2, r)
                        if t < 6 and more:
                            if t == 0:
                                act.wait_ge(s_used, KK * n + 2)
                            take_t(1 - b, c + 1, t, 1 - r)

                pairs(act, pair)

            @block.tensor
            def _(pe):
                gn.tensor(pe)
                pe.wait_ge(loaded, 16 * len(LOADS))
                for g in range(NQ):
                    pe.wait_ge(stack_in[g], 64)
                    for k in range(6):
                        for j in range(4):
                            mm = pe.matmul(off_ps[32 * j:32 * j + 32, g, :], w_off[:, k, :], tap(stack, 4 * g + j, k), start=(k == 0), stop=(k == 5))
                mm.then_inc(off_conv, 1)
                pe.sem_inc(s_used, 2)
                pe.wait_ge(off_ready, 2)
                pe.wait_ge(sel_ready, 1)

                def weigh(b, c, k, r):
                    if not isinstance(c, int) or c > 1:
                        pe.wait_ge(col_read, c - 1)
                    pe.matmul(col_ps[:, r, 0:TW], xn[:, b, k // 3 * P:(k // 3 + 1) * P], w_all[:, k % 3 * TW:(k % 3 + 1) * TW],
                              start=True, stop=True).then_inc(col_ready, 1)

                def spread(v, b, t, c, r):
                    q = (b + t) % 2
                    hat = hats[0:112, b, :, t * N:(t + 1) * N]
                    pe.wait_ge(s_ready, v + 1)
                    for h in range(2):
                        mm = pe.matmul(row_ps[:, q, h], sel[0:112, h], hat, start=True, stop=True)
                    mm.then_inc(row_ready, 1)
                    pe.wait_ge(col_read, c - 1)
                    pe.matmul(col_ps[:, r], sel[0:112, 2], hat, start=True, stop=True).then_inc(col_ready, 1)

                def samples(n, b, t):
                    u, q = KK * n + t, (b + t) % 2
                    pe.wait_ge(s_ready, u + 3)
                    if t == 0:
                        pe.wait_ge(added, n + 1)
                        pe.wait_ge(col_read, 15 * n + 6)
                    for h in range(2):
                        for e in range(2):
                            mm = pe.matmul(acc[C * e:C * e + C, b, 0:N], t_sb[:, b, h, (KK * e + t) * C:(KK * e + t + 1) * C],
                                           s[:, q, h, e * N:(e + 1) * N], start=(t == 0 and h == 0), stop=(t == KK - 1 and h == 1))
                    mm.then_inc(s_used, 1)

                pe.wait_ge(xn_ready, 1)
                for k in range(6):
                    weigh(0, k, k, k % 2)
                pe.wait_ge(hats_in, 32)
                spread(0, 0, 0, 6, 0)

                def pair(n, b, more):
                    for t in range(KK):
                        loc = col_step(t, more)
                        c, r = 7 + 15 * n + loc, (1 + b + loc) % 2
                        if t < KK - 1:
                            spread(KK * n + t + 1, b, t + 1, c, r)
                        elif more:
                            pe.wait_ge(hats_in, 32 * n + 64)
                            spread(KK * n + KK, 1 - b, 0, c, r)
                        if t < 6 and more:
                            if t == 0:
                                pe.wait_ge(xn_ready, n + 2)
                            weigh(1 - b, c + 1, t, 1 - r)
                        samples(n, b, t)

                pairs(pe, pair)


def col_step(t, more):
    return t + min(t, 6) if more else t


def pairs(eng, pair):
    with eng.Fori(0, NP // 2 - 1) as i:
        for b in range(2):
            pair(2 * i + b, b, 2)
    pair(NP - 2, 0, 1)
    pair(NP - 1, 1, 0)


def program(nc, ins, out, layers=4):
    Memory.semaphores = ExitStack()
    with Memory.semaphores, Memory(nc, "all") as m:
        x, avg2 = m.sb("x", [P, NP, N]), m.sb("avg2", [P, P])
        x_in, x_out = m.sems("x_in x_out")
        signals = NormSignals(m)
        with nc.Block() as block:
            @block.sync
            def _(sp):
                sp.dma_start(x[:], ins["x"].rearrange("(n e) c h w -> (e c) n (h w)", e=2)).then_inc(x_in, 16)
                sp.dma_start(avg2[:], ins["avg2"]).then_inc(x_in, 16)
        layer0(nc, ins, signals, x, x_in, avg2)
        if layers > 1:
            layer1(nc, ins, signals, x, avg2)
        if layers > 2:
            layer2(nc, ins, signals, x, avg2)
        if layers > 3:
            layer3(nc, ins, signals, x, avg2)
        with nc.Block() as block:
            @block.sync
            def _(sp):
                sp.dma_start(out.rearrange("(n e) c h w -> (e c) n (h w)", e=2), x[:]).then_inc(x_out, 16)
                sp.wait_ge(x_out, 16)


def two_blocks(a):
    r, c = a.shape
    out = np.zeros((2 * r, 2 * c), a.dtype)
    out[:r, :c], out[r:, c:] = a, a
    return out


def lay_out(a):
    f = np.float32
    part = np.arange(P)
    t = {"x": a["x"]}
    t["avg2"] = (part[:, None] // 2 == part[None, :] // 2).astype(f) / f(2)
    t["avg8"] = (part[:, None] // 8 == part[None, :] // 8).astype(f) / f(8)
    t["w_pre"], t["w_post"] = two_blocks(a["L0_conv_pre_w"].T), two_blocks(a["L0_conv_post_w"].T)
    names = ["pre_b", "pre_gn_g", "pre_gn_b", "post_b", "post_gn_g", "post_gn_b"]
    t["l0_vec"] = np.stack([np.tile(a["L0_conv_" + n], 2) for n in names], 1)
    t["w_s1"] = two_blocks(a["L0_conv_sp_w1"])
    t["b_s1"] = np.tile(a["L0_conv_sp_b1"], 2)[:, None]
    t["w_s2"] = np.tile(two_blocks(a["L0_conv_sp_w2"]), (1, G0))
    t["b_s2"] = np.tile(a["L0_conv_sp_b2"], 2 * G0)[:, None]
    group_k, parity_k = part // 32, part // 16 % 2
    group_c, parity_c = part % C // 16, part // C
    t["same_group"] = ((group_k[:, None] == group_c) & (parity_k[:, None] == parity_c)).astype(f)
    kinds = ["alpha", "mu", "sigma", "mix", "gate"]
    w = np.concatenate([a[f"L0_conv_{k}_w"].reshape(S0, G0, -1) for k in kinds], 2)
    b = np.concatenate([a[f"L0_conv_{k}_b"].reshape(G0, -1) for k in kinds], 1)
    t["w_par"] = np.repeat(w.transpose(1, 0, 2)[:, None], 2, 1).reshape(P, NPAR)
    w = a["L1_conv_W_in"].T
    none = np.zeros((C, DI), f)
    t["w_z"] = np.concatenate([w[:, :DI], none])
    t["w_in"] = np.tile(w[:, DI:2 * DI + 2 * DS1], (2, 1))
    t["w_dt"] = np.concatenate([np.pad(w[:, 2 * DI + 2 * DS1:], ((0, 0), (0, 32 - NH1))), none[:, :32]])
    t["w_out"], t["w_out2"] = a["L1_conv_W_out"].T, np.tile(a["L1_conv_W_out"].T, (1, 2))
    t["ident"] = np.eye(P, dtype=f)
    t["center"] = np.eye(P, dtype=f) - f(1 / DI)
    t["ones"] = np.full((P, C), 1 / DI, f)
    t["quarter"] = (part[:, None] // 32 == np.arange(4)).astype(f)
    heads = lambda v: np.tile(np.pad(v, (0, 32 - NH1)), 4)
    cb = a["L1_conv_conv_b"]
    t["l1_vec"] = np.stack([cb[:DI], np.tile(cb[DI:], 4), np.repeat(a["L1_conv_D"], HD1), a["L1_conv_ln_g"], a["L1_conv_ln_b"],
                            heads(a["L1_conv_dt_bias"]), heads(a["L1_conv_A_log"])], 1)
    t["conv_w"] = a["L1_conv_conv_w"][:, 0].transpose(1, 2, 0)
    order = np.arange(C).reshape(4, 2, HD2).transpose(1, 2, 0).reshape(C)
    t["w_q"], t["w_k"], t["w_v"] = two_blocks(a["L2_conv_Wq"][order].T), two_blocks(a["L2_conv_Wk"][order].T), two_blocks(a["L2_conv_Wv"].T)
    t["w_o"] = two_blocks(a["L2_conv_Wo"].T).reshape(P, 2, C)
    t["b_v"] = np.tile(a["L2_conv_bv"], (P, 2))
    t["l2_vec"] = np.stack([np.tile(v, 2) for v in (a["L2_conv_bq"][order], a["L2_conv_bk"][order], a["L2_conv_bo"])], 1)
    w = np.concatenate([a["L3_conv_off_w"][0::2], a["L3_conv_off_w"][1::2], a["L3_conv_mask_w"]])
    w_off = np.zeros((2, C, 2, W3, 32), f)
    w_off[0, :, :, :, :27] = w[:, :, 0::2].transpose(1, 2, 3, 0)
    w_off[1, :, 0, :, :27] = w[:, :, 1].transpose(1, 2, 0)
    t["w_off"] = w_off.reshape(P, 6, 32)
    t["w_all"] = two_blocks(a["L3_conv_weight"].transpose(1, 2, 3, 0).reshape(C, -1))
    bias = np.concatenate([a["L3_conv_off_b"][0::2], a["L3_conv_off_b"][1::2], a["L3_conv_mask_b"]])
    t["l3_vec"] = np.stack([np.tile(np.pad(bias, (0, 32 - 27)), 4), -(part % H).astype(f), np.tile(a["L3_conv_bias"], 2)], 1)
    k, r = np.divmod(part, 3)
    col = part[None, :]
    rows = [(part[:, None] < 48) & (k[:, None] == 8 * h + col // W) for h in range(2)]
    k = (part - 64) // 3
    t["sel"] = np.stack(rows + [(part[:, None] >= 64) & (part[:, None] < 112) & (k[:, None] == col % W)], 1).astype(f)
    tap_y, tap_x = np.divmod(np.arange(9), 3)
    pos_y, pos_x = np.divmod(np.arange(N), W)
    t["grid"] = np.stack([pos_y - 1 + tap_y[:, None], pos_x - 1 + tap_x[:, None]]).reshape(1, -1).astype(f)
    t["b_par"] = np.tile(np.repeat(b, 16, 0), (2, 1))
    return t


def kernel(**inputs):
    import concourse.bacc as bacc
    from concourse.bass_utils import run_bass_kernel_spmd

    nc = bacc.Bacc("TRN2", target_bir_lowering=False, num_devices=1)
    arrays, ins = {}, {}
    for name, a in lay_out({k: np.asarray(v) for k, v in inputs.items()}).items():
        a = np.ascontiguousarray(a)
        arrays[f"in_{name}"] = a
        ins[name] = nc.dram_tensor(f"in_{name}", a.shape, mybir.dt.from_np(a.dtype), kind="ExternalInput").ap()
    out = nc.dram_tensor("out_x", (B, C, H, W), F32, kind="ExternalOutput").ap()
    program(nc, ins, out)
    r = run_bass_kernel_spmd(nc, [arrays], core_ids=[0])
    return r.results[0]["out_x"]
```

```python
from contextlib import ExitStack

import numpy as np

import concourse.bass as bass
from concourse import mybir

F32 = mybir.dt.float32
BF16 = mybir.dt.bfloat16
ALU = mybir.AluOpType
ACT = mybir.ActivationFunctionType
AX = mybir.AxisListType

B, C, H, W = 16, 64, 16, 16
N = H * W
P = 128
NP = B // 2
EPS = 1e-5

G0, NB, S0 = 4, 6, 16
NPAR = 4 * NB + 1

DI, NH1, HD1, DS1 = 128, 8, 16, 16
HP, WP = H + 2, W + 2
W3 = 3
NH2, HD2 = 8, 8
NQ = B // 4


def ds(start, size):
    return bass.ds(start, size)


class Memory:

    semaphores = None

    def __init__(self, nc, name):
        self.nc, self.name, self.ctx = nc, name, ExitStack()

    def __enter__(self):
        self.ctx.__enter__()
        return self

    def __exit__(self, *a):
        return self.ctx.__exit__(*a)

    def sb(self, name, shape, dt=F32):
        return self.ctx.enter_context(self.nc.sbuf_tensor(f"{self.name}_{name}", shape, dt))

    def ps(self, name, shape, dt=F32):
        return self.ctx.enter_context(self.nc.psum_tensor(f"{self.name}_{name}", shape, dt))

    def sem(self, name):
        return Memory.semaphores.enter_context(self.nc.semaphore(f"{self.name}_{name}"))

    def sems(self, names):
        return [self.sem(n) for n in names.split()]


class Steps:

    def __init__(self, eng, sem, n=0):
        self.eng, self.sem, self.n = eng, sem, n

    def __call__(self, ins):
        ins.then_inc(self.sem, 1)
        self.n += 1
        self.eng.wait_ge(self.sem, self.n)

    def free(self, ins):
        ins.then_inc(self.sem, 1)
        self.n += 1

    def settle(self):
        self.eng.wait_ge(self.sem, self.n)


class NormSignals:

    def __init__(self, mem):
        self.own, self.stats_ready, self.mean_ready, self.sp_ready, self.spread_ready, self.var_ready, self.sd_ready = (
            mem.sems("norm_own norm_stats norm_mean norm_sp norm_spread norm_var norm_sd"))
        self.norms = self.own_steps = 0


class GroupNorm:

    def __init__(self, mem, signals, name, avg, mean, spread):
        self.signals = signals
        signals.norms += 1
        self.turn = signals.norms
        self.avg, self.mean, self.spread = avg, mean, spread
        self.bn, self.mv = mem.sb(name + "_bn", [P, NP, 6]), mem.sb(name + "_mv", [P, NP, 2])
        self.d, self.sp, self.var, self.sd, self.scale, self.shift = (
            mem.sb(f"{name}_{n}", [P, NP]) for n in ("d", "sp", "var", "sd", "scale", "shift"))

    def vector(self, dve, source, bias=None, gamma=None, beta=None):
        on, turn = self.signals, self.turn
        step = Steps(dve, on.own, on.own_steps)
        for p in range(NP):
            step.free(dve.bn_stats(self.bn[:, p, :], source(p)))
        step.settle()
        for p in range(NP):
            step.free(dve.bn_aggr(self.mv[:, p, :], self.bn[:, p, :]))
        step.settle()
        if bias is not None:
            step(dve.tensor_scalar(self.mv[:, :, 0], self.mv[:, :, 0], bias, None, ALU.add))
        dve.sem_inc(on.stats_ready, 1)
        dve.wait_ge(on.mean_ready, turn)
        step(dve.tensor_tensor(self.d[:], self.mv[:, :, 0], self.mean, ALU.subtract))
        step(dve.tensor_tensor(self.sp[:], self.d[:], self.d[:], ALU.mult))
        dve.tensor_tensor(self.var[:], self.sp[:], self.mv[:, :, 1], ALU.add).then_inc(on.sp_ready, 1)
        dve.wait_ge(on.spread_ready, turn)
        dve.tensor_scalar(self.sp[:], self.spread, EPS, None, ALU.add).then_inc(on.var_ready, 1)
        dve.wait_ge(on.sd_ready, turn)
        step(dve.reciprocal(self.scale[:], self.sd[:]))
        if gamma is not None:
            step(dve.tensor_scalar(self.scale[:], self.scale[:], gamma, None, ALU.mult))
        if bias is None:
            step(dve.tensor_scalar(self.d[:], self.mean, -1.0, None, ALU.mult))
        else:
            step(dve.tensor_scalar(self.d[:], self.mean, bias, -1.0, ALU.subtract, ALU.mult))
        step(dve.tensor_tensor(self.shift[:], self.d[:], self.scale[:], ALU.mult))
        if beta is not None:
            step(dve.tensor_scalar(self.shift[:], self.shift[:], beta, None, ALU.add))
        on.own_steps = step.n

    def tensor(self, pe):
        on, turn = self.signals, self.turn
        pe.wait_ge(on.stats_ready, turn)
        pe.matmul(self.mean, self.avg[:], self.mv[:, :, 0], start=True, stop=True).then_inc(on.mean_ready, 1)
        pe.wait_ge(on.sp_ready, turn)
        pe.matmul(self.spread, self.avg[:], self.var[:], start=True, stop=True).then_inc(on.spread_ready, 1)

    def scalar(self, act):
        on, turn = self.signals, self.turn
        act.wait_ge(on.var_ready, turn)
        act.activation(self.sd[:], self.sp[:], ACT.Sqrt).then_inc(on.sd_ready, 1)


def layer0(nc, ins, signals, x, x_in, avg2):
    with Memory(nc, "L0") as m:
        w_pre, w_post, avg8, same_group, w_s2 = (m.sb(n, [P, P]) for n in ("w_pre", "w_post", "avg8", "same_group", "w_s2"))
        w_s1, w_par, b_par = m.sb("w_s1", [P, 32]), m.sb("w_par", [P, NPAR]), m.sb("b_par", [P, NPAR])
        b_s1, b_s2, vec = m.sb("b_s1", [P, 1]), m.sb("b_s2", [P, 1]), m.sb("vec", [P, 6])
        xn, z = m.sb("xn", [P, NP, N]), m.sb("z", [P, NP, N])
        pooled, h1, h2, h2_sel = m.sb("pooled", [P, NP]), m.sb("h1", [32, NP]), m.sb("h2", [P, NP]), m.sb("h2_sel", [P, NP, P])
        par = m.sb("par", [P, NP, NPAR])
        ealpha, esigma, lnsigma, sigma, inv, minus_mu, mix, c0, c1, zc0, zc1, alpha = (
            m.sb(n, [P, NP, NB]) for n in ("ealpha", "esigma", "lnsigma", "sigma", "inv", "minus_mu", "mix", "c0", "c1", "zc0", "zc1", "alpha"))
        amax, asum, gate = m.sb("amax", [P, NP]), m.sb("asum", [P, NP]), m.sb("gate", [P, NP])
        uu, ex, poly, t = (m.sb(n, [P, 2, NB, N]) for n in ("uu", "ex", "poly", "t"))
        y1, y2 = m.ps("y1", [P, NP, N]), m.ps("y2", [P, NP, N])
        gn_x = GroupNorm(m, signals, "gn_x", avg2, y2[:, 0, 0:NP], y2[:, 2, 0:NP])
        gn_1 = GroupNorm(m, signals, "gn_1", avg8, y2[:, 0, 0:NP], y2[:, 2, 0:NP])
        gn_2 = GroupNorm(m, signals, "gn_2", avg8, y1[:, 0, 0:NP], y1[:, 2, 0:NP])
        s1, s2 = y2[0:32, 4, 0:NP], y2[:, 6, 0:NP]
        par_ps = y2[:, 4, 0:NP * NPAR].rearrange("p (n k) -> p n k", n=NP)

        (loaded, own, xn_ready, y1_ready, norm1_ready, z_ready, s1_ready, h1_ready, s2_ready, h2_ready, sel_ready,
         par_ready, exp_in, exp_out, coef_ready) = m.sems(
            "loaded own xn_ready y1_ready norm1_ready z_ready s1_ready h1_ready s2_ready h2_ready sel_ready "
            "par_ready exp_in exp_out coef_ready")
        (uu_ready, e_ready, poly_ready, t_ready, t_used, norm2_ready, out_ready, added) = m.sems(
            "uu_ready e_ready poly_ready t_ready t_used norm2_ready out_ready added")
        LOADS = [(w_pre[:], "w_pre"), (avg8[:], "avg8"), (vec[:], "l0_vec"), (w_s1[:], "w_s1"), (b_s1[0:32, :], "b_s1"),
                 (w_s2[0:32, :], "w_s2"), (b_s2[:], "b_s2"), (same_group[:], "same_group"), (w_par[:], "w_par"),
                 (b_par[:], "b_par"), (w_post[:], "w_post")]

        with nc.Block() as block:
            @block.sync
            def _(sp):
                for dst, src in LOADS:
                    sp.dma_start(dst, ins[src]).then_inc(loaded, 16)

            @block.vector
            def _(dve):
                def x_pair(p):
                    if p == 0:
                        dve.wait_ge(x_in, 32)
                    return x[:, p, :]

                gn_x.vector(dve, x_pair)
                for p in range(NP):
                    dve.tensor_scalar(xn[:, p, :], x[:, p, :], gn_x.scale[:, p:p + 1], gn_x.shift[:, p:p + 1],
                                      ALU.mult, ALU.add).then_inc(xn_ready, 1)

                def y1_pair(p):
                    if p % 2 == 0:
                        dve.wait_ge(y1_ready, p // 2 + 1)
                    return y1[:, p, :]

                dve.wait_ge(loaded, 16 * len(LOADS))
                gn_1.vector(dve, y1_pair, vec[:, 0:1], vec[:, 1:2], vec[:, 2:3])
                dve.sem_inc(norm1_ready, 1)

                step = Steps(dve, own)
                dve.wait_ge(h2_ready, 1)
                for p in range(NP):
                    dve.tensor_scalar(h2_sel[:, p, :], same_group[:], h2[:, p:p + 1], None, ALU.mult).then_inc(sel_ready, 1)
                dve.wait_ge(par_ready, 1)
                step(dve.tensor_tensor(par[:], par_ps, b_par[:, :].unsqueeze(1).broadcast_to([P, NP, NPAR]), ALU.add))
                al, mu, sg, mx = (par[:, :, NB * k:NB * (k + 1)] for k in range(4))
                per_basis = lambda v: v[:, :].unsqueeze(2).broadcast_to([P, NP, NB])
                step(dve.tensor_reduce(amax[:], al, AX.X, ALU.max))
                step(dve.tensor_tensor(alpha[:], al, per_basis(amax), ALU.subtract))
                step(dve.tensor_scalar(sigma[:], sg, -1.0, None, ALU.mult))
                step(dve.tensor_tensor(sigma[:], sigma[:], sg, ALU.min))
                dve.sem_inc(exp_in, 1)
                dve.wait_ge(exp_out, 5)
                step(dve.tensor_reduce(asum[:], ealpha[:], AX.X, ALU.add))
                step(dve.tensor_scalar(gate[:], gate[:], 1.0, None, ALU.add))
                step(dve.tensor_tensor(asum[:], asum[:], gate[:], ALU.mult))
                step(dve.reciprocal(asum[:], asum[:]))
                step(dve.tensor_tensor(alpha[:], ealpha[:], per_basis(asum), ALU.mult))
                step(dve.tensor_scalar(mix[:], mix[:], 1.0, None, ALU.add))
                step(dve.reciprocal(mix[:], mix[:]))
                step(dve.scalar_tensor_tensor(out=sigma[:], in0=sg, scalar=0.0, in1=lnsigma[:], op0=ALU.max, op1=ALU.add))
                step(dve.tensor_scalar(sigma[:], sigma[:], 0.001, None, ALU.add))
                step(dve.reciprocal(inv[:], sigma[:]))
                step(dve.scalar_tensor_tensor(out=minus_mu[:], in0=mu, scalar=-1.0, in1=inv[:], op0=ALU.mult, op1=ALU.mult))
                dve.sem_inc(coef_ready, 1)
                step(dve.tensor_tensor(c0[:], alpha[:], mix[:], ALU.mult))
                step(dve.tensor_tensor(c1[:], alpha[:], c0[:], ALU.subtract))
                step(dve.tensor_tensor(zc1[:], c1[:], inv[:], ALU.mult))
                step(dve.tensor_tensor(zc0[:], c1[:], minus_mu[:], ALU.mult))
                step(dve.tensor_tensor(zc0[:], zc0[:], c0[:], ALU.add))
                dve.sem_inc(t_ready, 2)

                with dve.Fori(0, NP // 2) as i:
                    for q in range(2):
                        k = 2 * i + q
                        dve.wait_ge(t_ready, k + 1)
                        for j in range(NB):
                            dve.tensor_scalar(poly[:, q, j, :], z[:, ds(k, 1), :], zc1[:, ds(k, 1), j], zc0[:, ds(k, 1), j],
                                              ALU.mult, ALU.add).then_inc(poly_ready, 1)
                        dve.wait_ge(poly_ready, NB * k + NB)
                        dve.wait_ge(e_ready, k + 1)
                        dve.wait_ge(t_used, k + 1)
                        dve.tensor_tensor(t[:, q], poly[:, q], ex[:, q], ALU.mult).then_inc(t_ready, 1)

                def y2_pair(p):
                    dve.wait_ge(t_used, (p | 1) + 3)
                    return y2[:, p, :]

                gn_2.vector(dve, y2_pair, vec[:, 3:4], vec[:, 4:5], vec[:, 5:6])
                dve.sem_inc(norm2_ready, 1)
                for p in range(NP):
                    dve.wait_ge(out_ready, p + 1)
                    dve.tensor_tensor(x[:, p, :], x[:, p, :], xn[:, p, :], ALU.add).then_inc(added, 1)
                dve.wait_ge(added, NP)

            @block.tensor
            def _(pe):
                pe.wait_ge(loaded, 16 * len(LOADS))
                gn_x.tensor(pe)
                for h in range(NP // 2):
                    pe.wait_ge(xn_ready, 2 * h + 2)
                    pe.matmul(y1[:, 2 * h:2 * h + 2, :], w_pre[:], xn[:, 2 * h:2 * h + 2, :], start=True, stop=True).then_inc(y1_ready, 1)
                gn_1.tensor(pe)
                pe.wait_ge(z_ready, NP)
                pe.matmul(s1, w_s1[:], pooled[:], start=True, stop=True).then_inc(s1_ready, 1)
                pe.wait_ge(h1_ready, 1)
                pe.matmul(s2, w_s2[0:32, :], h1[:], start=True, stop=True).then_inc(s2_ready, 1)
                for p in range(NP):
                    pe.wait_ge(sel_ready, p + 1)
                    mm = pe.matmul(par_ps[:, p, :], h2_sel[:, p, :], w_par[:], start=True, stop=True)
                mm.then_inc(par_ready, 1)
                pe.sem_inc(t_used, 2)
                pe.wait_ge(coef_ready, 1)
                with pe.Fori(0, NP // 2) as i:
                    for q in range(2):
                        k = 2 * i + q
                        pe.matmul(y2[:, ds(k, 1), :], w_post[:], z[:, ds(k, 1), :], start=True, stop=False)
                        pe.wait_ge(t_ready, k + 3)
                        for j in range(NB):
                            mm = pe.matmul(y2[:, ds(k, 1), :], w_post[:], t[:, q, j:j + 1, :], start=False, stop=(j == NB - 1))
                        mm.then_inc(t_used, 1)
                gn_2.tensor(pe)

            @block.scalar
            def _(act):
                gn_x.scalar(act)
                gn_1.scalar(act)
                act.wait_ge(norm1_ready, 1)
                for p in range(NP):
                    act.activation(z[:, p, :], y1[:, p, :], ACT.Silu, scale=gn_1.scale[:, p:p + 1], bias=gn_1.shift[:, p:p + 1],
                                   accum_out=pooled[:, p:p + 1]).then_inc(z_ready, 1)
                act.wait_ge(s1_ready, 1)
                act.activation(h1[:], s1, ACT.Gelu_apprx_tanh, scale=1.0 / N, bias=b_s1[0:32, :]).then_inc(h1_ready, 1)
                act.wait_ge(s2_ready, 1)
                act.activation(h2[:], s2, ACT.Gelu_apprx_tanh, bias=b_s2[:]).then_inc(h2_ready, 1)
                act.wait_ge(exp_in, 1)
                act.activation(ealpha[:], alpha[:], ACT.Exp).then_inc(exp_out, 1)
                act.activation(esigma[:], sigma[:], ACT.Exp).then_inc(exp_out, 1)
                act.activation(mix[:], par[:, :, 3 * NB:4 * NB], ACT.Exp, scale=-1.0).then_inc(exp_out, 1)
                act.activation(gate[:], par[:, :, NPAR - 1], ACT.Exp, scale=-1.0).then_inc(exp_out, 1)
                act.wait_ge(exp_out, 4)
                act.activation(lnsigma[:], esigma[:], ACT.Ln, bias=1.0).then_inc(exp_out, 1)
                act.wait_ge(coef_ready, 1)
                with act.Fori(0, NP // 2) as i:
                    for q in range(2):
                        k = 2 * i + q
                        act.wait_ge(t_ready, k + 1)
                        for j in range(NB):
                            act.activation(uu[:, q, j, :], z[:, ds(k, 1), :], ACT.Square, scale=inv[:, ds(k, 1), j],
                                           bias=minus_mu[:, ds(k, 1), j]).then_inc(uu_ready, 1)
                        act.wait_ge(uu_ready, NB * k + NB)
                        act.activation(ex[:, q], uu[:, q], ACT.Exp, scale=-1.0).then_inc(e_ready, 1)
                gn_2.scalar(act)
                act.wait_ge(norm2_ready, 1)
                for p in range(NP):
                    act.activation(xn[:, p, :], y2[:, p, :], ACT.Silu, scale=gn_2.scale[:, p:p + 1],
                                   bias=gn_2.shift[:, p:p + 1]).then_inc(out_ready, 1)


def pad_stack(nc, pool, edge_ready, xpad, stack):
    pool.memset(xpad[:], 0.0).then_inc(edge_ready, 1)
    pool.wait_ge(edge_ready, 1)
    pool.memset(stack[C:P, :, H * WP + WP:HP * WP], 0.0).then_inc(edge_ready, 1)


def send_stack(sp, xpad_ready, stack_in, xpad, stack):
    for g in range(NQ):
        sp.wait_ge(xpad_ready, 2 * g + 2)
        src = xpad[:, 2 * g:2 * g + 2, :]
        dst = stack[:, 4 * g:4 * g + 4, :].rearrange("p (n e) s -> p n e s", e=2)
        for e in range(2):
            sp.dma_start(dst[0:C, :, e, :], src[C * e:C * e + C]).then_inc(stack_in[g], 16)
            sp.dma_start(dst[C:P, :, e, 0:(HP - 1) * WP], src[C * e:C * e + C, :, WP:HP * WP]).then_inc(stack_in[g], 16)


def image(stack, b, n=1):
    return stack[:, ds(b, n), :].rearrange("p n (r c) -> p n r c", c=WP)


def tap(stack, b, g, n=1):
    r, c = (0, g) if g < 3 else (2, g - 3)
    return image(stack, b, n)[:, :, r:r + H, c:c + W]


def layer1(nc, ins, signals, x, avg2):
    with Memory(nc, "L1") as m:
        w_in, cw = m.sb("w_in", [P, DI + 32]), m.sb("cw", [P, 6, DI + 32])
        w_tap = m.sb("w_tap", [P, 6, DI + 32])
        w_z, w_dt, w_out, w_out2, w_cen = m.sb("w_z", [P, DI]), m.sb("w_dt", [P, 32]), m.sb("w_out", [P, C]), m.sb("w_out2", [P, P]), m.sb("w_cen", [P, C])
        w_g = m.sb("w_g", [P, C])
        ident, center, ones = m.sb("ident", [P, P]), m.sb("center", [P, P]), m.sb("ones", [P, C])
        quarter, vec = m.sb("quarter", [P, 4]), m.sb("vec", [P, 7])
        a_exp, b_out = m.sb("a_exp", [P, 1]), m.sb("b_out", [P, 1])
        xpad, stack = m.sb("xpad", [P, NP, HP * WP]), m.sb("stack", [P, B, HP * WP])
        dt, dt_e, da = m.sb("dt", [P, NQ, N]), m.sb("dt_e", [P, NQ, N]), m.sb("da", [P, NQ, N])
        xs, zs, bc = m.sb("xs", [P, 4, N]), m.sb("zs", [P, 4, N]), m.sb("bc", [P, NQ, N])
        b_t, bt_all, da_t, v = m.sb("b_t", [P, 2, 4, 32]), m.sb("bt_all", [P, NQ, 2, 4, DS1]), m.sb("da_t", [P, NQ, 2, 4, NH1]), m.sb("v", [P, 2, 4, DI])
        kv, y, sq = m.sb("kv", [P, 4, DI]), m.sb("y", [P, 4, N]), m.sb("sq", [P, 4, N])
        o_all, var_all = m.sb("o_all", [P, NP, N]), m.sb("var_all", [P, NP, N])
        xs_ps, z_ps, bc_ps = m.ps("xs_ps", [P, 4, N]), m.ps("z_ps", [P, 4, N]), m.ps("bc_ps", [P, NP])
        t_ps, k_ps = m.ps("t_ps", [P, 2, 4, DI]), m.ps("k_ps", [P, 2, N])
        gn = GroupNorm(m, signals, "gn", avg2, k_ps[:, 0, 0:NP], bc_ps[:])
        flat = lambda ap: ap.rearrange("p a n -> p (a n)")
        t_y = t_ps[:, :, :, :].rearrange("p h j d -> p (h j d)").rearrange("p (j n) -> p j n", n=N)

        (loaded, weights_in, own, edge_ready, xpad_ready, tap_ready, g_ready, cen_ps, cen_ready, dt_ps, dt_v, dt_exp, dt_ln, act_own, da_tps, bc_conv, bc_ready) = m.sems(
            "loaded weights_in own edge_ready xpad_ready tap_ready g_ready cen_ps cen_ready dt_ps dt_v dt_exp dt_ln act_own da_tps bc_conv bc_ready")
        stack_in = m.sems("stack_in0 stack_in1 stack_in2 stack_in3")
        (conv_ready, acts_ready, bt_ready, xt_ready, bt_copied, v_ready, kv_ps, kv_ready, y_ps, y_own, y_ready, cen_y, sq_ready, o_ready,
         var_ready, o_copied) = m.sems(
            "conv_ready acts_ready bt_ready xt_ready bt_copied v_ready kv_ps kv_ready y_ps y_own y_ready cen_y sq_ready o_ready var_ready o_copied")
        added, sd_ready, sd_in = m.sems("added sd_ready sd_in")
        LOADS = [(w_in[:], "w_in"), (w_z[:], "w_z"), (w_dt[:], "w_dt"), (w_out[:], "w_out"), (w_out2[:], "w_out2"),
                 (ident[:], "ident"), (center[:], "center"), (ones[:], "ones"), (quarter[:], "quarter"), (vec[:], "l1_vec")]
        LOADS += [(cw[C * e:C * e + C, 3 * k:3 * k + 3, :], ins["conv_w"][2 * k + e:2 * k + e + 1].broadcast_to([C, 3, DI + 32]))
                  for k, e in ((0, 0), (0, 1), (1, 0))]

        with nc.Block() as block:
            @block.sync
            def _(sp):
                for dst, src in LOADS:
                    sp.dma_start(dst, ins[src] if isinstance(src, str) else src).then_inc(loaded, 16)
                sp.wait_ge(edge_ready, 3)
                send_stack(sp, xpad_ready, stack_in, xpad, stack)

            @block.gpsimd
            def _(pool):
                pad_stack(nc, pool, edge_ready, xpad, stack)
                pool.wait_ge(edge_ready, 2)
                pool.memset(cw[C:P, 3:6, :], 0.0).then_inc(edge_ready, 1)
                pool.wait_ge(edge_ready, 3)
                pool.memset(b_t[:], 0.0).then_inc(edge_ready, 1)

            @block.vector
            def _(dve):
                gn.vector(dve, lambda p: x[:, p, :])
                dve.wait_ge(edge_ready, 4)
                for p in range(NP):
                    dst = xpad[:, p, :].rearrange("p (r c) -> p r c", c=WP)[:, 1:1 + H, 1:1 + W]
                    dve.tensor_scalar(dst, x[:, p, :].rearrange("p (r c) -> p r c", c=W), gn.scale[:, p:p + 1], gn.shift[:, p:p + 1],
                                      ALU.mult, ALU.add).then_inc(xpad_ready, 1)
                dve.wait_ge(loaded, 16 * len(LOADS))
                dve.tensor_tensor(w_tap[:], cw[:], w_in[:, :].unsqueeze(1).broadcast_to([P, 6, DI + 32]), ALU.mult).then_inc(tap_ready, 1)
                dve.tensor_scalar(w_g[:], w_out[:], vec[:, 3:4], None, ALU.mult).then_inc(g_ready, 1)
                dve.wait_ge(cen_ps, 2)
                dve.tensor_copy(w_cen[:], k_ps[:, 0, 0:C]).then_inc(cen_ready, 1)
                dve.tensor_copy(b_out[:], k_ps[:, 0, C:C + 1]).then_inc(cen_ready, 1)
                step = Steps(dve, own)
                dve.wait_ge(dt_ps, 16)
                step(dve.tensor_scalar(dt[:], t_y, vec[:, 5:6], None, ALU.add))
                step(dve.scalar_tensor_tensor(out=dt_e[:], in0=dt[:], scalar=-1.0, in1=dt[:], op0=ALU.mult, op1=ALU.min))
                dve.sem_inc(dt_v, 1)
                dve.wait_ge(dt_ln, 1)
                step(dve.scalar_tensor_tensor(out=da[:], in0=dt[:], scalar=0.0, in1=da[:], op0=ALU.max, op1=ALU.add))
                step(dve.tensor_scalar(da[:], da[:], a_exp[:], None, ALU.mult))
                dve.sem_inc(dt_v, 1)
                dve.wait_ge(da_tps, 1)
                step(dve.tensor_copy(da_t[:].rearrange("p q h j k -> p (q h j) k"), t_ps[:].rearrange("p a j (e k) -> p (a j e) k", k=32)[:, :, 0:NH1]))
                dve.wait_ge(bt_ready, 1)
                step(dve.tensor_copy(bt_all[:].rearrange("p q h j k -> p (q h j) k"),
                                     z_ps[:].rearrange("p q (h j k) -> p (q h j) k", h=2, k=32)[:, :, 0:DS1]))
                dve.sem_inc(y_ready, 2)
                dve.sem_inc(o_copied, 2)
                with dve.Fori(0, NQ) as q:
                    dve.tensor_copy(b_t[:, :, :, DS1:2 * DS1].rearrange("p h j k -> p (h j) k"),
                                    bt_all[:, ds(q, 1)].rearrange("p q h j k -> p (q h j) k")).then_inc(bt_copied, 1)
                    dve.wait_ge(xt_ready, q + 1)
                    for h in range(2):
                        dve.tensor_tensor(v[:, h].rearrange("p j (h d) -> p (j h) d", d=HD1),
                                          t_ps[:, h].rearrange("p j (h d) -> p (j h) d", d=HD1),
                                          da_t[:, ds(q, 1), h].rearrange("p q j h -> p (q j h)").unsqueeze(2).broadcast_to([P, 4 * NH1, HD1]),
                                          ALU.mult).then_inc(v_ready, 1)
                    dve.wait_ge(kv_ps, q + 1)
                    dve.tensor_tensor(kv[:], k_ps[:, 0, 0:DI].unsqueeze(1).broadcast_to([P, 4, DI]),
                                      quarter[:, :].unsqueeze(2).broadcast_to([P, 4, DI]), ALU.mult).then_inc(kv_ready, 1)
                    dve.wait_ge(y_ps, q + 1)
                    for h in range(2):
                        dve.scalar_tensor_tensor(out=y[:, 2 * h:2 * h + 2, :], in0=xs[:, 2 * h:2 * h + 2, :], scalar=vec[:, 2:3],
                                                 in1=t_y[:, 2 * h:2 * h + 2, :], op0=ALU.mult, op1=ALU.add).then_inc(y_own, 1)
                    dve.wait_ge(acts_ready, 2 * q + 2)
                    for h in range(2):
                        dve.wait_ge(y_own, 2 * q + 1 + h)
                        dve.tensor_tensor(y[:, 2 * h:2 * h + 2, :], y[:, 2 * h:2 * h + 2, :], zs[:, 2 * h:2 * h + 2, :],
                                          ALU.mult).then_inc(y_ready, 1)
                    dve.wait_ge(o_ready, q + 1)
                    dve.tensor_copy(o_all[:, ds(2 * q, 2), :], k_ps[:]).then_inc(o_copied, 1)
                    dve.wait_ge(var_ready, q + 1)
                    dve.tensor_copy(var_all[:, ds(2 * q, 2), :], t_y[:, 0:2, :]).then_inc(o_copied, 1)
                dve.wait_ge(o_copied, 2 * NQ + 2)
                for h in range(2):
                    r = slice(4 * h, 4 * h + 4)
                    step(dve.tensor_scalar(var_all[:, r, :], var_all[:, r, :], EPS, None, ALU.add))
                    dve.sem_inc(sd_in, 1)
                for h in range(2):
                    r = slice(4 * h, 4 * h + 4)
                    dve.wait_ge(sd_ready, h + 1)
                    step(dve.reciprocal(var_all[:, r, :], var_all[:, r, :]))
                    step(dve.tensor_tensor(o_all[:, r, :], o_all[:, r, :], var_all[:, r, :], ALU.mult))
                    step(dve.scalar_tensor_tensor(out=x[:, r, :], in0=o_all[:, r, :], scalar=b_out[:], in1=x[:, r, :], op0=ALU.add, op1=ALU.add))

            @block.scalar
            def _(act):
                gn.scalar(act)
                act.wait_ge(loaded, 16 * len(LOADS))
                act.activation(a_exp[:], vec[:, 6:7], ACT.Exp).then_inc(act_own, 1)
                act.wait_ge(dt_v, 1)
                act.activation(dt_e[:], dt_e[:], ACT.Exp).then_inc(dt_exp, 1)
                act.wait_ge(dt_exp, 1)
                act.wait_ge(act_own, 1)
                act.activation(da[:], dt_e[:], ACT.Ln, bias=1.0).then_inc(dt_ln, 1)
                act.wait_ge(bc_conv, 1)
                act.activation(bc[:], z_ps[:], ACT.Silu, bias=vec[:, 1:2]).then_inc(bc_ready, 1)
                with act.Fori(0, NQ) as q:
                    act.wait_ge(conv_ready, 2 * q + 2)
                    act.wait_ge(y_ready, 2 * q + 2)
                    act.activation(xs[:], xs_ps[:], ACT.Silu, bias=vec[:, 0:1]).then_inc(acts_ready, 1)
                    act.activation(zs[:], z_ps[:], ACT.Silu).then_inc(acts_ready, 1)
                    act.wait_ge(cen_y, q + 1)
                    act.activation(sq[:], t_y, ACT.Square).then_inc(sq_ready, 1)
                for h in range(2):
                    r = slice(4 * h, 4 * h + 4)
                    act.wait_ge(sd_in, h + 1)
                    act.activation(var_all[:, r, :], var_all[:, r, :], ACT.Sqrt).then_inc(sd_ready, 1)

            @block.tensor
            def _(pe):
                gn.tensor(pe)
                pe.wait_ge(loaded, 16 * len(LOADS))
                pe.wait_ge(g_ready, 1)
                pe.matmul(k_ps[:, 0, 0:C], center[:], w_g[:], start=True, stop=True).then_inc(cen_ps, 1)
                pe.matmul(k_ps[:, 0, C:C + 1], w_out2[:], vec[:, 4:5], start=True, stop=True).then_inc(cen_ps, 1)
                for g in range(NQ):
                    pe.wait_ge(stack_in[g], 64)
                    for j in range(4):
                        pe.matmul(t_y[32 * j:32 * j + 32, g, :], w_dt[:], image(stack, 4 * g + j)[:, 0, 1:1 + H, 1:1 + W],
                                  start=True, stop=True).then_inc(dt_ps, 1)
                pe.wait_ge(tap_ready, 1)

                def conv_xs(q, h):
                    for g in range(6):
                        mm = pe.matmul(xs_ps[:, 2 * h:2 * h + 2, :], w_tap[:, g, 0:DI], tap(stack, 4 * q + 2 * h, g, 2),
                                       start=(g == 0), stop=(g == 5))
                    if h == 1:
                        mm.then_inc(conv_ready, 1)

                def conv_bc(q):
                    for g in range(6):
                        for j in range(4):
                            mm = pe.matmul(z_ps[32 * j:32 * j + 32, q, :], w_tap[:, g, DI:DI + 32], tap(stack, 4 * q + j, g),
                                           start=(g == 0), stop=(g == 5))
                    return mm

                def proj_z(q):
                    for h in range(2):
                        mm = pe.matmul(z_ps[:, 2 * h:2 * h + 2, :], w_z[:], image(stack, 4 * q + 2 * h, 2)[:, :, 1:1 + H, 1:1 + W],
                                       start=True, stop=True)
                    mm.then_inc(conv_ready, 1)

                def quad(q, more):
                    pe.wait_ge(o_copied, 2 * q + 2)
                    pe.wait_ge(acts_ready, 2 * q + 1)
                    for h in range(2):
                        for j in range(4):
                            mm = pe.transpose(t_ps[:, h, j, :], xs[:, j, h * P:(h + 1) * P], ident[:])
                    mm.then_inc(xt_ready, 1)
                    if more:
                        conv_xs(q + 1, 0)
                    pe.wait_ge(bt_copied, q + 1)
                    pe.wait_ge(v_ready, 2 * q + 2)
                    for h in range(2):
                        for j in range(4):
                            mm = pe.matmul(k_ps[32 * j:32 * j + 32, 0, 0:DI], b_t[:, h, j, :], v[:, h, j, :], start=(h == 0), stop=(h == 1))
                    mm.then_inc(kv_ps, 1)
                    if more:
                        conv_xs(q + 1, 1)
                    pe.wait_ge(kv_ready, q + 1)
                    for j in range(4):
                        mm = pe.matmul(t_y[:, j, :], kv[:, j, :], bc[:, ds(q, 1), :], start=True, stop=True)
                    mm.then_inc(y_ps, 1)
                    if more:
                        pe.wait_ge(acts_ready, 2 * q + 2)
                        proj_z(q + 1)
                    pe.wait_ge(y_ready, 2 * q + 4)
                    for h in range(2):
                        mm = pe.matmul(t_y[:, 2 * h:2 * h + 2, :], center[:], y[:, 2 * h:2 * h + 2, :], start=True, stop=True)
                    mm.then_inc(cen_y, 1)
                    for j in range(4):
                        mm = pe.matmul(k_ps[C * (j % 2):C * (j % 2) + C, j // 2, :], w_cen[:], y[:, j, :], start=True, stop=True)
                    mm.then_inc(o_ready, 1)
                    pe.wait_ge(sq_ready, q + 1)
                    for j in range(4):
                        mm = pe.matmul(t_y[C * (j % 2):C * (j % 2) + C, j // 2, :], ones[:], sq[:, j, :], start=True, stop=True)
                    mm.then_inc(var_ready, 1)

                for g in range(NQ):
                    mm = conv_bc(g)
                mm.then_inc(bc_conv, 1)
                for h in range(2):
                    conv_xs(0, h)
                pe.wait_ge(dt_v, 2)
                for g in range(NQ):
                    for h in range(2):
                        mm = pe.transpose(t_ps[:, g // 2, 2 * (g % 2) + h, :], da[:, g, h * P:(h + 1) * P], ident[:])
                mm.then_inc(da_tps, 1)
                pe.wait_ge(bc_ready, 1)
                for g in range(NQ):
                    for h in range(2):
                        mm = pe.transpose(z_ps[:, g, h * P:(h + 1) * P], bc[:, g, h * P:(h + 1) * P], ident[:])
                mm.then_inc(bt_ready, 1)
                pe.wait_ge(y_ready, 2)
                proj_z(0)
                with pe.Fori(0, NQ - 1) as q:
                    quad(q, True)
                quad(NQ - 1, False)


def layer2(nc, ins, signals, x, avg2):
    TOP = 48
    with Memory(nc, "L2") as m:
        w_q, w_k, w_v, ident = (m.sb(n, [P, P]) for n in ("w_q", "w_k", "w_v", "ident"))
        w_o, b_v, vec = m.sb("w_o", [P, 2, C]), m.sb("b_v", [P, P]), m.sb("vec", [P, 3])
        xn = m.sb("xn", [P, NP, N])
        full, rest = m.sb("full", [P, 2, 2 * N]), m.sb("rest", [P, 2, 2 * N])
        parts = m.sb("parts", [P, 4, 2, 3, 2 * N], BF16)
        k_st, q_st = m.sb("k_st", [P, NQ, 4, 2, 2, N], BF16), m.sb("q_st", [P, 2, NQ, 4, 2, 2, N], BF16)
        v_all, v_x = m.sb("v_all", [P, NP, 2, 2, C]), m.sb("v_x", [P, 2, 2, NH2, 32])
        e = m.sb("e", [P, 8, 2 * N])
        mx, m_parts = m.sb("mx", [P, 2, 2, 8]), m.sb("m_parts", [8, 2, 2, N], BF16)
        ctx, ctx_r, ctx_n, ctx_c = m.sb("ctx", [P, 2, 2, N]), m.sb("ctx_r", [P, 16]), m.sb("ctx_n", [P, 2, 2, 4 * HD2]), m.sb("ctx_c", [P, P])
        ring, ctx_ps, a_ps, m_ps = m.ps("ring", [P, 4, 2 * N]), m.ps("ctx_ps", [P, 2, 2 * N]), m.ps("a_ps", [P, 2 * N]), m.ps("m_ps", [P, 2 * N])
        k_bank = lambda g: [ctx_ps[:, 0], ctx_ps[:, 1], a_ps[:], m_ps[:]][g]
        gn = GroupNorm(m, signals, "gn", avg2, a_ps[:, 0:NP], m_ps[:, 0:NP])
        scratch = [nc.dram_tensor(f"L2_{n}_parts", (NQ, 3, 2, HD2, 4, 2, 2 * N), BF16, kind="Internal").ap() for n in "qk"]

        (loaded, own, filled, xn_ready, q_ps_ready, k_ps_ready, full_ready, hi_ready, parts_ready, v_ps_ready, v_all_ready,
         pool_own) = m.sems("loaded own filled xn_ready q_ps_ready k_ps_ready full_ready hi_ready parts_ready v_ps_ready v_all_ready pool_own")
        stored = m.sems("stored0 stored1 stored2 stored3")
        stacked = m.sem("stacked")
        (max_ps, max_read, mx_turned, m_ready, m_stacked, s_ready, e_ready, ev_done, ctx_ready, ctx_turned, ctx_normed, ctx_back,
         ctx_copied, o_ready, o_added, v_x_ready, norm_own, passed) = m.sems(
            "max_ps max_read mx_turned m_ready m_stacked s_ready e_ready ev_done ctx_ready ctx_turned ctx_normed ctx_back "
            "ctx_copied o_ready o_added v_x_ready norm_own passed")
        LOADS = [(t[:], n) for t, n in ((w_q, "w_q"), (w_k, "w_k"), (w_v, "w_v"), (ident, "ident"), (w_o, "w_o"), (b_v, "b_v"), (vec, "l2_vec"))]

        with nc.Block() as block:
            @block.sync
            def _(sp):
                for dst, src in LOADS:
                    sp.dma_start(dst, ins[src]).then_inc(loaded, 16)
                sp.sem_inc(m_stacked, 128)

                def store_parts(g):
                    for s in range(2):
                        sp.wait_ge(parts_ready, 2 * g + s + 1)
                        for b in range(2):
                            dst = scratch[s][g].rearrange("t e d p b n -> b (e d p) t n")[b]
                            sp.dma_start(dst, parts[C * b:C * b + C, g, s]).then_inc(stored[g], 16)

                def load_stacks(g, h):
                    for slot, part, count in ((0, 0, 3), (3, 1, 2), (5, 2, 1)):
                        rows = slice(64 * h + HD2 * slot, 64 * h + HD2 * (slot + count))
                        src = scratch[0][g, part, h].rearrange("d p b n -> d (p b n)").unsqueeze(0).broadcast_to([count, HD2, 4 * 4 * N])
                        sp.dma_start(q_st[rows, h, g].rearrange("r p b n s -> r (p b n s)"), src).then_inc(stacked, 16)
                        src = scratch[1][g, 0:count, h].rearrange("t d p b n -> t d (p b n)")
                        sp.dma_start(k_st[rows, g].rearrange("r p b n s -> r (p b n s)"), src).then_inc(stacked, 16)

                def send_maxima(i, j):
                    n, b = 4 * i + j, j % 2
                    sp.wait_ge(m_ready, 2 * n + 2)
                    sp.sem_inc(passed, 1)
                    for h in range(2):
                        for t in range(2):
                            dst = q_st[64 * h + TOP + t:64 * h + TOP + t + 1, h, ds(i, 1), :, b, j // 2, :].rearrange("t i p s -> t (i p) s")
                            sp.dma_start(dst, m_parts[4 * h:4 * h + 4, b, t, :]).then_inc(m_stacked, 16)
                    sp.wait_ge(m_stacked, 64 * n + 192)
                    sp.sem_inc(passed, 1)

                store_parts(0)
                store_parts(1)
                for g in range(NQ):
                    sp.wait_ge(stored[g], 64)
                    sp.wait_ge(filled, 2 * g + 2)
                    if g:
                        sp.wait_ge(stacked, 12 * 16 * g)
                    for h in range(2):
                        load_stacks(g, h)
                        if h == 0 and g + 2 < NQ:
                            store_parts(g + 2)
                        if 2 <= 2 * g + h < 6:
                            send_maxima(0, 2 * g + h - 2)
                with sp.Fori(1, NQ) as i:
                    for j in range(4):
                        send_maxima(i, j)

            @block.gpsimd
            def _(pool):
                for g in range(NQ):
                    pool.memset(q_st[:, :, g], 0.0).then_inc(filled, 1)
                    pool.memset(k_st[:, g], 1.0).then_inc(filled, 1)
                pool.wait_ge(filled, 2 * NQ)
                pool.memset(v_x[:], 0.0).then_inc(pool_own, 1)
                pool.wait_ge(pool_own, 1)
                pool.memset(v_x[:, :, :, :, HD2:HD2 + 1], 1.0).then_inc(pool_own, 1)
                pool.wait_ge(pool_own, 2)
                pool.wait_ge(v_all_ready, 2)
                with pool.Fori(0, NP) as i:
                    for b in range(2):
                        n = 2 * i + b
                        pool.wait_ge(ev_done, 2 * n + 2)
                        pool.tensor_copy(v_x[:, b, :, :, 0:HD2],
                                         v_all[:, ds(i, 1), :, b, :].rearrange("p i t (h d) -> p (i t) h d", d=HD2)).then_inc(v_x_ready, 1)

            @block.vector
            def _(dve):
                gn.vector(dve, lambda p: x[:, p, :])
                for p in range(NP):
                    dve.tensor_scalar(xn[:, p, :], x[:, p, :], gn.scale[:, p:p + 1], gn.shift[:, p:p + 1],
                                      ALU.mult, ALU.add).then_inc(xn_ready, 1)
                step = Steps(dve, own)
                for g in range(NQ):
                    for s in range(2):
                        dve.wait_ge(hi_ready, 2 * g + s + 1)
                        step(dve.tensor_tensor(rest[:, s], full[:, s], parts[:, g, s, 0], ALU.subtract))
                        step(dve.tensor_copy(parts[:, g, s, 1], rest[:, s]))
                        dve.tensor_tensor(parts[:, g, s, 2], rest[:, s], parts[:, g, s, 1], ALU.subtract).then_inc(parts_ready, 1)
                for h in range(2):
                    dve.wait_ge(v_ps_ready, h + 1)
                    dve.tensor_tensor(v_all[:, 4 * h:4 * h + 4].rearrange("p n t e c -> p (n t) (e c)"),
                                      ring[:, 2 * h:2 * h + 2].rearrange("p a (t c) -> p (a t) c", c=P),
                                      b_v[:, :].unsqueeze(1).broadcast_to([P, 8, P]), ALU.add).then_inc(v_all_ready, 1)
                dve.sem_inc(max_read, 2)
                dve.sem_inc(o_added, 1)

                def largest(n, b, k):
                    if k == 0:
                        dve.wait_ge(mx_turned, n + 1)
                    dve.wait_ge(max_ps, 8 * n + k + 1)
                    head = 4 * (k % 2) + k // 2
                    dve.tensor_reduce(mx[:, b, :, head], ring[:, k % 2].rearrange("p (q s) -> p q s", q=2), AX.X, ALU.max).then_inc(max_read, 1)

                def split_max(n, b):
                    dve.wait_ge(mx_turned, n + 3)
                    dve.wait_ge(m_stacked, 64 * n + 64)
                    dve.tensor_scalar(m_parts[:, b, 0], m_ps[0:8, 0:N], -1.0, None, ALU.mult).then_inc(m_ready, 1)
                    dve.wait_ge(m_ready, 2 * n + 1)
                    dve.scalar_tensor_tensor(out=m_parts[:, b, 1], in0=m_ps[0:8, 0:N], scalar=-1.0, in1=m_parts[:, b, 0],
                                             op0=ALU.mult, op1=ALU.subtract).then_inc(m_ready, 1)

                def normalize(n):
                    dve.wait_ge(ctx_turned, n + 3)
                    cols = a_ps[:, :].rearrange("p (g q j k) -> p (g q) j k", g=2, q=2, j=4)
                    dve.reciprocal(ctx_r[:].rearrange("p (a j) -> p a j", j=4), cols[:, :, :, HD2]).then_inc(norm_own, 1)
                    dve.wait_ge(norm_own, n + 1)
                    for q in range(2):
                        ins_ = dve.tensor_tensor(ctx_n[:, q].rearrange("p g (j d) -> p g j d", d=HD2), cols[:, q::2, :, 0:HD2],
                                                 ctx_r[:].rearrange("p (g q j) -> p g q j", g=2, q=2)[:, :, q, :].unsqueeze(3).broadcast_to([P, 2, 4, HD2]),
                                                 ALU.mult).then_inc(ctx_normed, 1)

                def take_back(n):
                    dve.wait_ge(ctx_back, n + 1)
                    dve.tensor_copy(ctx_c[:], a_ps[:, 0:P]).then_inc(ctx_copied, 1)

                def add(n, i, b):
                    half = slice(C * b, C * b + C)
                    dve.wait_ge(o_ready, n + 1)
                    dve.scalar_tensor_tensor(out=x[half, ds(i, 1), :], in0=a_ps[half, N:2 * N], scalar=vec[half, 2:3], in1=x[half, ds(i, 1), :],
                                             op0=ALU.add, op1=ALU.add).then_inc(o_added, 1)

                def turn(g, j, A, S, D):
                    n, i, b = 4 * g + j, 2 * g + j // 2, j % 2
                    for k in range(8):
                        if A:
                            largest(n, b, k)
                        if k == 1 and S:
                            split_max(n - 1, 1 - b)
                        if k == 3 and D:
                            normalize(n - 3)
                        if k == 5 and D:
                            take_back(n - 3)
                        if k == 7 and D:
                            add(n - 3, i - 2 + b, 1 - b)

                turns(dve, turn)

            @block.scalar
            def _(act):
                gn.scalar(act)
                act.wait_ge(loaded, 16 * len(LOADS))
                for g in range(NQ):
                    for s, src, ready in ((0, ring[:, g], q_ps_ready), (1, k_bank(g), k_ps_ready)):
                        act.wait_ge(ready, g + 1)
                        if g:
                            act.wait_ge(parts_ready, 2 * g)
                        act.activation(full[:, s], src, ACT.Identity, bias=vec[:, s:s + 1]).then_inc(full_ready, 1)
                        act.wait_ge(full_ready, 2 * g + s + 1)
                        act.activation(parts[:, g, s, 0], src, ACT.Identity, bias=vec[:, s:s + 1]).then_inc(hi_ready, 1)
                act.sem_inc(e_ready, 2)
                act.sem_inc(ctx_ready, 2)

                def turn(g, j, A, S, D):
                    n, b = 4 * g + j, j % 2
                    c = n - 2
                    for k in range(8):
                        if A:
                            act.wait_ge(s_ready, 8 * c + k + 1)
                            if k in (0, 4):
                                act.wait_ge(ev_done, 2 * c + 3 + k // 4)
                            act.activation(e[:, k], ring[:, 2 + k % 2], ACT.Exp, scale=HD2 ** -0.5).then_inc(e_ready, 1)
                        if k == 1 and D:
                            act.wait_ge(ev_done, 2 * (c - 1) + 6)
                            act.wait_ge(ctx_turned, c)
                            act.activation(ctx[:, 1 - b], ctx_ps[:, 1 - b], ACT.Copy).then_inc(ctx_ready, 1)

                turns(act, turn, lag=2)

            @block.tensor
            def _(pe):
                gn.tensor(pe)
                pe.wait_ge(loaded, 16 * len(LOADS))
                for g in range(NQ):
                    pe.wait_ge(xn_ready, 2 * g + 2)
                    if g == 0:
                        pe.wait_ge(xn_ready, NP)
                    pe.matmul(ring[:, g], w_q[:], xn[:, 2 * g:2 * g + 2, :], start=True, stop=True).then_inc(q_ps_ready, 1)
                    pe.matmul(k_bank(g), w_k[:], xn[:, 2 * g:2 * g + 2, :], start=True, stop=True).then_inc(k_ps_ready, 1)
                for h in range(2):
                    pe.wait_ge(hi_ready, 4 * h + 4)
                    for p in range(4 * h, 4 * h + 4):
                        for t in range(2):
                            mm = pe.matmul(ring[:, p // 2, (2 * (p % 2) + t) * P:(2 * (p % 2) + t + 1) * P], xn[:, p, t * P:(t + 1) * P], w_v[:],
                                           start=True, stop=True)
                    mm.then_inc(v_ps_ready, 1)
                pe.sem_inc(mx_turned, 2)
                pe.sem_inc(ev_done, 4)
                pe.sem_inc(ctx_turned, 2)
                pe.wait_ge(v_all_ready, 2)
                pe.wait_ge(hi_ready, 2 * NQ)

                def largest(n, k, at):
                    h, p = k % 2, k // 2
                    g, j = at
                    pe.wait_ge(max_read, 8 * n + k + 1)
                    for q in range(2):
                        mm = pe.matmul(ring[:, k % 2, q * N:(q + 1) * N], q_st[:, h, ds(g, 1), p, j % 2, j // 2, q * P:(q + 1) * P], k_st[:, ds(g, 1), p, j % 2, j // 2, :],
                                       start=True, stop=True)
                    mm.then_inc(max_ps, 1)

                def scores(c, k, at):
                    p, t = k // 2, k % 2
                    g, j = at
                    if k == 0:
                        pe.wait_ge(m_stacked, 64 * c + 192)
                    pe.wait_ge(e_ready, 8 * c + k + 1)
                    pe.matmul(ring[:, 2 + k % 2], k_st[:, ds(g, 1), p, j % 2, j // 2, t * P:(t + 1) * P], q_st[:, :, ds(g, 1), p, j % 2, j // 2, :],
                              start=True, stop=True).then_inc(s_ready, 1)

                def context(c, b, g):
                    pe.wait_ge(e_ready, 8 * c + 4 * g + 6)
                    pe.wait_ge(v_x_ready, c + 1)
                    pe.wait_ge(ctx_ready, c + 1)
                    for t in range(2):
                        for j in range(4):
                            mm = pe.matmul(ctx_ps[32 * j:32 * j + 32, b, g * N:(g + 1) * N], v_x[:, b, t, 4 * g + j, :],
                                           e[:, 4 * g + 2 * (j // 2) + t, (j % 2) * N:(j % 2 + 1) * N], start=(t == 0), stop=(t == 1))
                    mm.then_inc(ev_done, 1)

                def turn(g, j, A, S, D):
                    n, b = 4 * g + j, j % 2
                    if j == 0 and A:
                        pe.wait_ge(stacked, 12 * 16 * (g + 1))
                    scored = not isinstance(g, int) or 2 <= n < B + 2
                    for k in range(8):
                        if A:
                            largest(n, k, (g, j))
                        if scored:
                            scores(n - 2, k, (g, j - 2) if j >= 2 else (g - 1, j + 2))
                        if k == 0 and S:
                            if not isinstance(g, int) or n > 1:
                                pe.wait_ge(m_ready, 2 * n - 2)
                            pe.wait_ge(max_read, 8 * n + 2)
                            for q in range(2):
                                mm = pe.transpose(m_ps[0:8, q * P:(q + 1) * P], mx[:, 1 - b, q, :], ident[:])
                            mm.then_inc(mx_turned, 1)
                        if k == 1 and D:
                            context(n - 3, 1 - b, 1)
                        if k == 2 and D:
                            pe.wait_ge(ctx_ready, n)
                            pe.wait_ge(o_added, n - 2)
                            for four in range(2):
                                for q in range(2):
                                    mm = pe.transpose(a_ps[:, (2 * four + q) * P:(2 * four + q + 1) * P], ctx[:, 1 - b, four, q * P:(q + 1) * P], ident[:])
                            mm.then_inc(ctx_turned, 1)
                        if k == 4 and D:
                            pe.wait_ge(ctx_normed, 2 * (n - 3) + 2)
                            pe.transpose(a_ps[:, 0:P], ctx_n[:].rearrange("p q g c -> p (q g c)"), ident[:]).then_inc(ctx_back, 1)
                        if k == 5 and scored:
                            context(n - 2, b, 0)
                        if k == 6 and D:
                            pe.wait_ge(ctx_copied, n - 2)
                            half = slice(C * (1 - b), C * (1 - b) + C)
                            for q in range(2):
                                mm = pe.matmul(a_ps[half, N + q * P:N + (q + 1) * P], w_o[:, q, :], ctx_c[:], start=True, stop=True)
                            mm.then_inc(o_ready, 1)

                turns(pe, turn)


def turns(eng, turn, lag=0):
    for n in range(4):
        turn(0, n, n >= lag, n >= 1, n >= 3)
    with eng.Fori(1, NQ) as g:
        for j in range(4):
            turn(g, j, True, True, True)
    for j in range(3):
        turn(NQ, j, j < lag, j == 0, True)


def layer3(nc, ins, signals, x, avg2):
    KK = 9
    TN = KK * N
    TW = 2 * KK * C // 3
    CH = 4
    THIRD = TN // 3
    with Memory(nc, "L3") as m:
        w_off, w_all = m.sb("w_off", [P, 6, 32]), m.sb("w_all", [P, 2 * KK * C])
        sel_f, sel = m.sb("sel_f", [P, 3, P]), m.sb("sel", [P, 3, P], BF16)
        grid, w_grid, vec = m.sb("grid", [P, N]), m.sb("w_grid", [P, 32]), m.sb("vec", [P, 3])
        xpad, stack = m.sb("xpad", [P, NP, HP * WP]), m.sb("stack", [P, B, HP * WP])
        off, sig = m.sb("off", [P, NQ, N]), m.sb("sig", [P, NQ, N])
        hat, mask = m.sb("hat", [P, TN]), m.sb("mask", [C, TN])
        rest, parts = m.sb("rest", [P, 2, THIRD]), m.sb("parts", [P, 3, TN], BF16)
        hats = m.sb("hats", [P, 2, 2, TN], BF16)
        xn, t_sb = m.sb("xn", [P, 2, N]), m.sb("t_sb", [P, 2, 2, 2 * KK * C])
        cols, s = m.sb("cols", [P, 2, 2 * N]), m.sb("s", [P, 2, 2, 2 * N])
        row_ps, col_ps, acc = m.ps("row_ps", [P, 2, 2, 2 * N]), m.ps("col_ps", [P, 2, 2 * N]), m.ps("acc", [P, 2, 2 * N])
        off_ps = lambda g: row_ps[:, g // 2, g % 2, 0:N]
        gn = GroupNorm(m, signals, "gn", avg2, acc[:, 0, 0:NP], acc[:, 1, 0:NP])
        off_dram = nc.dram_tensor("L3_offsets", (B, 3 * KK, N), F32, kind="Internal").ap()
        hat_dram = nc.dram_tensor("L3_hat_parts", (B // CH, 2, CH, H, 3, TN), BF16, kind="Internal").ap()

        (loaded, edge_ready, xpad_ready, sel_ready, off_conv, off_ready, off_stored, dist_ready, hat_ready, masked, hi_ready,
         rest_ready, mid_ready, parts_ready, hats_stored, hat_in) = m.sems(
            "loaded edge_ready xpad_ready sel_ready off_conv off_ready off_stored dist_ready hat_ready masked hi_ready "
            "rest_ready mid_ready parts_ready hats_stored hat_in")
        stack_in = m.sems("stack_in0 stack_in1 stack_in2 stack_in3")
        (hats_in, xn_ready, row_ready, col_ready, col_read, s_ready, s_used, added, passed) = m.sems(
            "hats_in xn_ready row_ready col_ready col_read s_ready s_used added passed")
        LOADS = [(w_off[:], "w_off"), (w_all[:], "w_all"), (sel_f[:], "sel"), (grid[:], "grid"), (w_grid[:], "w_grid"),
                 (vec[:], "l3_vec")]

        def hat_split(eng):
            def weigh_hat(c, j):
                cut = slice(THIRD * j, THIRD * j + THIRD)
                eng.wait_ge(hat_ready, 3 * c + j + 1)
                eng.tensor_tensor(hat[0:C, cut], hat[0:C, cut], mask[:, cut], ALU.mult).then_inc(masked, 1)

            def take_rest(c, j):
                cut = slice(THIRD * j, THIRD * j + THIRD)
                if not isinstance(c, int) or 3 * c + j > 1:
                    eng.wait_ge(parts_ready, 3 * c + j - 1)
                eng.wait_ge(hi_ready, 3 * c + j + 1)
                eng.tensor_tensor(rest[:, j % 2], hat[:, cut], parts[:, 0, cut], ALU.subtract).then_inc(rest_ready, 1)

            def take_last(c, j):
                cut = slice(THIRD * j, THIRD * j + THIRD)
                eng.wait_ge(mid_ready, 3 * c + j + 1)
                eng.tensor_tensor(parts[:, 2, cut], rest[:, j % 2], parts[:, 1, cut], ALU.subtract).then_inc(parts_ready, 1)

            return ((weigh_hat, 0), (weigh_hat, 1), (take_rest, 0), (weigh_hat, 2), (take_rest, 1), (take_last, 0),
                    (take_rest, 2), (take_last, 1), (take_last, 2))

        with nc.Block() as block:
            @block.sync
            def _(sp):
                for dst, src in LOADS:
                    sp.dma_start(dst, ins[src] if isinstance(src, str) else src).then_inc(loaded, 16)
                sp.wait_ge(edge_ready, 2)
                send_stack(sp, xpad_ready, stack_in, xpad, stack)

                def store_offsets(quads):
                    for j in range(4):
                        dst = off_dram.rearrange("(g j) r n -> j r g n", j=4)[j]
                        sp.dma_start(dst[0:2 * KK, quads], off[32 * j:32 * j + 2 * KK, quads]).then_inc(off_stored, 16)
                        sp.dma_start(dst[2 * KK:, quads], sig[32 * j + 2 * KK:32 * j + 3 * KK, quads]).then_inc(off_stored, 16)

                def load_positions(c):
                    four = off_dram[ds(CH * c, CH)]
                    for k in range(2):
                        src = four[:, KK * k:KK * k + KK].rearrange("u r n -> u (r n)").unsqueeze(1).broadcast_to([CH, H, TN])
                        sp.dma_start(hat[C * k:C * k + C, :], src).then_inc(hat_in, 16)
                    sp.dma_start(mask[:], four[:, 2 * KK:].rearrange("u r n -> u (r n)").unsqueeze(1).broadcast_to([CH, H, TN])).then_inc(hat_in, 16)

                def store_hats(c):
                    for j in range(3):
                        cut = slice(THIRD * j, THIRD * j + THIRD)
                        sp.wait_ge(parts_ready, 3 * c + j + 1)
                        sp.sem_inc(passed, 1)
                        sp.dma_start(hat_dram[ds(c, 1), :, :, :, :, cut].rearrange("c k u y t n -> (c k u y) t n"),
                                     parts[:, :, cut]).then_inc(hats_stored, 16)
                    sp.wait_ge(hats_stored, 48 * c + 48)
                    sp.sem_inc(passed, 1)

                def load_hats(n, c, b):
                    for k in range(2):
                        src = hat_dram[ds(c, 1), k, 2 * b:2 * b + 2].rearrange("c e y t n -> (c y t) e n")
                        sp.dma_start(hats[64 * k:64 * k + 3 * H, b], src).then_inc(hats_in, 16)
                    sp.wait_ge(hats_in, 32 * n + 32)
                    sp.sem_inc(passed, 1)

                def next_chunk(i, more):
                    store_hats(i + 1)
                    for b in range(2):
                        sp.wait_ge(s_used, KK * (2 * i + b) + 11)
                        sp.sem_inc(passed, 1)
                        load_hats(2 * i + 2 + b, i + 1, b)
                        if more and b == 0:
                            load_positions(i + 2)

                sp.wait_ge(off_ready, 2)
                store_offsets(slice(0, 1))
                sp.wait_ge(off_stored, 128)
                load_positions(0)
                sp.wait_ge(off_ready, 2 * NQ)
                store_offsets(slice(1, NQ))
                sp.wait_ge(edge_ready, 3)
                store_hats(0)
                load_hats(0, 0, 0)
                sp.wait_ge(off_stored, 256)
                load_positions(1)
                load_hats(1, 0, 1)
                with sp.Fori(0, B // CH - 2) as i:
                    next_chunk(i, True)
                next_chunk(B // CH - 2, False)

            @block.gpsimd
            def _(pool):
                pad_stack(nc, pool, edge_ready, xpad, stack)
                pool.wait_ge(edge_ready, 2)
                pool.memset(hats[32:64], 0.0).then_inc(edge_ready, 1)
                with pool.Fori(1, B // CH) as c:
                    for hat_step, j in hat_split(pool):
                        hat_step(c, j)

            @block.vector
            def _(dve):
                gn.vector(dve, lambda p: x[:, p, :])
                dve.wait_ge(edge_ready, 2)
                for p in range(NP):
                    dst = xpad[:, p, :].rearrange("p (r c) -> p r c", c=WP)[:, 1:1 + H, 1:1 + W]
                    dve.tensor_scalar(dst, x[:, p, :].rearrange("p (r c) -> p r c", c=W), gn.scale[:, p:p + 1], gn.shift[:, p:p + 1],
                                      ALU.mult, ALU.add).then_inc(xpad_ready, 1)
                dve.wait_ge(loaded, 16 * len(LOADS))
                dve.tensor_copy(sel[:], sel_f[:]).then_inc(sel_ready, 1)

                def norm(n, b):
                    dve.tensor_scalar(xn[:, b, :], x[:, ds(n, 1), :], gn.scale[:, ds(n, 1)], gn.shift[:, ds(n, 1)], ALU.mult, ALU.add).then_inc(xn_ready, 1)

                norm(0, 0)
                norm(1, 1)

                for hat_step, j in hat_split(dve):
                    hat_step(0, j)
                dve.sem_inc(s_ready, 2)
                dve.sem_inc(added, 2)

                def sample(n, b, t, c):
                    u, q = KK * n + t, (b + t) % 2
                    dve.wait_ge(row_ready, u + 1)
                    dve.wait_ge(col_read, c + 1)
                    dve.wait_ge(s_used, u + 1)
                    dve.tensor_tensor(s[:, q], row_ps[:, q], cols[:, q:q + 1].broadcast_to([P, 2, 2 * N]), ALU.mult).then_inc(s_ready, 1)

                def pair(n, b, more, _):
                    for t in range(1, KK):
                        sample(n, b, t, 7 + 15 * n + col_step(t - 1, more))
                        if t == 4 and more > 1:
                            dve.wait_ge(col_ready, 15 * n + 6)
                            norm(n + 2, b)
                    if more:
                        sample(n + 1, 1 - b, 0, 7 + 15 * n + col_step(KK - 1, more))
                    dve.wait_ge(s_used, KK * n + KK + 2)
                    dve.scalar_tensor_tensor(out=x[:, ds(n, 1), :], in0=acc[:, b, 0:N], scalar=vec[:, 2:3], in1=x[:, ds(n, 1), :],
                                             op0=ALU.add, op1=ALU.add).then_inc(added, 1)

                sample(0, 0, 0, 6)
                pairs(dve, pair)

            @block.scalar
            def _(act):
                gn.scalar(act)
                act.wait_ge(loaded, 16 * len(LOADS))
                for g in range(NQ):
                    act.wait_ge(off_conv, g + 1)
                    act.activation(off[:, g], off_ps(g), ACT.Identity, bias=vec[:, 0:1]).then_inc(off_ready, 1)
                    act.activation(sig[:, g], off_ps(g), ACT.Sigmoid, bias=vec[:, 0:1]).then_inc(off_ready, 1)

                def make_hat(c, j):
                    cut = slice(THIRD * j, THIRD * j + THIRD)
                    act.wait_ge(hat_in, 48 * c + 48)
                    act.activation(hat[:, cut], hat[:, cut], ACT.Abs, bias=vec[:, 1:2]).then_inc(dist_ready, 1)
                    act.wait_ge(dist_ready, 3 * c + j + 1)
                    act.activation(hat[:, cut], hat[:, cut], ACT.Relu, bias=1.0, scale=-1.0).then_inc(hat_ready, 1)

                def take_first(c, j):
                    cut = slice(THIRD * j, THIRD * j + THIRD)
                    act.wait_ge(masked, 3 * c + j + 1)
                    if not isinstance(c, int) or c > 0:
                        act.wait_ge(hats_stored, 48 * c)
                    act.activation(parts[:, 0, cut], hat[:, cut], ACT.Copy).then_inc(hi_ready, 1)

                def take_second(c, j):
                    cut = slice(THIRD * j, THIRD * j + THIRD)
                    act.wait_ge(rest_ready, 3 * c + j + 1)
                    act.activation(parts[:, 1, cut], rest[:, j % 2], ACT.Copy).then_inc(mid_ready, 1)

                def take_cols(v, c, q, r):
                    act.wait_ge(col_ready, c + 1)
                    act.wait_ge(s_ready, v + 1)
                    act.activation(cols[:, q], col_ps[:, r], ACT.Copy).then_inc(col_read, 1)

                def take_t(b, c, k, r):
                    act.wait_ge(col_ready, c + 1)
                    act.activation(t_sb[:, b, k // 3, ds(k % 3 * TW, TW)], col_ps[:, r, 0:TW], ACT.Copy).then_inc(col_read, 1)

                for hat_step, j in ((make_hat, 0), (make_hat, 1), (take_first, 0), (make_hat, 2), (take_first, 1), (take_second, 0),
                                    (take_first, 2), (take_second, 1), (take_second, 2)):
                    hat_step(0, j)
                for k in range(6):
                    take_t(0, k, k, k % 2)
                take_cols(0, 6, 0, 0)
                hat_steps = {1: (make_hat, 0), 2: (make_hat, 1), 3: (take_first, 0), 4: (make_hat, 2), 5: (take_first, 1),
                             6: (take_second, 0), 7: (take_first, 2), 8: (take_second, 1), 10: (take_second, 2)}

                def pair(n, b, more, chunk):
                    for t in range(KK):
                        loc = col_step(t, more)
                        c, r = 7 + 15 * n + loc, (1 + b + loc) % 2
                        if t < KK - 1 or more:
                            take_cols(KK * n + t + 1, c, (b + t + 1) % 2, r)
                        if t < 6 and more:
                            if t == 0:
                                act.wait_ge(s_used, KK * n + 2)
                            take_t(1 - b, c + 1, t, 1 - r)
                        if more > 1 and KK * b + t in hat_steps:
                            hat_step, j = hat_steps[KK * b + t]
                            hat_step(chunk, j)

                pairs(act, pair)

            @block.tensor
            def _(pe):
                gn.tensor(pe)
                pe.wait_ge(loaded, 16 * len(LOADS))
                for g in range(NQ):
                    pe.wait_ge(stack_in[g], 64)
                    for k in range(6):
                        for j in range(4):
                            mm = pe.matmul(off_ps(g)[32 * j:32 * j + 32], w_off[:, k, :], tap(stack, 4 * g + j, k), start=(k == 0), stop=False)
                    for j in range(4):
                        mm = pe.matmul(off_ps(g)[32 * j:32 * j + 32], w_grid[:], grid[:], start=False, stop=True)
                    mm.then_inc(off_conv, 1)
                pe.sem_inc(s_used, 2)

                def weigh(b, c, k, r):
                    if not isinstance(c, int) or c > 1:
                        pe.wait_ge(col_read, c - 1)
                    pe.matmul(col_ps[:, r, 0:TW], xn[:, b, k // 3 * P:(k // 3 + 1) * P], w_all[:, k % 3 * TW:(k % 3 + 1) * TW],
                              start=True, stop=True).then_inc(col_ready, 1)

                def spread(v, b, t, c, r):
                    q = (b + t) % 2
                    hat = hats[0:112, b, :, t * N:(t + 1) * N]
                    pe.wait_ge(s_ready, v + 1)
                    for h in range(2):
                        mm = pe.matmul(row_ps[:, q, h], sel[0:112, h], hat, start=True, stop=True)
                    mm.then_inc(row_ready, 1)
                    pe.wait_ge(col_read, c - 1)
                    pe.matmul(col_ps[:, r], sel[0:112, 2], hat, start=True, stop=True).then_inc(col_ready, 1)

                def samples(n, b, t):
                    u, q = KK * n + t, (b + t) % 2
                    pe.wait_ge(s_ready, u + 3)
                    if t == 0:
                        pe.wait_ge(added, n + 1)
                        pe.wait_ge(col_read, 15 * n + 6)
                    for h in range(2):
                        for e in range(2):
                            mm = pe.matmul(acc[C * e:C * e + C, b, 0:N], t_sb[:, b, h, (KK * e + t) * C:(KK * e + t + 1) * C],
                                           s[:, q, h, e * N:(e + 1) * N], start=(t == 0 and h == 0), stop=(t == KK - 1 and h == 1))
                    mm.then_inc(s_used, 1)

                pe.wait_ge(xn_ready, 1)
                for k in range(6):
                    weigh(0, k, k, k % 2)
                pe.wait_ge(off_ready, 2 * NQ)
                pe.wait_ge(sel_ready, 1)
                pe.wait_ge(hats_in, 32)
                spread(0, 0, 0, 6, 0)

                def pair(n, b, more, _):
                    for t in range(KK):
                        loc = col_step(t, more)
                        c, r = 7 + 15 * n + loc, (1 + b + loc) % 2
                        if t < KK - 1:
                            spread(KK * n + t + 1, b, t + 1, c, r)
                        elif more:
                            pe.wait_ge(hats_in, 32 * n + 64)
                            spread(KK * n + KK, 1 - b, 0, c, r)
                        if t < 6 and more:
                            if t == 0:
                                pe.wait_ge(xn_ready, n + 2)
                            weigh(1 - b, c + 1, t, 1 - r)
                        samples(n, b, t)

                pairs(pe, pair)


def col_step(t, more):
    return t + min(t, 6) if more else t


def pairs(eng, pair):
    with eng.Fori(0, NP // 2 - 1) as i:
        for b in range(2):
            pair(2 * i + b, b, 2, i + 1)
    pair(NP - 2, 0, 1, None)
    pair(NP - 1, 1, 0, None)


def program(nc, ins, out, layers=4):
    Memory.semaphores = ExitStack()
    with Memory.semaphores, Memory(nc, "all") as m:
        x, avg2 = m.sb("x", [P, NP, N]), m.sb("avg2", [P, P])
        x_in, x_out = m.sems("x_in x_out")
        signals = NormSignals(m)
        with nc.Block() as block:
            @block.sync
            def _(sp):
                sp.dma_start(x[:], ins["x"].rearrange("(n e) c h w -> (e c) n (h w)", e=2)).then_inc(x_in, 16)
                sp.dma_start(avg2[:], ins["avg2"]).then_inc(x_in, 16)
        layer0(nc, ins, signals, x, x_in, avg2)
        if layers > 1:
            layer1(nc, ins, signals, x, avg2)
        if layers > 2:
            layer2(nc, ins, signals, x, avg2)
        if layers > 3:
            layer3(nc, ins, signals, x, avg2)
        with nc.Block() as block:
            @block.sync
            def _(sp):
                sp.dma_start(out.rearrange("(n e) c h w -> (e c) n (h w)", e=2), x[:]).then_inc(x_out, 16)
                sp.wait_ge(x_out, 16)


def two_blocks(a):
    r, c = a.shape
    out = np.zeros((2 * r, 2 * c), a.dtype)
    out[:r, :c], out[r:, c:] = a, a
    return out


def lay_out(a):
    f = np.float32
    part = np.arange(P)
    t = {"x": a["x"]}
    t["avg2"] = (part[:, None] // 2 == part[None, :] // 2).astype(f) / f(2)
    t["avg8"] = (part[:, None] // 8 == part[None, :] // 8).astype(f) / f(8)
    t["w_pre"], t["w_post"] = two_blocks(a["L0_conv_pre_w"].T), two_blocks(a["L0_conv_post_w"].T)
    names = ["pre_b", "pre_gn_g", "pre_gn_b", "post_b", "post_gn_g", "post_gn_b"]
    t["l0_vec"] = np.stack([np.tile(a["L0_conv_" + n], 2) for n in names], 1)
    t["w_s1"] = two_blocks(a["L0_conv_sp_w1"])
    t["b_s1"] = np.tile(a["L0_conv_sp_b1"], 2)[:, None]
    t["w_s2"] = np.tile(two_blocks(a["L0_conv_sp_w2"]), (1, G0))
    t["b_s2"] = np.tile(a["L0_conv_sp_b2"], 2 * G0)[:, None]
    group_k, parity_k = part // 32, part // 16 % 2
    group_c, parity_c = part % C // 16, part // C
    t["same_group"] = ((group_k[:, None] == group_c) & (parity_k[:, None] == parity_c)).astype(f)
    kinds = ["alpha", "mu", "sigma", "mix", "gate"]
    w = np.concatenate([a[f"L0_conv_{k}_w"].reshape(S0, G0, -1) for k in kinds], 2)
    b = np.concatenate([a[f"L0_conv_{k}_b"].reshape(G0, -1) for k in kinds], 1)
    t["w_par"] = np.repeat(w.transpose(1, 0, 2)[:, None], 2, 1).reshape(P, NPAR)
    w = a["L1_conv_W_in"].T
    none = np.zeros((C, DI), f)
    t["w_z"] = np.concatenate([w[:, :DI], none])
    t["w_in"] = np.tile(w[:, DI:2 * DI + 2 * DS1], (2, 1))
    t["w_dt"] = np.concatenate([np.pad(w[:, 2 * DI + 2 * DS1:], ((0, 0), (0, 32 - NH1))), none[:, :32]])
    t["w_out"], t["w_out2"] = a["L1_conv_W_out"].T, np.tile(a["L1_conv_W_out"].T, (1, 2))
    t["ident"] = np.eye(P, dtype=f)
    t["center"] = np.eye(P, dtype=f) - f(1 / DI)
    t["ones"] = np.full((P, C), 1 / DI, f)
    t["quarter"] = (part[:, None] // 32 == np.arange(4)).astype(f)
    heads = lambda v: np.tile(np.pad(v, (0, 32 - NH1)), 4)
    cb = a["L1_conv_conv_b"]
    t["l1_vec"] = np.stack([cb[:DI], np.tile(cb[DI:], 4), np.repeat(a["L1_conv_D"], HD1), a["L1_conv_ln_g"], a["L1_conv_ln_b"],
                            heads(a["L1_conv_dt_bias"]), heads(a["L1_conv_A_log"])], 1)
    t["conv_w"] = a["L1_conv_conv_w"][:, 0].transpose(1, 2, 0)
    order = np.arange(C).reshape(4, 2, HD2).transpose(1, 2, 0).reshape(C)
    t["w_q"], t["w_k"], t["w_v"] = two_blocks(a["L2_conv_Wq"][order].T), two_blocks(a["L2_conv_Wk"][order].T), two_blocks(a["L2_conv_Wv"].T)
    t["w_o"] = two_blocks(a["L2_conv_Wo"].T).reshape(P, 2, C)
    t["b_v"] = np.tile(a["L2_conv_bv"], (P, 2))
    t["l2_vec"] = np.stack([np.tile(v, 2) for v in (a["L2_conv_bq"][order], a["L2_conv_bk"][order], a["L2_conv_bo"])], 1)
    w = np.concatenate([a["L3_conv_off_w"][0::2], a["L3_conv_off_w"][1::2], a["L3_conv_mask_w"]])
    w_off = np.zeros((2, C, 2, W3, 32), f)
    w_off[0, :, :, :, :27] = w[:, :, 0::2].transpose(1, 2, 3, 0)
    w_off[1, :, 0, :, :27] = w[:, :, 1].transpose(1, 2, 0)
    t["w_off"] = w_off.reshape(P, 6, 32)
    t["w_all"] = two_blocks(a["L3_conv_weight"].transpose(1, 2, 3, 0).reshape(C, -1))
    bias = np.concatenate([a["L3_conv_off_b"][0::2], a["L3_conv_off_b"][1::2], a["L3_conv_mask_b"]])
    t["l3_vec"] = np.stack([np.tile(np.pad(bias, (0, 32 - 27)), 4), -(part % H).astype(f), np.tile(a["L3_conv_bias"], 2)], 1)
    k, r = np.divmod(part, 3)
    col = part[None, :]
    rows = [(part[:, None] < 48) & (k[:, None] == 8 * h + col // W) for h in range(2)]
    k = (part - 64) // 3
    t["sel"] = np.stack(rows + [(part[:, None] >= 64) & (part[:, None] < 112) & (k[:, None] == col % W)], 1).astype(f)
    tap_y, tap_x = np.divmod(np.arange(9), 3)
    pos_y, pos_x = np.divmod(np.arange(N), W)
    t["grid"] = np.concatenate([np.stack([pos_y, pos_x, np.ones(N)]), np.zeros((P - 3, N))]).astype(f)
    w_grid = np.zeros((P, 32), f)
    w_grid[0, :9], w_grid[1, 9:18], w_grid[2, :18] = 1, 1, np.concatenate([tap_y, tap_x]) - 1
    t["w_grid"] = w_grid
    t["b_par"] = np.tile(np.repeat(b, 16, 0), (2, 1))
    return t


def kernel(**inputs):
    import concourse.bacc as bacc
    from concourse.bass_utils import run_bass_kernel_spmd

    nc = bacc.Bacc("TRN2", target_bir_lowering=False, num_devices=1)
    arrays, ins = {}, {}
    for name, a in lay_out({k: np.asarray(v) for k, v in inputs.items()}).items():
        a = np.ascontiguousarray(a)
        arrays[f"in_{name}"] = a
        ins[name] = nc.dram_tensor(f"in_{name}", a.shape, mybir.dt.from_np(a.dtype), kind="ExternalInput").ap()
    out = nc.dram_tensor("out_x", (B, C, H, W), F32, kind="ExternalOutput").ap()
    program(nc, ins, out)
    r = run_bass_kernel_spmd(nc, [arrays], core_ids=[0])
    return r.results[0]["out_x"]
```

```python
from contextlib import ExitStack

import numpy as np

import concourse.bass as bass
from concourse import mybir

F32 = mybir.dt.float32
BF16 = mybir.dt.bfloat16
ALU = mybir.AluOpType
ACT = mybir.ActivationFunctionType
AX = mybir.AxisListType

B, C, H, W = 16, 64, 16, 16
N = H * W
P = 128
NP = B // 2
EPS = 1e-5

G0, NB, S0 = 4, 6, 16
NPAR = 4 * NB + 1
POOLED = 2

DI, NH1, HD1, DS1 = 128, 8, 16, 16
HP, WP = H + 2, W + 2
W3 = 3
NH2, HD2 = 8, 8
NQ = B // 4
WEIGHED = (0, 2, 3, 5, 6, 7)


def ds(start, size):
    return bass.ds(start, size)


def from_turn(n, first):
    return not isinstance(n, int) or n >= first


class Memory:

    semaphores = None

    def __init__(self, nc, name):
        self.nc, self.name, self.ctx = nc, name, ExitStack()

    def __enter__(self):
        self.ctx.__enter__()
        return self

    def __exit__(self, *a):
        return self.ctx.__exit__(*a)

    def sb(self, name, shape, dt=F32):
        return self.ctx.enter_context(self.nc.sbuf_tensor(f"{self.name}_{name}", shape, dt))

    def ps(self, name, shape, dt=F32):
        return self.ctx.enter_context(self.nc.psum_tensor(f"{self.name}_{name}", shape, dt))

    def sem(self, name):
        return Memory.semaphores.enter_context(self.nc.semaphore(f"{self.name}_{name}"))

    def sems(self, names):
        return [self.sem(n) for n in names.split()]


class Steps:

    def __init__(self, eng, sem, n=0):
        self.eng, self.sem, self.n = eng, sem, n

    def __call__(self, ins):
        ins.then_inc(self.sem, 1)
        self.n += 1
        self.eng.wait_ge(self.sem, self.n)

    def free(self, ins):
        ins.then_inc(self.sem, 1)
        self.n += 1

    def settle(self):
        self.eng.wait_ge(self.sem, self.n)


class NormSignals:

    def __init__(self, mem):
        self.own, self.stats_ready, self.mean_ready, self.sp_ready, self.spread_ready, self.var_ready, self.sd_ready = (
            mem.sems("norm_own norm_stats norm_mean norm_sp norm_spread norm_var norm_sd"))
        self.norms = self.own_steps = 0
        self.x_bn, self.x_stats = mem.sb("x_bn", [P, NP, 6]), mem.sem("x_stats")


class GroupNorm:

    def __init__(self, mem, signals, name, avg, mean, spread, of_x=0):
        self.signals = signals
        signals.norms += 1
        self.turn = signals.norms
        self.avg, self.mean, self.spread = avg, mean, spread
        self.of_x = of_x
        self.bn, self.mv = signals.x_bn if of_x else mem.sb(name + "_bn", [P, NP, 6]), mem.sb(name + "_mv", [P, NP, 2])
        self.d, self.sp, self.var, self.sd, self.scale, self.shift = (
            mem.sb(f"{name}_{n}", [P, NP]) for n in ("d", "sp", "var", "sd", "scale", "shift"))

    def vector(self, dve, source=None, bias=None, gamma=None, beta=None):
        on, turn = self.signals, self.turn
        step = Steps(dve, on.own, on.own_steps)
        if self.of_x:
            dve.wait_ge(on.x_stats, NP * self.of_x)
        else:
            for p in range(NP):
                step.free(dve.bn_stats(self.bn[:, p, :], source(p)))
            step.settle()
        for p in range(NP):
            step.free(dve.bn_aggr(self.mv[:, p, :], self.bn[:, p, :]))
        step.settle()
        if bias is not None:
            step(dve.tensor_scalar(self.mv[:, :, 0], self.mv[:, :, 0], bias, None, ALU.add))
        dve.sem_inc(on.stats_ready, 1)
        dve.wait_ge(on.mean_ready, turn)
        step(dve.tensor_tensor(self.d[:], self.mv[:, :, 0], self.mean, ALU.subtract))
        step(dve.tensor_tensor(self.sp[:], self.d[:], self.d[:], ALU.mult))
        dve.tensor_tensor(self.var[:], self.sp[:], self.mv[:, :, 1], ALU.add).then_inc(on.sp_ready, 1)
        dve.wait_ge(on.spread_ready, turn)
        dve.tensor_scalar(self.sp[:], self.spread, EPS, None, ALU.add).then_inc(on.var_ready, 1)
        dve.wait_ge(on.sd_ready, turn)
        step(dve.reciprocal(self.scale[:], self.sd[:]))
        if gamma is not None:
            step(dve.tensor_scalar(self.scale[:], self.scale[:], gamma, None, ALU.mult))
        if bias is None:
            step(dve.tensor_scalar(self.d[:], self.mean, -1.0, None, ALU.mult))
        else:
            step(dve.tensor_scalar(self.d[:], self.mean, bias, -1.0, ALU.subtract, ALU.mult))
        step(dve.tensor_tensor(self.shift[:], self.d[:], self.scale[:], ALU.mult))
        if beta is not None:
            step(dve.tensor_scalar(self.shift[:], self.shift[:], beta, None, ALU.add))
        on.own_steps = step.n

    def tensor(self, pe):
        on, turn = self.signals, self.turn
        pe.wait_ge(on.stats_ready, turn)
        pe.matmul(self.mean, self.avg[:], self.mv[:, :, 0], start=True, stop=True).then_inc(on.mean_ready, 1)
        pe.wait_ge(on.sp_ready, turn)
        pe.matmul(self.spread, self.avg[:], self.var[:], start=True, stop=True).then_inc(on.spread_ready, 1)

    def scalar(self, act):
        on, turn = self.signals, self.turn
        act.wait_ge(on.var_ready, turn)
        act.activation(self.sd[:], self.sp[:], ACT.Sqrt).then_inc(on.sd_ready, 1)


class Weights:

    def __init__(self, m, ins):
        shapes = [
            dict(w_pre=[P, P], avg8=[P, P], l0_vec=[P, 6], w_s1=[P, 32], b_s1=[32, 1], w_s2=[32, P], b_s2=[P, 1],
                 same_group=[P, P], w_par=[P, NPAR], b_par=[P, NPAR], w_post=[P, P]),
            dict(w_in=[P, DI + 32], w_z=[P, DI], w_dt=[P, 32], w_out=[P, C], w_out2=[P, P], ident=[P, P], center=[P, P],
                 ones=[P, C], quarter=[P, 4], l1_vec=[P, 7]),
            dict(w_q=[P, P], w_k=[P, P], w_v=[P, P], w_o=[P, 2, C], b_v=[P, P], l2_vec=[P, 3]),
            dict(w_off=[P, 6, 32], w_all=[P, 2 * W3 * W3 * C], sel=[P, 3, P], grid=[P, N], w_grid=[P, 32], l3_vec=[P, 3])]
        self.loaded = m.sems("loaded0 loaded1 loaded2 loaded3")
        self.tile = {name: m.sb(name, shape) for layer in shapes for name, shape in layer.items()}
        self.loads = [[(self.tile[name][:], ins[name]) for name in layer] for layer in shapes]
        cw = self.tile["conv_w"] = m.sb("conv_w", [P, 6, DI + 32])
        self.loads[1] += [(cw[C * e:C * e + C, 3 * k:3 * k + 3, :], ins["conv_w"][2 * k + e:2 * k + e + 1].broadcast_to([C, 3, DI + 32]))
                          for k, e in ((0, 0), (0, 1), (1, 0))]

    def load(self, sp, layers):
        for layer in layers:
            for dst, src in self.loads[layer]:
                sp.dma_start(dst, src).then_inc(self.loaded[layer], 16)

    def wait(self, eng, layer):
        eng.wait_ge(self.loaded[layer], 16 * len(self.loads[layer]))

    def named(self, names):
        return [self.tile[n] for n in names.split()]


def layer0(nc, ins, signals, weights, x, avg2):
    with Memory(nc, "L0") as m:
        w_pre, w_post, avg8, same_group, w_s1, w_s2, w_par, b_par, b_s1, b_s2, vec = weights.named(
            "w_pre w_post avg8 same_group w_s1 w_s2 w_par b_par b_s1 b_s2 l0_vec")
        xn, z = m.sb("xn", [P, NP, N]), m.sb("z", [P, NP, N])
        pooled, h1, h2, h2_w = m.sb("pooled", [P, NP]), m.sb("h1", [32, NP]), m.sb("h2", [P, NP]), m.sb("h2_w", [P, NP, NPAR])
        par = m.sb("par", [P, NP, NPAR])
        ealpha, esigma, lnsigma, sigma, inv, minus_mu, mix, c0, c1, zc0, zc1, alpha = (
            m.sb(n, [P, NP, NB]) for n in ("ealpha", "esigma", "lnsigma", "sigma", "inv", "minus_mu", "mix", "c0", "c1", "zc0", "zc1", "alpha"))
        amax, asum, gate = m.sb("amax", [P, NP]), m.sb("asum", [P, NP]), m.sb("gate", [P, NP])
        uu, ex, poly, t = (m.sb(n, [P, 2, NB, N]) for n in ("uu", "ex", "poly", "t"))
        y1, y2 = m.ps("y1", [P, NP, N]), m.ps("y2", [P, NP, N])
        gn_x = GroupNorm(m, signals, "gn_x", avg2, y2[:, 0, 0:NP], y2[:, 2, 0:NP], of_x=1)
        gn_1 = GroupNorm(m, signals, "gn_1", avg8, y2[:, 0, 0:NP], y2[:, 2, 0:NP])
        gn_2 = GroupNorm(m, signals, "gn_2", avg8, y1[:, 0, 0:NP], y1[:, 2, 0:NP])
        s1, s2 = y2[0:32, 4, 0:NP], y2[:, 6, 0:NP]
        par_ps = y2[:, 4, 0:NP * NPAR].rearrange("p (n k) -> p n k", n=NP)

        avg_in, *x_in = m.sems("avg_in x_in0 x_in1")
        (own, xn_ready, y1_ready, norm1_ready, z_ready, s1_ready, h1_ready, s2_ready, h2_ready, h2_w_ready,
         par_ready, exp_in, exp_out, coef_ready) = m.sems(
            "own xn_ready y1_ready norm1_ready z_ready s1_ready h1_ready s2_ready h2_ready h2_w_ready "
            "par_ready exp_in exp_out coef_ready")
        (uu_ready, pooled_ready, e_ready, poly_ready, t_ready, t_used, norm2_ready, out_ready, added, odd_added) = m.sems(
            "uu_ready pooled_ready e_ready poly_ready t_ready t_used norm2_ready out_ready added odd_added")

        with nc.Block() as block:
            @block.gpsimd
            def _(pool):
                pool.wait_ge(coef_ready, 1)
                with pool.Fori(0, NP // 2) as i:
                    for q in range(2):
                        k = 2 * i + q
                        z_k = z[:, ds(k, 1), :].broadcast_to([P, POOLED, N])
                        per_basis = lambda v: v[:, ds(k, 1), NB - POOLED:].rearrange("p k j -> p (k j)").unsqueeze(2).broadcast_to([P, POOLED, N])
                        last = uu[:, q, NB - POOLED:, :]
                        pool.wait_ge(t_ready, k + 1)
                        pool.tensor_tensor(last, z_k, per_basis(inv), ALU.mult).then_inc(pooled_ready, 1)
                        pool.wait_ge(pooled_ready, 3 * k + 1)
                        pool.tensor_tensor(last, last, per_basis(minus_mu), ALU.add).then_inc(pooled_ready, 1)
                        pool.wait_ge(pooled_ready, 3 * k + 2)
                        pool.tensor_tensor(last, last, last, ALU.mult).then_inc(pooled_ready, 1)
                for p in range(1, NP, 2):
                    pool.wait_ge(out_ready, p + 1)
                    pool.tensor_tensor(x[:, p, :], x[:, p, :], xn[:, p, :], ALU.add).then_inc(odd_added, 1)

            @block.sync
            def _(sp):
                sp.dma_start(avg2[:], ins["avg2"]).then_inc(avg_in, 16)
                for h in range(2):
                    half = slice(4 * h, 4 * h + 4)
                    sp.dma_start(x[:, half], ins["x"].rearrange("(n e) c h w -> (e c) n (h w)", e=2)[:, half]).then_inc(x_in[h], 16)
                weights.load(sp, range(4))

            @block.vector
            def _(dve):
                for p in range(NP):
                    if p % 4 == 0:
                        dve.wait_ge(x_in[p // 4], 16)
                    dve.bn_stats(signals.x_bn[:, p, :], x[:, p, :]).then_inc(signals.x_stats, 1)
                gn_x.vector(dve)
                for p in range(NP):
                    dve.tensor_scalar(xn[:, p, :], x[:, p, :], gn_x.scale[:, p:p + 1], gn_x.shift[:, p:p + 1],
                                      ALU.mult, ALU.add).then_inc(xn_ready, 1)

                def y1_pair(p):
                    if p % 2 == 0:
                        dve.wait_ge(y1_ready, p // 2 + 1)
                    return y1[:, p, :]

                weights.wait(dve, 0)
                gn_1.vector(dve, y1_pair, vec[:, 0:1], vec[:, 1:2], vec[:, 2:3])
                dve.sem_inc(norm1_ready, 1)

                step = Steps(dve, own)
                dve.wait_ge(h2_ready, 1)
                dve.tensor_tensor(h2_w[:], w_par[:, :].unsqueeze(1).broadcast_to([P, NP, NPAR]),
                                  h2[:, :].unsqueeze(2).broadcast_to([P, NP, NPAR]), ALU.mult).then_inc(h2_w_ready, 1)
                dve.wait_ge(par_ready, 1)
                step(dve.tensor_tensor(par[:], par_ps, b_par[:, :].unsqueeze(1).broadcast_to([P, NP, NPAR]), ALU.add))
                al, mu, sg, mx = (par[:, :, NB * k:NB * (k + 1)] for k in range(4))
                per_basis = lambda v: v[:, :].unsqueeze(2).broadcast_to([P, NP, NB])
                step(dve.tensor_reduce(amax[:], al, AX.X, ALU.max))
                step(dve.tensor_tensor(alpha[:], al, per_basis(amax), ALU.subtract))
                step(dve.tensor_scalar(sigma[:], sg, -1.0, None, ALU.mult))
                step(dve.tensor_tensor(sigma[:], sigma[:], sg, ALU.min))
                dve.sem_inc(exp_in, 1)
                dve.wait_ge(exp_out, 5)
                step(dve.tensor_reduce(asum[:], ealpha[:], AX.X, ALU.add))
                step(dve.tensor_scalar(gate[:], gate[:], 1.0, None, ALU.add))
                step(dve.tensor_tensor(asum[:], asum[:], gate[:], ALU.mult))
                step(dve.reciprocal(asum[:], asum[:]))
                step(dve.tensor_tensor(alpha[:], ealpha[:], per_basis(asum), ALU.mult))
                step(dve.tensor_scalar(mix[:], mix[:], 1.0, None, ALU.add))
                step(dve.reciprocal(mix[:], mix[:]))
                step(dve.scalar_tensor_tensor(out=sigma[:], in0=sg, scalar=0.0, in1=lnsigma[:], op0=ALU.max, op1=ALU.add))
                step(dve.tensor_scalar(sigma[:], sigma[:], 0.001, None, ALU.add))
                step(dve.reciprocal(inv[:], sigma[:]))
                step(dve.scalar_tensor_tensor(out=minus_mu[:], in0=mu, scalar=-1.0, in1=inv[:], op0=ALU.mult, op1=ALU.mult))
                dve.sem_inc(coef_ready, 1)
                step(dve.tensor_tensor(c0[:], alpha[:], mix[:], ALU.mult))
                step(dve.tensor_tensor(c1[:], alpha[:], c0[:], ALU.subtract))
                step(dve.tensor_tensor(zc1[:], c1[:], inv[:], ALU.mult))
                step(dve.tensor_tensor(zc0[:], c1[:], minus_mu[:], ALU.mult))
                step(dve.tensor_tensor(zc0[:], zc0[:], c0[:], ALU.add))
                dve.sem_inc(t_ready, 2)

                with dve.Fori(0, NP // 2) as i:
                    for q in range(2):
                        k = 2 * i + q
                        dve.wait_ge(t_ready, k + 1)
                        for j in range(NB):
                            dve.tensor_scalar(poly[:, q, j, :], z[:, ds(k, 1), :], zc1[:, ds(k, 1), j], zc0[:, ds(k, 1), j],
                                              ALU.mult, ALU.add).then_inc(poly_ready, 1)
                        dve.wait_ge(poly_ready, NB * k + NB)
                        dve.wait_ge(e_ready, k + 1)
                        dve.wait_ge(t_used, k + 1)
                        dve.tensor_tensor(t[:, q], poly[:, q], ex[:, q], ALU.mult).then_inc(t_ready, 1)

                def y2_pair(p):
                    dve.wait_ge(t_used, (p | 1) + 3)
                    return y2[:, p, :]

                gn_2.vector(dve, y2_pair, vec[:, 3:4], vec[:, 4:5], vec[:, 5:6])
                dve.sem_inc(norm2_ready, 1)
                for p in range(NP):
                    if p % 2 == 0:
                        dve.wait_ge(out_ready, p + 1)
                        dve.tensor_tensor(x[:, p, :], x[:, p, :], xn[:, p, :], ALU.add).then_inc(added, 1)
                        dve.wait_ge(added, p // 2 + 1)
                    else:
                        dve.wait_ge(odd_added, p // 2 + 1)
                    dve.bn_stats(signals.x_bn[:, p, :], x[:, p, :]).then_inc(signals.x_stats, 1)

            @block.tensor
            def _(pe):
                pe.wait_ge(avg_in, 16)
                gn_x.tensor(pe)
                weights.wait(pe, 0)
                for h in range(NP // 2):
                    pe.wait_ge(xn_ready, 2 * h + 2)
                    pe.matmul(y1[:, 2 * h:2 * h + 2, :], w_pre[:], xn[:, 2 * h:2 * h + 2, :], start=True, stop=True).then_inc(y1_ready, 1)
                gn_1.tensor(pe)
                pe.wait_ge(z_ready, NP)
                pe.matmul(s1, w_s1[:], pooled[:], start=True, stop=True).then_inc(s1_ready, 1)
                pe.wait_ge(h1_ready, 1)
                pe.matmul(s2, w_s2[0:32, :], h1[:], start=True, stop=True).then_inc(s2_ready, 1)
                pe.wait_ge(h2_w_ready, 1)
                pe.matmul(par_ps, same_group[:], h2_w[:], start=True, stop=True).then_inc(par_ready, 1)
                pe.sem_inc(t_used, 2)
                pe.wait_ge(coef_ready, 1)
                with pe.Fori(0, NP // 2) as i:
                    for q in range(2):
                        k = 2 * i + q
                        pe.matmul(y2[:, ds(k, 1), :], w_post[:], z[:, ds(k, 1), :], start=True, stop=False)
                        pe.wait_ge(t_ready, k + 3)
                        for j in range(NB):
                            mm = pe.matmul(y2[:, ds(k, 1), :], w_post[:], t[:, q, j:j + 1, :], start=False, stop=(j == NB - 1))
                        mm.then_inc(t_used, 1)
                gn_2.tensor(pe)

            @block.scalar
            def _(act):
                gn_x.scalar(act)
                gn_1.scalar(act)
                act.wait_ge(norm1_ready, 1)
                for p in range(NP):
                    act.activation(z[:, p, :], y1[:, p, :], ACT.Silu, scale=gn_1.scale[:, p:p + 1], bias=gn_1.shift[:, p:p + 1],
                                   accum_out=pooled[:, p:p + 1]).then_inc(z_ready, 1)
                act.wait_ge(s1_ready, 1)
                act.activation(h1[:], s1, ACT.Gelu_apprx_tanh, scale=1.0 / N, bias=b_s1[0:32, :]).then_inc(h1_ready, 1)
                act.wait_ge(s2_ready, 1)
                act.activation(h2[:], s2, ACT.Gelu_apprx_tanh, bias=b_s2[:]).then_inc(h2_ready, 1)
                act.wait_ge(exp_in, 1)
                act.activation(ealpha[:], alpha[:], ACT.Exp).then_inc(exp_out, 1)
                act.activation(esigma[:], sigma[:], ACT.Exp).then_inc(exp_out, 1)
                act.activation(mix[:], par[:, :, 3 * NB:4 * NB], ACT.Exp, scale=-1.0).then_inc(exp_out, 1)
                act.activation(gate[:], par[:, :, NPAR - 1], ACT.Exp, scale=-1.0).then_inc(exp_out, 1)
                act.wait_ge(exp_out, 4)
                act.activation(lnsigma[:], esigma[:], ACT.Ln, bias=1.0).then_inc(exp_out, 1)
                with act.Fori(0, NP // 4) as i:
                    for turn in range(4):
                        k, q = 4 * i + turn, turn % 2
                        act.wait_ge(t_ready, k + 1)
                        for j in range(NB - POOLED):
                            act.activation(uu[:, q, j, :], z[:, ds(k, 1), :], ACT.Square, scale=inv[:, ds(k, 1), j],
                                           bias=minus_mu[:, ds(k, 1), j]).then_inc(uu_ready, 1)
                        act.wait_ge(uu_ready, (NB - POOLED) * (k + 1))
                        act.wait_ge(pooled_ready, 3 * k + 3)
                        act.activation(ex[:, q], uu[:, q], ACT.Exp, scale=-1.0).then_inc(e_ready, 1)
                gn_2.scalar(act)
                act.wait_ge(norm2_ready, 1)
                for p in range(NP):
                    act.activation(xn[:, p, :], y2[:, p, :], ACT.Silu, scale=gn_2.scale[:, p:p + 1],
                                   bias=gn_2.shift[:, p:p + 1]).then_inc(out_ready, 1)


def pad_stack(pool, edge_ready, xpad, stack):
    pool.memset(xpad[:], 0.0).then_inc(edge_ready, 1)
    pool.wait_ge(edge_ready, 1)
    pool.memset(stack[C:P, :, H * WP + WP:HP * WP], 0.0).then_inc(edge_ready, 1)


def send_stack(sp, xpad_ready, stack_in, xpad, stack):
    for g in range(NQ):
        sp.wait_ge(xpad_ready, 2 * g + 2)
        src = xpad[:, 2 * g:2 * g + 2, :]
        dst = stack[:, 4 * g:4 * g + 4, :].rearrange("p (n e) s -> p n e s", e=2)
        for e in range(2):
            sp.dma_start(dst[0:C, :, e, :], src[C * e:C * e + C]).then_inc(stack_in[g], 16)
            sp.dma_start(dst[C:P, :, e, 0:(HP - 1) * WP], src[C * e:C * e + C, :, WP:HP * WP]).then_inc(stack_in[g], 16)


def image(stack, b, n=1):
    return stack[:, ds(b, n), :].rearrange("p n (r c) -> p n r c", c=WP)


def tap(stack, b, g, n=1):
    r, c = (0, g) if g < 3 else (2, g - 3)
    return image(stack, b, n)[:, :, r:r + H, c:c + W]


class Stacks:

    def __init__(self, m):
        self.k_st, self.q_st = m.sb("k_st", [P, NQ, 4, 2, 2, N], BF16), m.sb("q_st", [P, 2, NQ, 4, 2, 2, N], BF16)
        self.filled = m.sem("filled")

    def fill(self, pool):
        for g in range(NQ):
            pool.memset(self.q_st[:, :, g], 0.0).then_inc(self.filled, 1)
            pool.memset(self.k_st[:, g], 1.0).then_inc(self.filled, 1)


def layer1(nc, ins, signals, weights, x, avg2, stacks):
    with Memory(nc, "L1") as m:
        w_in, cw, w_z, w_dt, w_out, w_out2, ident, center, ones, quarter, vec = weights.named(
            "w_in conv_w w_z w_dt w_out w_out2 ident center ones quarter l1_vec")
        w_tap, w_cen, w_g = m.sb("w_tap", [P, 6, DI + 32]), m.sb("w_cen", [P, C]), m.sb("w_g", [P, C])
        a_exp, b_out = m.sb("a_exp", [P, 1]), m.sb("b_out", [P, 1])
        xpad, stack = m.sb("xpad", [P, NP, HP * WP]), m.sb("stack", [P, B, HP * WP])
        xs, zs, bc = m.sb("xs", [P, 4, N]), m.sb("zs", [P, 4, N]), m.sb("bc", [P, NQ, N])
        b_t, bt_all, da_t, v = m.sb("b_t", [P, 2, 4, 32]), m.sb("bt_all", [P, NQ, 2, 4, DS1]), m.sb("da_t", [P, NQ, 2, 4, NH1]), m.sb("v", [P, 2, 4, DI])
        kv, y, sq = m.sb("kv", [P, 4, DI]), m.sb("y", [P, 4, N]), m.sb("sq", [P, 4, N])
        dt, dt_e, da = zs, y, sq
        o, var, sd = m.sb("o", [P, 2, N]), m.sb("var", [P, 2, N]), m.sb("sd", [P, 2, N])
        xs_ps, z_ps, bc_ps = m.ps("xs_ps", [P, 4, N]), m.ps("z_ps", [P, 4, N]), m.ps("bc_ps", [P, NP])
        t_ps, k_ps = m.ps("t_ps", [P, 2, 4, DI]), m.ps("k_ps", [P, 2, N])
        gn = GroupNorm(m, signals, "gn", avg2, k_ps[:, 0, 0:NP], bc_ps[:], of_x=2)
        t_y = t_ps[:, :, :, :].rearrange("p h j d -> p (h j d)").rearrange("p (j n) -> p j n", n=N)

        (own, edge_ready, xpad_ready, tap_ready, g_ready, cen_ps, cen_ready, dt_ps, dt_v, dt_exp, dt_ln, act_own, da_tps, bc_conv, bc_ready) = m.sems(
            "own edge_ready xpad_ready tap_ready g_ready cen_ps cen_ready dt_ps dt_v dt_exp dt_ln act_own da_tps bc_conv bc_ready")
        stack_in = m.sems("stack_in0 stack_in1 stack_in2 stack_in3")
        (conv_ready, acts_ready, bt_ready, xt_ready, bt_copied, v_ready, kv_ps, kv_ready, y_ps, y_own, y_ready, cen_y, sq_ready, o_ready,
         var_ready, o_copied) = m.sems(
            "conv_ready acts_ready bt_ready xt_ready bt_copied v_ready kv_ps kv_ready y_ps y_own y_ready cen_y sq_ready o_ready var_ready o_copied")
        added, scaled, sd_ready = m.sems("added scaled sd_ready")

        with nc.Block() as block:
            @block.sync
            def _(sp):
                sp.wait_ge(edge_ready, 3)
                send_stack(sp, xpad_ready, stack_in, xpad, stack)

            @block.gpsimd
            def _(pool):
                pad_stack(pool, edge_ready, xpad, stack)
                pool.wait_ge(edge_ready, 2)
                pool.memset(cw[C:P, 3:6, :], 0.0).then_inc(edge_ready, 1)
                pool.wait_ge(edge_ready, 3)
                pool.memset(b_t[:], 0.0).then_inc(edge_ready, 1)
                stacks.fill(pool)

            @block.vector
            def _(dve):
                gn.vector(dve)
                dve.wait_ge(edge_ready, 4)
                for p in range(NP):
                    dst = xpad[:, p, :].rearrange("p (r c) -> p r c", c=WP)[:, 1:1 + H, 1:1 + W]
                    dve.tensor_scalar(dst, x[:, p, :].rearrange("p (r c) -> p r c", c=W), gn.scale[:, p:p + 1], gn.shift[:, p:p + 1],
                                      ALU.mult, ALU.add).then_inc(xpad_ready, 1)
                weights.wait(dve, 1)
                dve.tensor_tensor(w_tap[:], cw[:], w_in[:, :].unsqueeze(1).broadcast_to([P, 6, DI + 32]), ALU.mult).then_inc(tap_ready, 1)
                dve.tensor_scalar(w_g[:], w_out[:], vec[:, 3:4], None, ALU.mult).then_inc(g_ready, 1)
                dve.wait_ge(cen_ps, 2)
                dve.tensor_copy(w_cen[:], k_ps[:, 0, 0:C]).then_inc(cen_ready, 1)
                dve.tensor_copy(b_out[:], k_ps[:, 0, C:C + 1]).then_inc(cen_ready, 1)
                step = Steps(dve, own)
                dve.wait_ge(dt_ps, 16)
                step(dve.tensor_scalar(dt[:], t_y, vec[:, 5:6], None, ALU.add))
                step(dve.scalar_tensor_tensor(out=dt_e[:], in0=dt[:], scalar=-1.0, in1=dt[:], op0=ALU.mult, op1=ALU.min))
                dve.sem_inc(dt_v, 1)
                dve.wait_ge(dt_ln, 1)
                step(dve.scalar_tensor_tensor(out=da[:], in0=dt[:], scalar=0.0, in1=da[:], op0=ALU.max, op1=ALU.add))
                step(dve.tensor_scalar(da[:], da[:], a_exp[:], None, ALU.mult))
                dve.sem_inc(dt_v, 1)
                dve.wait_ge(da_tps, 1)
                step(dve.tensor_copy(da_t[:].rearrange("p q h j k -> p (q h j) k"), t_ps[:].rearrange("p a j (e k) -> p (a j e) k", k=32)[:, :, 0:NH1]))
                dve.wait_ge(bt_ready, 1)
                step(dve.tensor_copy(bt_all[:].rearrange("p q h j k -> p (q h j) k"),
                                     z_ps[:].rearrange("p q (h j k) -> p (q h j) k", h=2, k=32)[:, :, 0:DS1]))
                dve.sem_inc(y_ready, 2)
                dve.sem_inc(o_copied, 2)
                def over_deviation(q):
                    dve.wait_ge(sd_ready, q + 1)
                    dve.reciprocal(sd[:], sd[:]).then_inc(scaled, 1)
                    dve.wait_ge(scaled, 2 * q + 1)
                    dve.tensor_tensor(sd[:], o[:], sd[:], ALU.mult).then_inc(scaled, 1)
                    dve.wait_ge(scaled, 2 * q + 2)

                def add(q):
                    x_quad = x[:, ds(2 * q, 2), :]
                    dve.scalar_tensor_tensor(out=x_quad, in0=sd[:], scalar=b_out[:], in1=x_quad, op0=ALU.add, op1=ALU.add).then_inc(added, 1)
                    dve.wait_ge(added, q + 1)
                    for h in range(2):
                        dve.bn_stats(signals.x_bn[:, ds(2 * q + h, 1), :].rearrange("p i s -> p (i s)"),
                                     x[:, ds(2 * q + h, 1), :].rearrange("p i s -> p (i s)")).then_inc(signals.x_stats, 1)

                def quad(q, first=False, last=False):
                    dve.tensor_copy(b_t[:, :, :, DS1:2 * DS1].rearrange("p h j k -> p (h j) k"),
                                    bt_all[:, ds(q, 1)].rearrange("p q h j k -> p (q h j) k")).then_inc(bt_copied, 1)
                    dve.wait_ge(xt_ready, q + 1)
                    for h in range(2):
                        dve.tensor_tensor(v[:, h].rearrange("p j (h d) -> p (j h) d", d=HD1),
                                          t_ps[:, h].rearrange("p j (h d) -> p (j h) d", d=HD1),
                                          da_t[:, ds(q, 1), h].rearrange("p q j h -> p (q j h)").unsqueeze(2).broadcast_to([P, 4 * NH1, HD1]),
                                          ALU.mult).then_inc(v_ready, 1)
                    dve.wait_ge(kv_ps, q + 1)
                    dve.tensor_tensor(kv[:], k_ps[:, 0, 0:DI].unsqueeze(1).broadcast_to([P, 4, DI]),
                                      quarter[:, :].unsqueeze(2).broadcast_to([P, 4, DI]), ALU.mult).then_inc(kv_ready, 1)
                    dve.wait_ge(y_ps, q + 1)
                    for h in range(2):
                        dve.scalar_tensor_tensor(out=y[:, 2 * h:2 * h + 2, :], in0=xs[:, 2 * h:2 * h + 2, :], scalar=vec[:, 2:3],
                                                 in1=t_y[:, 2 * h:2 * h + 2, :], op0=ALU.mult, op1=ALU.add).then_inc(y_own, 1)
                    dve.wait_ge(acts_ready, 2 * q + 2)
                    for h in range(2):
                        dve.wait_ge(y_own, 2 * q + 1 + h)
                        dve.tensor_tensor(y[:, 2 * h:2 * h + 2, :], y[:, 2 * h:2 * h + 2, :], zs[:, 2 * h:2 * h + 2, :],
                                          ALU.mult).then_inc(y_ready, 1)
                    if not first:
                        over_deviation(q - 1)
                    dve.wait_ge(o_ready, q + 1)
                    dve.tensor_copy(o[:], k_ps[:]).then_inc(o_copied, 1)
                    if not first and not last:
                        add(q - 1)
                    dve.wait_ge(var_ready, q + 1)
                    dve.tensor_scalar(var[:], t_y[:, 0:2, :], EPS, None, ALU.add).then_inc(o_copied, 1)
                    if last:
                        add(q - 1)

                quad(0, first=True)
                with dve.Fori(1, NQ - 1) as q:
                    quad(q)
                quad(NQ - 1, last=True)
                over_deviation(NQ - 1)
                add(NQ - 1)

            @block.scalar
            def _(act):
                gn.scalar(act)
                weights.wait(act, 1)
                act.activation(a_exp[:], vec[:, 6:7], ACT.Exp).then_inc(act_own, 1)
                act.wait_ge(dt_v, 1)
                act.activation(dt_e[:], dt_e[:], ACT.Exp).then_inc(dt_exp, 1)
                act.wait_ge(dt_exp, 1)
                act.wait_ge(act_own, 1)
                act.activation(da[:], dt_e[:], ACT.Ln, bias=1.0).then_inc(dt_ln, 1)
                act.wait_ge(bc_conv, 1)
                act.activation(bc[:], z_ps[:], ACT.Silu, bias=vec[:, 1:2]).then_inc(bc_ready, 1)

                def deviation(q):
                    act.wait_ge(o_copied, 2 * q + 4)
                    act.activation(sd[:], var[:], ACT.Sqrt).then_inc(sd_ready, 1)

                def quad(q, first):
                    act.wait_ge(conv_ready, 2 * q + 1)
                    act.wait_ge(y_ready, 2 * q + 2)
                    act.activation(xs[:], xs_ps[:], ACT.Silu, bias=vec[:, 0:1]).then_inc(acts_ready, 1)
                    act.wait_ge(conv_ready, 2 * q + 2)
                    act.activation(zs[:], z_ps[:], ACT.Silu).then_inc(acts_ready, 1)
                    if not first:
                        deviation(q - 1)
                    act.wait_ge(cen_y, q + 1)
                    act.activation(sq[:], t_y, ACT.Square).then_inc(sq_ready, 1)

                quad(0, True)
                with act.Fori(1, NQ) as q:
                    quad(q, False)
                act.wait_ge(added, NQ - 1)
                deviation(NQ - 1)

            @block.tensor
            def _(pe):
                gn.tensor(pe)
                weights.wait(pe, 1)
                pe.wait_ge(g_ready, 1)
                pe.matmul(k_ps[:, 0, 0:C], center[:], w_g[:], start=True, stop=True).then_inc(cen_ps, 1)
                pe.matmul(k_ps[:, 0, C:C + 1], w_out2[:], vec[:, 4:5], start=True, stop=True).then_inc(cen_ps, 1)

                def conv_xs(q, start, stop):
                    for k in range(start, stop):
                        h, g = divmod(k, 6)
                        mm = pe.matmul(xs_ps[:, 2 * h:2 * h + 2, :], w_tap[:, g, 0:DI], tap(stack, 4 * q + 2 * h, g, 2),
                                       start=(g == 0), stop=(g == 5))
                    if stop == 12:
                        mm.then_inc(conv_ready, 1)

                def conv_bc(q):
                    for g in range(6):
                        for j in range(4):
                            mm = pe.matmul(z_ps[32 * j:32 * j + 32, q, :], w_tap[:, g, DI:DI + 32], tap(stack, 4 * q + j, g),
                                           start=(g == 0), stop=(g == 5))
                    return mm

                def proj_z(q):
                    for h in range(2):
                        mm = pe.matmul(z_ps[:, 2 * h:2 * h + 2, :], w_z[:], image(stack, 4 * q + 2 * h, 2)[:, :, 1:1 + H, 1:1 + W],
                                       start=True, stop=True)
                    mm.then_inc(conv_ready, 1)

                def quad(q, more):
                    pe.wait_ge(o_copied, 2 * q + 2)
                    pe.wait_ge(acts_ready, 2 * q + 1)
                    for h in range(2):
                        for j in range(4):
                            mm = pe.transpose(t_ps[:, h, j, :], xs[:, j, h * P:(h + 1) * P], ident[:])
                    mm.then_inc(xt_ready, 1)
                    if more:
                        conv_xs(q + 1, 0, 3)
                    pe.wait_ge(bt_copied, q + 1)
                    pe.wait_ge(v_ready, 2 * q + 2)
                    for h in range(2):
                        for j in range(4):
                            mm = pe.matmul(k_ps[32 * j:32 * j + 32, 0, 0:DI], b_t[:, h, j, :], v[:, h, j, :], start=(h == 0), stop=(h == 1))
                    mm.then_inc(kv_ps, 1)
                    if more:
                        conv_xs(q + 1, 3, 5)
                    pe.wait_ge(kv_ready, q + 1)
                    for j in range(4):
                        mm = pe.matmul(t_y[:, j, :], kv[:, j, :], bc[:, ds(q, 1), :], start=True, stop=True)
                    mm.then_inc(y_ps, 1)
                    if more:
                        conv_xs(q + 1, 5, 9)
                    pe.wait_ge(y_ready, 2 * q + 4)
                    for h in range(2):
                        mm = pe.matmul(t_y[:, 2 * h:2 * h + 2, :], center[:], y[:, 2 * h:2 * h + 2, :], start=True, stop=True)
                    mm.then_inc(cen_y, 1)
                    for j in range(4):
                        mm = pe.matmul(k_ps[C * (j % 2):C * (j % 2) + C, j // 2, :], w_cen[:], y[:, j, :], start=True, stop=True)
                    mm.then_inc(o_ready, 1)
                    if more:
                        conv_xs(q + 1, 9, 12)
                    pe.wait_ge(sq_ready, q + 1)
                    for j in range(4):
                        mm = pe.matmul(t_y[C * (j % 2):C * (j % 2) + C, j // 2, :], ones[:], sq[:, j, :], start=True, stop=True)
                    mm.then_inc(var_ready, 1)
                    if more:
                        pe.wait_ge(acts_ready, 2 * q + 2)
                        proj_z(q + 1)

                for g in range(NQ):
                    pe.wait_ge(stack_in[g], 64)
                    for j in range(4):
                        pe.matmul(t_y[32 * j:32 * j + 32, g, :], w_dt[:], image(stack, 4 * g + j)[:, 0, 1:1 + H, 1:1 + W],
                                  start=True, stop=True).then_inc(dt_ps, 1)
                    if g == 0:
                        pe.wait_ge(tap_ready, 1)
                    mm = conv_bc(g)
                mm.then_inc(bc_conv, 1)
                conv_xs(0, 0, 12)
                pe.wait_ge(dt_v, 2)
                for g in range(NQ):
                    for h in range(2):
                        mm = pe.transpose(t_ps[:, g // 2, 2 * (g % 2) + h, :], da[:, g, h * P:(h + 1) * P], ident[:])
                mm.then_inc(da_tps, 1)
                pe.wait_ge(cen_ready, 2)
                pe.wait_ge(bc_ready, 1)
                for g in range(NQ):
                    for h in range(2):
                        mm = pe.transpose(z_ps[:, g, h * P:(h + 1) * P], bc[:, g, h * P:(h + 1) * P], ident[:])
                mm.then_inc(bt_ready, 1)
                pe.wait_ge(y_ready, 2)
                proj_z(0)
                with pe.Fori(0, NQ - 1) as q:
                    quad(q, True)
                quad(NQ - 1, False)


def layer2(nc, ins, signals, weights, x, avg2, stacks):
    TOP = 48
    with Memory(nc, "L2") as m:
        w_q, w_k, w_v, ident, w_o, b_v, vec = weights.named("w_q w_k w_v ident w_o b_v l2_vec")
        xn = m.sb("xn", [P, NP, N])
        parts = m.sb("parts", [P, 4, 2, 3, 2 * N], BF16)
        k_st, q_st = stacks.k_st, stacks.q_st
        v_all, v_x = m.sb("v_all", [P, NP, 2, 2, C]), m.sb("v_x", [P, 2, 2, NH2, 32])
        e = m.sb("e", [P, 8, 2 * N])
        full, rest = (e[:, 4 * k:4 * k + 4].rearrange("p (g s) n -> p g s n", s=2) for k in range(2))
        mx, m_parts = m.sb("mx", [P, 2, 2, 8]), m.sb("m_parts", [8, 2, 2, N], BF16)
        ctx, ctx_r, ctx_n, ctx_c = m.sb("ctx", [P, 2, 2, N]), m.sb("ctx_r", [P, 16]), m.sb("ctx_n", [P, 2, 2, 4 * HD2]), m.sb("ctx_c", [P, P])
        ring, ctx_ps, a_ps, m_ps = m.ps("ring", [P, 4, 2 * N]), m.ps("ctx_ps", [P, 2, 2 * N]), m.ps("a_ps", [P, 2 * N]), m.ps("m_ps", [P, 2 * N])
        k_bank = lambda g: [ctx_ps[:, 0], ctx_ps[:, 1], a_ps[:], m_ps[:]][g]
        gn = GroupNorm(m, signals, "gn", avg2, a_ps[:, 0:NP], m_ps[:, 0:NP], of_x=3)
        scratch = [nc.dram_tensor(f"L2_{n}_parts", (NQ, 3, 2, HD2, 4, 2, 2 * N), BF16, kind="Internal").ap() for n in "qk"]

        (own, xn_ready, q_ps_ready, k_ps_ready, full_ready, hi_ready, mid_ready, parts_ready, v_ps_ready, v_all_ready,
         pool_own) = m.sems("own xn_ready q_ps_ready k_ps_ready full_ready hi_ready mid_ready parts_ready v_ps_ready v_all_ready pool_own")
        stored = m.sems(" ".join(f"stored_{s}{g}" for g in range(NQ) for s in "qk"))
        stacked = m.sem("stacked")
        (max_ps, max_read, mx_turned, m_ready, m_stacked, s_ready, e_ready, ev_done, ctx_ready, ctx_turned, ctx_normed, ctx_back,
         ctx_copied, o_ready, o_added, v_x_ready, norm_own, passed) = m.sems(
            "max_ps max_read mx_turned m_ready m_stacked s_ready e_ready ev_done ctx_ready ctx_turned ctx_normed ctx_back "
            "ctx_copied o_ready o_added v_x_ready norm_own passed")

        with nc.Block() as block:
            @block.sync
            def _(sp):
                sp.sem_inc(m_stacked, 128)

                def store_parts(g):
                    for s in range(2):
                        sp.wait_ge(parts_ready, 2 * g + s + 1)
                        for b in range(2):
                            dst = scratch[s][g].rearrange("t e d p b n -> b (e d p) t n")[b]
                            sp.dma_start(dst, parts[C * b:C * b + C, g, s]).then_inc(stored[2 * g + s], 16)

                def load_stacks(g, s):
                    if s == 0:
                        sp.wait_ge(stacks.filled, 2 * g + 2)
                        if g:
                            sp.wait_ge(stacked, 12 * 16 * g)
                    sp.wait_ge(stored[2 * g + s], 32)
                    for h in range(2):
                        for slot, part, count in ((0, 0, 3), (3, 1, 2), (5, 2, 1)):
                            rows = slice(64 * h + HD2 * slot, 64 * h + HD2 * (slot + count))
                            if s == 0:
                                src = scratch[0][g, part, h].rearrange("d p b n -> d (p b n)").unsqueeze(0).broadcast_to([count, HD2, 4 * 4 * N])
                                dst = q_st[rows, h, g]
                            else:
                                src = scratch[1][g, 0:count, h].rearrange("t d p b n -> t d (p b n)")
                                dst = k_st[rows, g]
                            sp.dma_start(dst.rearrange("r p b n s -> r (p b n s)"), src).then_inc(stacked, 16)

                def send_maxima(i, j):
                    n, b = 4 * i + j, j % 2
                    sp.wait_ge(m_ready, 2 * n + 2)
                    sp.sem_inc(passed, 1)
                    for h in range(2):
                        for t in range(2):
                            dst = q_st[64 * h + TOP + t:64 * h + TOP + t + 1, h, ds(i, 1), :, b, j // 2, :].rearrange("t i p s -> t (i p) s")
                            sp.dma_start(dst, m_parts[4 * h:4 * h + 4, b, t, :]).then_inc(m_stacked, 16)
                    sp.wait_ge(m_stacked, 64 * n + 192)
                    sp.sem_inc(passed, 1)

                store_parts(0)
                load_stacks(0, 0)
                load_stacks(0, 1)
                store_parts(1)
                load_stacks(1, 0)
                load_stacks(1, 1)
                store_parts(2)
                send_maxima(0, 0)
                store_parts(3)
                send_maxima(0, 1)
                load_stacks(2, 0)
                load_stacks(2, 1)
                send_maxima(0, 2)
                load_stacks(3, 0)
                send_maxima(0, 3)
                load_stacks(3, 1)
                with sp.Fori(1, NQ) as i:
                    for j in range(4):
                        send_maxima(i, j)

            @block.gpsimd
            def _(pool):
                pool.memset(v_x[:], 0.0).then_inc(pool_own, 1)
                pool.wait_ge(pool_own, 1)
                pool.memset(v_x[:, :, :, :, HD2:HD2 + 1], 1.0).then_inc(pool_own, 1)
                for g in range(NQ):
                    for s in range(2):
                        pool.wait_ge(mid_ready, 2 * g + s + 1)
                        pool.tensor_tensor(parts[:, g, s, 2], rest[:, g % 2, s], parts[:, g, s, 1], ALU.subtract).then_inc(parts_ready, 1)
                pool.wait_ge(pool_own, 2)
                pool.wait_ge(v_all_ready, 2)
                with pool.Fori(0, NP) as i:
                    for b in range(2):
                        n = 2 * i + b
                        pool.wait_ge(ev_done, 2 * n + 2)
                        pool.tensor_copy(v_x[:, b, :, :, 0:HD2],
                                         v_all[:, ds(i, 1), :, b, :].rearrange("p i t (h d) -> p (i t) h d", d=HD2)).then_inc(v_x_ready, 1)

            @block.vector
            def _(dve):
                gn.vector(dve)
                for p in range(NP):
                    dve.tensor_scalar(xn[:, p, :], x[:, p, :], gn.scale[:, p:p + 1], gn.shift[:, p:p + 1],
                                      ALU.mult, ALU.add).then_inc(xn_ready, 1)
                step = Steps(dve, own)
                for g in range(NQ):
                    for s in range(2):
                        dve.wait_ge(hi_ready, 2 * g + s + 1)
                        if g > 1:
                            dve.wait_ge(parts_ready, 2 * g + s - 3)
                        step(dve.tensor_tensor(rest[:, g % 2, s], full[:, g % 2, s], parts[:, g, s, 0], ALU.subtract))
                        dve.tensor_copy(parts[:, g, s, 1], rest[:, g % 2, s]).then_inc(mid_ready, 1)
                for h in range(2):
                    dve.wait_ge(v_ps_ready, h + 1)
                    dve.tensor_tensor(v_all[:, 4 * h:4 * h + 4].rearrange("p n t e c -> p (n t) (e c)"),
                                      ring[:, 2 * h:2 * h + 2].rearrange("p a (t c) -> p (a t) c", c=P),
                                      b_v[:, :].unsqueeze(1).broadcast_to([P, 8, P]), ALU.add).then_inc(v_all_ready, 1)
                dve.sem_inc(max_read, 2)
                dve.sem_inc(o_added, 1)

                def largest(n, b, k):
                    if k == 0:
                        dve.wait_ge(mx_turned, n + 1)
                    dve.wait_ge(max_ps, 8 * n + k + 1)
                    head = 4 * (k % 2) + k // 2
                    dve.tensor_reduce(mx[:, b, :, head], ring[:, k % 2].rearrange("p (q s) -> p q s", q=2), AX.X, ALU.max).then_inc(max_read, 1)

                def split_max(n, b):
                    dve.wait_ge(mx_turned, n + 3)
                    dve.wait_ge(m_stacked, 64 * n + 64)
                    dve.tensor_scalar(m_parts[:, b, 0], m_ps[0:8, 0:N], -1.0, None, ALU.mult).then_inc(m_ready, 1)
                    dve.wait_ge(m_ready, 2 * n + 1)
                    dve.scalar_tensor_tensor(out=m_parts[:, b, 1], in0=m_ps[0:8, 0:N], scalar=-1.0, in1=m_parts[:, b, 0],
                                             op0=ALU.mult, op1=ALU.subtract).then_inc(m_ready, 1)

                def normalize(n):
                    dve.wait_ge(ctx_turned, n + 3)
                    cols = a_ps[:, :].rearrange("p (g q j k) -> p (g q) j k", g=2, q=2, j=4)
                    dve.reciprocal(ctx_r[:].rearrange("p (a j) -> p a j", j=4), cols[:, :, :, HD2]).then_inc(norm_own, 1)
                    dve.wait_ge(norm_own, n + 1)
                    for q in range(2):
                        dve.tensor_tensor(ctx_n[:, q].rearrange("p g (j d) -> p g j d", d=HD2), cols[:, q::2, :, 0:HD2],
                                                 ctx_r[:].rearrange("p (g q j) -> p g q j", g=2, q=2)[:, :, q, :].unsqueeze(3).broadcast_to([P, 2, 4, HD2]),
                                                 ALU.mult).then_inc(ctx_normed, 1)

                def take_back(n):
                    dve.wait_ge(ctx_back, n + 1)
                    dve.tensor_copy(ctx_c[:], a_ps[:, 0:P]).then_inc(ctx_copied, 1)

                def add(n, i, b):
                    half = slice(C * b, C * b + C)
                    dve.wait_ge(o_ready, n + 1)
                    dve.scalar_tensor_tensor(out=x[half, ds(i, 1), :], in0=a_ps[half, N:2 * N], scalar=vec[half, 2:3], in1=x[half, ds(i, 1), :],
                                             op0=ALU.add, op1=ALU.add).then_inc(o_added, 1)
                    if b == 1:
                        dve.wait_ge(o_added, n + 2)
                        dve.bn_stats(signals.x_bn[:, ds(i, 1), :].rearrange("p i s -> p (i s)"), x[:, ds(i, 1), :].rearrange("p i s -> p (i s)")).then_inc(signals.x_stats, 1)

                def turn(g, j, A, S, D):
                    n, i, b = 4 * g + j, 2 * g + j // 2, j % 2
                    for k in range(8):
                        if A:
                            largest(n, b, k)
                        if k == 1 and S:
                            split_max(n - 1, 1 - b)
                        if k == 3 and D:
                            normalize(n - 3)
                        if k == 5 and D:
                            take_back(n - 3)
                        if k == 7 and D:
                            add(n - 3, i - 2 + b, 1 - b)

                turns(dve, turn)

            @block.scalar
            def _(act):
                gn.scalar(act)
                weights.wait(act, 2)
                for g in range(NQ):
                    for s, src, ready in ((0, ring[:, g], q_ps_ready), (1, k_bank(g), k_ps_ready)):
                        act.wait_ge(ready, g + 1)
                        if g > 1:
                            act.wait_ge(mid_ready, 2 * g + s - 3)
                        act.activation(full[:, g % 2, s], src, ACT.Identity, bias=vec[:, s:s + 1]).then_inc(full_ready, 1)
                        act.wait_ge(full_ready, 2 * g + s + 1)
                        act.activation(parts[:, g, s, 0], src, ACT.Identity, bias=vec[:, s:s + 1]).then_inc(hi_ready, 1)
                act.wait_ge(parts_ready, 2 * NQ)
                act.sem_inc(e_ready, 2)
                act.sem_inc(ctx_ready, 2)

                def turn(g, j, A, S, D):
                    n, b = 4 * g + j, j % 2
                    c = n - 2
                    for k in range(8):
                        if A:
                            act.wait_ge(s_ready, 8 * c + k + 1)
                            if k in (0, 4):
                                act.wait_ge(ev_done, 2 * c + 3 + k // 4)
                            act.activation(e[:, k], ring[:, 2 + k % 2], ACT.Exp, scale=HD2 ** -0.5).then_inc(e_ready, 1)
                        if k == 1 and D:
                            act.wait_ge(ev_done, 2 * (c - 1) + 6)
                            act.wait_ge(ctx_turned, c)
                            act.activation(ctx[:, 1 - b], ctx_ps[:, 1 - b], ACT.Copy).then_inc(ctx_ready, 1)

                turns(act, turn, lag=2)

            @block.tensor
            def _(pe):
                gn.tensor(pe)
                weights.wait(pe, 2)
                for g in range(NQ):
                    pe.wait_ge(xn_ready, 2 * g + 2)
                    pe.matmul(ring[:, g], w_q[:], xn[:, 2 * g:2 * g + 2, :], start=True, stop=True).then_inc(q_ps_ready, 1)
                    pe.matmul(k_bank(g), w_k[:], xn[:, 2 * g:2 * g + 2, :], start=True, stop=True).then_inc(k_ps_ready, 1)
                for h in range(2):
                    pe.wait_ge(hi_ready, 4 * h + 4)
                    for p in range(4 * h, 4 * h + 4):
                        for t in range(2):
                            mm = pe.matmul(ring[:, p // 2, (2 * (p % 2) + t) * P:(2 * (p % 2) + t + 1) * P], xn[:, p, t * P:(t + 1) * P], w_v[:],
                                           start=True, stop=True)
                    mm.then_inc(v_ps_ready, 1)
                pe.sem_inc(mx_turned, 2)
                pe.sem_inc(ev_done, 4)
                pe.sem_inc(ctx_turned, 2)
                pe.wait_ge(v_all_ready, 2)
                pe.wait_ge(hi_ready, 2 * NQ)

                def largest(n, k, at):
                    h, p = k % 2, k // 2
                    g, j = at
                    pe.wait_ge(max_read, 8 * n + k + 1)
                    for q in range(2):
                        mm = pe.matmul(ring[:, k % 2, q * N:(q + 1) * N], q_st[:, h, ds(g, 1), p, j % 2, j // 2, q * P:(q + 1) * P], k_st[:, ds(g, 1), p, j % 2, j // 2, :],
                                       start=True, stop=True)
                    mm.then_inc(max_ps, 1)

                def scores(c, k, at):
                    p, t = k // 2, k % 2
                    g, j = at
                    if k == 0:
                        pe.wait_ge(m_stacked, 64 * c + 192)
                    pe.wait_ge(e_ready, 8 * c + k + 1)
                    pe.matmul(ring[:, 2 + k % 2], k_st[:, ds(g, 1), p, j % 2, j // 2, t * P:(t + 1) * P], q_st[:, :, ds(g, 1), p, j % 2, j // 2, :],
                              start=True, stop=True).then_inc(s_ready, 1)

                def context(c, b, g):
                    pe.wait_ge(e_ready, 8 * c + 4 * g + 6)
                    pe.wait_ge(v_x_ready, c + 1)
                    pe.wait_ge(ctx_ready, c + 1)
                    for t in range(2):
                        for j in range(4):
                            mm = pe.matmul(ctx_ps[32 * j:32 * j + 32, b, g * N:(g + 1) * N], v_x[:, b, t, 4 * g + j, :],
                                           e[:, 4 * g + 2 * (j // 2) + t, (j % 2) * N:(j % 2 + 1) * N], start=(t == 0), stop=(t == 1))
                    mm.then_inc(ev_done, 1)

                def turn(g, j, A, S, D):
                    n, b = 4 * g + j, j % 2
                    if j == 0 and A:
                        pe.wait_ge(stacked, 12 * 16 * (g + 1))
                    scored = from_turn(n, 2) and not (isinstance(n, int) and n >= B + 2)
                    for k in range(8):
                        if A:
                            largest(n, k, (g, j))
                        if scored:
                            scores(n - 2, k, (g, j - 2) if j >= 2 else (g - 1, j + 2))
                        if k == 0 and S:
                            if from_turn(n, 2):
                                pe.wait_ge(m_ready, 2 * n - 2)
                            pe.wait_ge(max_read, 8 * n + 2)
                            for q in range(2):
                                mm = pe.transpose(m_ps[0:8, q * P:(q + 1) * P], mx[:, 1 - b, q, :], ident[:])
                            mm.then_inc(mx_turned, 1)
                        if k == 1 and D:
                            context(n - 3, 1 - b, 1)
                        if k == 3 and D:
                            pe.wait_ge(ctx_ready, n)
                            pe.wait_ge(o_added, n - 2)
                            for four in range(2):
                                for q in range(2):
                                    mm = pe.transpose(a_ps[:, (2 * four + q) * P:(2 * four + q + 1) * P], ctx[:, 1 - b, four, q * P:(q + 1) * P], ident[:])
                            mm.then_inc(ctx_turned, 1)
                        if k == 5 and D:
                            pe.wait_ge(ctx_normed, 2 * (n - 3) + 2)
                            pe.transpose(a_ps[:, 0:P], ctx_n[:].rearrange("p q g c -> p (q g c)"), ident[:]).then_inc(ctx_back, 1)
                        if k == 5 and scored:
                            context(n - 2, b, 0)
                        if k == 7 and D:
                            pe.wait_ge(ctx_copied, n - 2)
                            half = slice(C * (1 - b), C * (1 - b) + C)
                            for q in range(2):
                                mm = pe.matmul(a_ps[half, N + q * P:N + (q + 1) * P], w_o[:, q, :], ctx_c[:], start=True, stop=True)
                            mm.then_inc(o_ready, 1)

                turns(pe, turn)


def turns(eng, turn, lag=0):
    for n in range(4):
        turn(0, n, n >= lag, n >= 1, n >= 3)
    with eng.Fori(1, NQ) as g:
        for j in range(4):
            turn(g, j, True, True, True)
    for j in range(3):
        turn(NQ, j, j < lag, j == 0, True)


def layer3(nc, ins, signals, weights, x, avg2):
    KK = 9
    TN = KK * N
    TW = 2 * KK * C // 3
    CH = 4
    THIRD = TN // 3
    with Memory(nc, "L3") as m:
        w_off, w_all, sel_f, grid, w_grid, vec = weights.named("w_off w_all sel grid w_grid l3_vec")
        sel = m.sb("sel", [P, 3, P], BF16)
        xpad, stack = m.sb("xpad", [P, NP, HP * WP]), m.sb("stack", [P, B, HP * WP])
        off, sig = m.sb("off", [P, NQ, N]), m.sb("sig", [P, NQ, N])
        hat, mask = m.sb("hat", [P, TN]), m.sb("mask", [C, TN])
        rest, parts = m.sb("rest", [P, 2, THIRD]), m.sb("parts", [P, 3, TN], BF16)
        hats = m.sb("hats", [P, 2, 2, TN], BF16)
        xn, t_sb = m.sb("xn", [P, 2, N]), m.sb("t_sb", [P, 2, 2, 2 * KK * C])
        cols, s = m.sb("cols", [P, 2, 2 * N]), m.sb("s", [P, 2, 2, 2 * N])
        row_ps, col_ps, acc = m.ps("row_ps", [P, 2, 2, 2 * N]), m.ps("col_ps", [P, 2, 2 * N]), m.ps("acc", [P, 2, 2 * N])
        off_ps = lambda g: row_ps[:, g // 2, g % 2, 0:N]
        gn = GroupNorm(m, signals, "gn", avg2, acc[:, 0, 0:NP], acc[:, 1, 0:NP], of_x=4)
        off_dram = nc.dram_tensor("L3_offsets", (B, 3 * KK, N), F32, kind="Internal").ap()

        (edge_ready, xpad_ready, sel_ready, off_conv, off_ready, off_stored, dist_ready, hat_ready, masked, hi_ready,
         rest_ready, mid_ready, parts_ready, mask_stored) = m.sems(
            "edge_ready xpad_ready sel_ready off_conv off_ready off_stored dist_ready hat_ready masked hi_ready "
            "rest_ready mid_ready parts_ready mask_stored")
        stack_in = m.sems("stack_in0 stack_in1 stack_in2 stack_in3")
        hat_in, mask_in = m.sems("hat_in0 hat_in1 hat_in2"), m.sems("mask_in0 mask_in1 mask_in2")
        (hats_in, xn_ready, row_ready, col_ready, col_read, s_ready, s_used, added, passed) = m.sems(
            "hats_in xn_ready row_ready col_ready col_read s_ready s_used added passed")

        def hat_split(eng):
            def weigh_hat(c, j):
                cut = slice(THIRD * j, THIRD * j + THIRD)
                eng.wait_ge(hat_ready, 3 * c + j + 1)
                eng.wait_ge(mask_in[j], 16 * c + 16)
                eng.tensor_tensor(hat[0:C, cut], hat[0:C, cut], mask[:, cut], ALU.mult).then_inc(masked, 1)

            def take_rest(c, j):
                cut = slice(THIRD * j, THIRD * j + THIRD)
                if from_turn(3 * c + j, 2):
                    eng.wait_ge(parts_ready, 3 * c + j - 1)
                eng.wait_ge(hi_ready, 3 * c + j + 1)
                eng.tensor_tensor(rest[:, j % 2], hat[:, cut], parts[:, 0, cut], ALU.subtract).then_inc(rest_ready, 1)

            def take_last(c, j):
                cut = slice(THIRD * j, THIRD * j + THIRD)
                eng.wait_ge(mid_ready, 3 * c + j + 1)
                eng.tensor_tensor(parts[:, 2, cut], rest[:, j % 2], parts[:, 1, cut], ALU.subtract).then_inc(parts_ready, 1)

            return ((weigh_hat, 0), (weigh_hat, 1), (take_rest, 0), (weigh_hat, 2), (take_rest, 1), (take_last, 0),
                    (take_rest, 2), (take_last, 1), (take_last, 2))

        with nc.Block() as block:
            @block.sync
            def _(sp):
                sp.wait_ge(edge_ready, 2)
                send_stack(sp, xpad_ready, stack_in, xpad, stack)

                by_place = off_dram.rearrange("(g j) r n -> j r g n", j=4)

                def store_offsets(quads):
                    for j in range(4):
                        sp.dma_start(by_place[j, 0:2 * KK, quads], off[32 * j:32 * j + 2 * KK, quads]).then_inc(off_stored, 16)

                def store_masks(quads):
                    for j in range(4):
                        sp.dma_start(by_place[j, 2 * KK:, quads], sig[32 * j + 2 * KK:32 * j + 3 * KK, quads]).then_inc(mask_stored, 16)

                def load_positions(c, j):
                    taps = slice(KK * j // 3, KK * (j + 1) // 3)
                    for k in range(2):
                        src = off_dram[ds(CH * c, CH), KK * k:KK * k + KK][:, taps].rearrange("u r n -> u (r n)").unsqueeze(1).broadcast_to([CH, H, THIRD])
                        sp.dma_start(hat[C * k:C * k + C, THIRD * j:THIRD * j + THIRD], src).then_inc(hat_in[j], 16)

                def load_masks(c, j):
                    taps = slice(KK * j // 3, KK * (j + 1) // 3)
                    src = off_dram[ds(CH * c, CH), 2 * KK:][:, taps].rearrange("u r n -> u (r n)").unsqueeze(1).broadcast_to([CH, H, THIRD])
                    sp.dma_start(mask[:, THIRD * j:THIRD * j + THIRD], src).then_inc(mask_in[j], 16)

                def send_hats(n, b):
                    for k in range(2):
                        for e in range(2):
                            four = C * k + H * (2 * b + e)
                            sp.dma_start(hats[C * k:C * k + 3 * H, b, e, :], parts[four:four + H]).then_inc(hats_in, 16)
                    sp.wait_ge(hats_in, 64 * n + 64)
                    sp.sem_inc(passed, 1)

                def next_chunk(i, more):
                    sp.wait_ge(parts_ready, 3 * i + 6)
                    for b in range(2):
                        sp.wait_ge(s_used, KK * (2 * i + b) + 11)
                        send_hats(2 * i + 2 + b, b)
                        if more and b == 0:
                            for j in range(3):
                                load_positions(i + 2, j)
                                load_masks(i + 2, j)

                sp.wait_ge(off_ready, 1)
                store_offsets(slice(0, 1))
                sp.wait_ge(off_ready, 2)
                store_masks(slice(0, 1))
                sp.wait_ge(off_stored, 64)
                load_positions(0, 0)
                sp.wait_ge(mask_stored, 64)
                load_masks(0, 0)
                for j in range(1, 3):
                    load_positions(0, j)
                    load_masks(0, j)
                sp.wait_ge(off_ready, 2 * NQ)
                store_offsets(slice(1, NQ))
                store_masks(slice(1, NQ))
                sp.wait_ge(edge_ready, 3)
                sp.wait_ge(parts_ready, 3)
                send_hats(0, 0)
                sp.wait_ge(off_stored, 128)
                sp.wait_ge(mask_stored, 128)
                for j in range(3):
                    load_positions(1, j)
                    load_masks(1, j)
                send_hats(1, 1)
                with sp.Fori(0, B // CH - 2) as i:
                    next_chunk(i, True)
                next_chunk(B // CH - 2, False)

            @block.gpsimd
            def _(pool):
                pad_stack(pool, edge_ready, xpad, stack)
                pool.wait_ge(edge_ready, 2)
                pool.memset(hats[32:64], 0.0).then_inc(edge_ready, 1)
                with pool.Fori(1, B // CH) as c:
                    for hat_step, j in hat_split(pool):
                        hat_step(c, j)

            @block.vector
            def _(dve):
                gn.vector(dve)
                dve.wait_ge(edge_ready, 2)
                for p in range(NP):
                    dst = xpad[:, p, :].rearrange("p (r c) -> p r c", c=WP)[:, 1:1 + H, 1:1 + W]
                    dve.tensor_scalar(dst, x[:, p, :].rearrange("p (r c) -> p r c", c=W), gn.scale[:, p:p + 1], gn.shift[:, p:p + 1],
                                      ALU.mult, ALU.add).then_inc(xpad_ready, 1)
                weights.wait(dve, 3)
                dve.tensor_copy(sel[:], sel_f[:]).then_inc(sel_ready, 1)

                def norm(n, b):
                    dve.tensor_scalar(xn[:, b, :], x[:, ds(n, 1), :], gn.scale[:, ds(n, 1)], gn.shift[:, ds(n, 1)], ALU.mult, ALU.add).then_inc(xn_ready, 1)

                norm(0, 0)
                norm(1, 1)

                for hat_step, j in hat_split(dve):
                    hat_step(0, j)
                dve.sem_inc(s_ready, 2)
                dve.sem_inc(added, 2)

                def sample(n, b, t, c):
                    u, q = KK * n + t, (b + t) % 2
                    dve.wait_ge(row_ready, u + 1)
                    dve.wait_ge(col_read, c + 1)
                    dve.wait_ge(s_used, u + 1)
                    dve.tensor_tensor(s[:, q], row_ps[:, q], cols[:, q:q + 1].broadcast_to([P, 2, 2 * N]), ALU.mult).then_inc(s_ready, 1)

                def pair(n, b, more, _):
                    for t in range(1, KK):
                        sample(n, b, t, 7 + 15 * n + col_step(t - 1, more))
                        if t == 4 and more > 1:
                            dve.wait_ge(col_ready, 15 * n + 6)
                            norm(n + 2, b)
                    if more:
                        sample(n + 1, 1 - b, 0, 7 + 15 * n + col_step(KK - 1, more))
                    dve.wait_ge(s_used, KK * n + KK + 2)
                    dve.scalar_tensor_tensor(out=x[:, ds(n, 1), :], in0=acc[:, b, 0:N], scalar=vec[:, 2:3], in1=x[:, ds(n, 1), :],
                                             op0=ALU.add, op1=ALU.add).then_inc(added, 1)

                sample(0, 0, 0, 6)
                pairs(dve, pair)

            @block.scalar
            def _(act):
                gn.scalar(act)
                weights.wait(act, 3)
                for g in range(NQ):
                    act.wait_ge(off_conv, g + 1)
                    act.activation(off[:, g], off_ps(g), ACT.Identity, bias=vec[:, 0:1]).then_inc(off_ready, 1)
                    act.activation(sig[:, g], off_ps(g), ACT.Sigmoid, bias=vec[:, 0:1]).then_inc(off_ready, 1)

                def make_hat(c, j):
                    cut = slice(THIRD * j, THIRD * j + THIRD)
                    act.wait_ge(hat_in[j], 32 * c + 32)
                    act.activation(hat[:, cut], hat[:, cut], ACT.Abs, bias=vec[:, 1:2]).then_inc(dist_ready, 1)
                    act.wait_ge(dist_ready, 3 * c + j + 1)
                    act.activation(hat[:, cut], hat[:, cut], ACT.Relu, bias=1.0, scale=-1.0).then_inc(hat_ready, 1)

                def take_first(c, j):
                    cut = slice(THIRD * j, THIRD * j + THIRD)
                    act.wait_ge(masked, 3 * c + j + 1)
                    if from_turn(c, 1):
                        act.wait_ge(hats_in, 128 * c)
                    act.activation(parts[:, 0, cut], hat[:, cut], ACT.Copy).then_inc(hi_ready, 1)

                def take_second(c, j):
                    cut = slice(THIRD * j, THIRD * j + THIRD)
                    act.wait_ge(rest_ready, 3 * c + j + 1)
                    act.activation(parts[:, 1, cut], rest[:, j % 2], ACT.Copy).then_inc(mid_ready, 1)

                def take_cols(v, c, q, r):
                    act.wait_ge(col_ready, c + 1)
                    act.wait_ge(s_ready, v + 1)
                    act.activation(cols[:, q], col_ps[:, r], ACT.Copy).then_inc(col_read, 1)

                def take_t(b, c, k, r):
                    act.wait_ge(col_ready, c + 1)
                    act.activation(t_sb[:, b, k // 3, ds(k % 3 * TW, TW)], col_ps[:, r, 0:TW], ACT.Copy).then_inc(col_read, 1)

                for hat_step, j in ((make_hat, 0), (make_hat, 1), (take_first, 0), (make_hat, 2), (take_first, 1), (take_second, 0),
                                    (take_first, 2), (take_second, 1), (take_second, 2)):
                    hat_step(0, j)
                for k in range(6):
                    take_t(0, k, k, k % 2)
                take_cols(0, 6, 0, 0)
                hat_steps = {1: (make_hat, 0), 2: (make_hat, 1), 3: (take_first, 0), 4: (make_hat, 2), 5: (take_first, 1),
                             6: (take_second, 0), 7: (take_first, 2), 8: (take_second, 1), 10: (take_second, 2)}

                def pair(n, b, more, chunk):
                    for t in range(KK):
                        loc = col_step(t, more)
                        c, r = 7 + 15 * n + loc, (1 + b + loc) % 2
                        if t < KK - 1 or more:
                            take_cols(KK * n + t + 1, c, (b + t + 1) % 2, r)
                        if t in WEIGHED and more:
                            if t == 0:
                                act.wait_ge(s_used, KK * n + 2)
                            take_t(1 - b, c + 1, WEIGHED.index(t), 1 - r)
                        if more > 1 and KK * b + t in hat_steps:
                            hat_step, j = hat_steps[KK * b + t]
                            hat_step(chunk, j)

                pairs(act, pair)

            @block.tensor
            def _(pe):
                gn.tensor(pe)
                weights.wait(pe, 3)
                for g in range(NQ):
                    pe.wait_ge(stack_in[g], 64)
                    for k in range(6):
                        for j in range(4):
                            mm = pe.matmul(off_ps(g)[32 * j:32 * j + 32], w_off[:, k, :], tap(stack, 4 * g + j, k), start=(k == 0), stop=False)
                    for j in range(4):
                        mm = pe.matmul(off_ps(g)[32 * j:32 * j + 32], w_grid[:], grid[:], start=False, stop=True)
                    mm.then_inc(off_conv, 1)
                pe.sem_inc(s_used, 2)

                def weigh(b, c, k, r):
                    if from_turn(c, 2):
                        pe.wait_ge(col_read, c - 1)
                    pe.matmul(col_ps[:, r, 0:TW], xn[:, b, k // 3 * P:(k // 3 + 1) * P], w_all[:, k % 3 * TW:(k % 3 + 1) * TW],
                              start=True, stop=True).then_inc(col_ready, 1)

                def spread(v, b, t, c, r):
                    q = (b + t) % 2
                    hat = hats[0:112, b, :, t * N:(t + 1) * N]
                    pe.wait_ge(s_ready, v + 1)
                    for h in range(2):
                        mm = pe.matmul(row_ps[:, q, h], sel[0:112, h], hat, start=True, stop=True)
                    mm.then_inc(row_ready, 1)
                    pe.wait_ge(col_read, c - 1)
                    pe.matmul(col_ps[:, r], sel[0:112, 2], hat, start=True, stop=True).then_inc(col_ready, 1)

                def samples(n, b, t):
                    u, q = KK * n + t, (b + t) % 2
                    pe.wait_ge(s_ready, u + 3)
                    if t == 0:
                        pe.wait_ge(added, n + 1)
                        pe.wait_ge(col_read, 15 * n + 6)
                    for h in range(2):
                        for e in range(2):
                            mm = pe.matmul(acc[C * e:C * e + C, b, 0:N], t_sb[:, b, h, (KK * e + t) * C:(KK * e + t + 1) * C],
                                           s[:, q, h, e * N:(e + 1) * N], start=(t == 0 and h == 0), stop=(t == KK - 1 and h == 1))
                    mm.then_inc(s_used, 1)

                pe.wait_ge(xn_ready, 1)
                for k in range(6):
                    weigh(0, k, k, k % 2)
                pe.wait_ge(off_ready, 2 * NQ)
                pe.wait_ge(sel_ready, 1)
                pe.wait_ge(hats_in, 64)
                spread(0, 0, 0, 6, 0)

                def pair(n, b, more, _):
                    for t in range(KK):
                        loc = col_step(t, more)
                        c, r = 7 + 15 * n + loc, (1 + b + loc) % 2
                        if t < KK - 1:
                            spread(KK * n + t + 1, b, t + 1, c, r)
                        elif more:
                            pe.wait_ge(hats_in, 64 * n + 128)
                            spread(KK * n + KK, 1 - b, 0, c, r)
                        if t in WEIGHED and more:
                            if t == 0:
                                pe.wait_ge(xn_ready, n + 2)
                            weigh(1 - b, c + 1, WEIGHED.index(t), 1 - r)
                        samples(n, b, t)

                pairs(pe, pair)


def col_step(t, more):
    return t + sum(w < t for w in WEIGHED) if more else t


def pairs(eng, pair):
    with eng.Fori(0, NP // 2 - 1) as i:
        for b in range(2):
            pair(2 * i + b, b, 2, i + 1)
    pair(NP - 2, 0, 1, None)
    pair(NP - 1, 1, 0, None)


def program(nc, ins, out, layers=4):
    Memory.semaphores = ExitStack()
    with Memory.semaphores, Memory(nc, "all") as m:
        x, avg2 = m.sb("x", [P, NP, N]), m.sb("avg2", [P, P])
        x_out = m.sem("x_out")
        signals = NormSignals(m)
        weights = Weights(m, ins)
        layer0(nc, ins, signals, weights, x, avg2)
        with Memory(nc, "stacks") as between:
            stacks = Stacks(between)
            if layers > 1:
                layer1(nc, ins, signals, weights, x, avg2, stacks)
            if layers > 2:
                layer2(nc, ins, signals, weights, x, avg2, stacks)
        if layers > 3:
            layer3(nc, ins, signals, weights, x, avg2)
        with nc.Block() as block:
            @block.sync
            def _(sp):
                sp.dma_start(out.rearrange("(n e) c h w -> (e c) n (h w)", e=2), x[:]).then_inc(x_out, 16)
                sp.wait_ge(x_out, 16)


def two_blocks(a):
    r, c = a.shape
    out = np.zeros((2 * r, 2 * c), a.dtype)
    out[:r, :c], out[r:, c:] = a, a
    return out


def lay_out(a):
    f = np.float32
    part = np.arange(P)
    t = {"x": a["x"]}
    t["avg2"] = (part[:, None] // 2 == part[None, :] // 2).astype(f) / f(2)
    t["avg8"] = (part[:, None] // 8 == part[None, :] // 8).astype(f) / f(8)
    t["w_pre"], t["w_post"] = two_blocks(a["L0_conv_pre_w"].T), two_blocks(a["L0_conv_post_w"].T)
    names = ["pre_b", "pre_gn_g", "pre_gn_b", "post_b", "post_gn_g", "post_gn_b"]
    t["l0_vec"] = np.stack([np.tile(a["L0_conv_" + n], 2) for n in names], 1)
    t["w_s1"] = two_blocks(a["L0_conv_sp_w1"])
    t["b_s1"] = np.tile(a["L0_conv_sp_b1"], 2)[:, None]
    t["w_s2"] = np.tile(two_blocks(a["L0_conv_sp_w2"]), (1, G0))
    t["b_s2"] = np.tile(a["L0_conv_sp_b2"], 2 * G0)[:, None]
    group_k, parity_k = part // 32, part // 16 % 2
    group_c, parity_c = part % C // 16, part // C
    t["same_group"] = ((group_k[:, None] == group_c) & (parity_k[:, None] == parity_c)).astype(f)
    kinds = ["alpha", "mu", "sigma", "mix", "gate"]
    w = np.concatenate([a[f"L0_conv_{k}_w"].reshape(S0, G0, -1) for k in kinds], 2)
    b = np.concatenate([a[f"L0_conv_{k}_b"].reshape(G0, -1) for k in kinds], 1)
    t["w_par"] = np.repeat(w.transpose(1, 0, 2)[:, None], 2, 1).reshape(P, NPAR)
    w = a["L1_conv_W_in"].T
    none = np.zeros((C, DI), f)
    t["w_z"] = np.concatenate([w[:, :DI], none])
    t["w_in"] = np.tile(w[:, DI:2 * DI + 2 * DS1], (2, 1))
    t["w_dt"] = np.concatenate([np.pad(w[:, 2 * DI + 2 * DS1:], ((0, 0), (0, 32 - NH1))), none[:, :32]])
    t["w_out"], t["w_out2"] = a["L1_conv_W_out"].T, np.tile(a["L1_conv_W_out"].T, (1, 2))
    t["ident"] = np.eye(P, dtype=f)
    t["center"] = np.eye(P, dtype=f) - f(1 / DI)
    t["ones"] = np.full((P, C), 1 / DI, f)
    t["quarter"] = (part[:, None] // 32 == np.arange(4)).astype(f)
    heads = lambda v: np.tile(np.pad(v, (0, 32 - NH1)), 4)
    cb = a["L1_conv_conv_b"]
    t["l1_vec"] = np.stack([cb[:DI], np.tile(cb[DI:], 4), np.repeat(a["L1_conv_D"], HD1), a["L1_conv_ln_g"], a["L1_conv_ln_b"],
                            heads(a["L1_conv_dt_bias"]), heads(a["L1_conv_A_log"])], 1)
    t["conv_w"] = a["L1_conv_conv_w"][:, 0].transpose(1, 2, 0)
    order = np.arange(C).reshape(4, 2, HD2).transpose(1, 2, 0).reshape(C)
    t["w_q"], t["w_k"], t["w_v"] = two_blocks(a["L2_conv_Wq"][order].T), two_blocks(a["L2_conv_Wk"][order].T), two_blocks(a["L2_conv_Wv"].T)
    t["w_o"] = two_blocks(a["L2_conv_Wo"].T).reshape(P, 2, C)
    t["b_v"] = np.tile(a["L2_conv_bv"], (P, 2))
    t["l2_vec"] = np.stack([np.tile(v, 2) for v in (a["L2_conv_bq"][order], a["L2_conv_bk"][order], a["L2_conv_bo"])], 1)
    w = np.concatenate([a["L3_conv_off_w"][0::2], a["L3_conv_off_w"][1::2], a["L3_conv_mask_w"]])
    w_off = np.zeros((2, C, 2, W3, 32), f)
    w_off[0, :, :, :, :27] = w[:, :, 0::2].transpose(1, 2, 3, 0)
    w_off[1, :, 0, :, :27] = w[:, :, 1].transpose(1, 2, 0)
    t["w_off"] = w_off.reshape(P, 6, 32)
    t["w_all"] = two_blocks(a["L3_conv_weight"].transpose(1, 2, 3, 0).reshape(C, -1))
    bias = np.concatenate([a["L3_conv_off_b"][0::2], a["L3_conv_off_b"][1::2], a["L3_conv_mask_b"]])
    t["l3_vec"] = np.stack([np.tile(np.pad(bias, (0, 32 - 27)), 4), -(part % H).astype(f), np.tile(a["L3_conv_bias"], 2)], 1)
    k, r = np.divmod(part, 3)
    col = part[None, :]
    rows = [(part[:, None] < 48) & (k[:, None] == 8 * h + col // W) for h in range(2)]
    k = (part - 64) // 3
    t["sel"] = np.stack(rows + [(part[:, None] >= 64) & (part[:, None] < 112) & (k[:, None] == col % W)], 1).astype(f)
    tap_y, tap_x = np.divmod(np.arange(9), 3)
    pos_y, pos_x = np.divmod(np.arange(N), W)
    t["grid"] = np.concatenate([np.stack([pos_y, pos_x, np.ones(N)]), np.zeros((P - 3, N))]).astype(f)
    w_grid = np.zeros((P, 32), f)
    w_grid[0, :9], w_grid[1, 9:18], w_grid[2, :18] = 1, 1, np.concatenate([tap_y, tap_x]) - 1
    t["w_grid"] = w_grid
    t["b_par"] = np.tile(np.repeat(b, 16, 0), (2, 1))
    return t


def kernel(**inputs):
    import concourse.bacc as bacc
    from concourse.bass_utils import run_bass_kernel_spmd

    nc = bacc.Bacc("TRN2", target_bir_lowering=False, num_devices=1)
    arrays, ins = {}, {}
    for name, a in lay_out({k: np.asarray(v) for k, v in inputs.items()}).items():
        a = np.ascontiguousarray(a)
        arrays[f"in_{name}"] = a
        ins[name] = nc.dram_tensor(f"in_{name}", a.shape, mybir.dt.from_np(a.dtype), kind="ExternalInput").ap()
    out = nc.dram_tensor("out_x", (B, C, H, W), F32, kind="ExternalOutput").ap()
    program(nc, ins, out)
    r = run_bass_kernel_spmd(nc, [arrays], core_ids=[0])
    return r.results[0]["out_x"]
```
